# Optimizing a Trainium2 kernel written in Bass

```python
import numpy as np
import jax
import jax.numpy as jnp

def _softmax(x, axis=-1):
    return jax.nn.softmax(x, axis=axis)

def _gelu(x):
    return jax.nn.gelu(x, approximate=True)

def _silu(x):
    return jax.nn.silu(x)

def _sigmoid(x):
    return jax.nn.sigmoid(x)

def _layernorm(x, axis=-1, eps=1e-05):
    m = jnp.mean(x, axis=axis, keepdims=True)
    v = jnp.var(x, axis=axis, keepdims=True)
    return (x - m) / jnp.sqrt(v + eps)

def _scatter_add(tgt, idx, src, axis=0):
    return tgt.at[idx].add(src)

def _segment_sum(src, seg, n):
    return jax.ops.segment_sum(src, seg, n)
kernel_name = 'mk_cond_resid_d1_seqx_r2_696c7f'

def setup_inputs(seed: int=0):
    np.random.seed(seed)
    _w = jnp.asarray

    def _rec_inputs():
        import jax
        import jax.numpy as jnp
        _rk = jax.random.key(seed)
        x = 7.22e-05 + 1 * jax.random.normal(jax.random.fold_in(_rk, 1), (4, 1024, 512), jnp.float32)
        _lenS = 1024 - jax.random.randint(jax.random.fold_in(_rk, 7), (4,), 0, max(1, 1024 // 4) + 1, jnp.int32)
        _lenS2 = 1024 - jax.random.randint(jax.random.fold_in(_rk, 8), (4,), 0, max(1, 1024 // 4) + 1, jnp.int32)
        cond_256 = 0.000887014 + 1.03683 * jax.random.normal(jax.random.fold_in(_rk, 11), (4, 128), jnp.float32)
        return (x, cond_256)
    x, cond_256 = _rec_inputs()

    def _L0_cond_setup():
        import jax, jax.numpy as jnp
        import numpy as np
        D_MODEL = 512
        D_T = 128
        N_HEADS = 16
        HIDDEN = 4 * D_MODEL
        EPS = 1e-06

        def _tc_rmsnorm(x, t, gw, gb, bw, bb):
            g = (t @ gw.T + gb)[:, None, :]
            b = (t @ bw.T + bb)[:, None, :]
            inv_rms = jax.lax.rsqrt(jnp.mean(x * x, axis=-1, keepdims=True) + EPS)
            return g * x * inv_rms + b

        def _attention(x, Wq, Wk, Wv, Wo):
            B, L, D = x.shape
            H = N_HEADS
            dh = D // H
            scale = np.sqrt(dh).astype(np.float32)
            q = (x @ Wq.T).reshape(B, L, H, dh)
            k = (x @ Wk.T).reshape(B, L, H, dh)
            v = (x @ Wv.T).reshape(B, L, H, dh)
            attn = jnp.einsum('blhd,bmhd->bhlm', q, k) / scale
            p = jax.nn.softmax(attn, axis=-1)
            o = jnp.einsum('bhlm,bmhd->blhd', p, v).reshape(B, L, D)
            return o @ Wo.T

        def _swiglu(x, gate_w, hid_w, out_w):
            return jax.nn.silu(x @ gate_w.T) * (x @ hid_w.T) @ out_w.T
        key = jax.random.key(seed)
        ks = jax.random.split(key, 20)
        B, L = (8, 512)
        s_d = 1.0 / np.sqrt(D_MODEL)
        s_t = 1.0 / np.sqrt(D_T)
        s_h = 1.0 / np.sqrt(HIDDEN)
        return {'x': jax.random.normal(ks[0], (B, L, D_MODEL), jnp.float32), 't': jax.random.normal(ks[1], (B, D_T), jnp.float32), 'Wq': jax.random.normal(ks[2], (D_MODEL, D_MODEL), jnp.float32) * s_d, 'Wk': jax.random.normal(ks[3], (D_MODEL, D_MODEL), jnp.float32) * s_d, 'Wv': jax.random.normal(ks[4], (D_MODEL, D_MODEL), jnp.float32) * s_d, 'Wo': jax.random.normal(ks[5], (D_MODEL, D_MODEL), jnp.float32) * s_d, 'g1w': jax.random.normal(ks[6], (D_MODEL, D_T), jnp.float32) * s_t, 'g1b': jnp.ones((D_MODEL,), jnp.float32), 'b1w': jax.random.normal(ks[7], (D_MODEL, D_T), jnp.float32) * s_t, 'b1b': jnp.zeros((D_MODEL,), jnp.float32), 'g2w': jax.random.normal(ks[8], (D_MODEL, D_T), jnp.float32) * s_t, 'g2b': jnp.ones((D_MODEL,), jnp.float32), 'b2w': jax.random.normal(ks[9], (D_MODEL, D_T), jnp.float32) * s_t, 'b2b': jnp.zeros((D_MODEL,), jnp.float32), 'gate_w': jax.random.normal(ks[10], (HIDDEN, D_MODEL), jnp.float32) * s_d, 'hid_w': jax.random.normal(ks[11], (HIDDEN, D_MODEL), jnp.float32) * s_d, 'out_w': jax.random.normal(ks[12], (D_MODEL, HIDDEN), jnp.float32) * s_h}
    _L0_cond_all = _L0_cond_setup()
    _L0_cond_in = {k: v for k, v in _L0_cond_all.items() if k in ('Wq', 'Wk', 'Wv', 'Wo', 'g1w', 'g1b', 'b1w', 'b1b', 'g2w', 'g2b', 'b2w', 'b2b', 'gate_w', 'hid_w', 'out_w')}
    del _L0_cond_all
    return {'x': x, 'cond_256': cond_256, 'L0_cond_Wq': _L0_cond_in['Wq'], 'L0_cond_Wk': _L0_cond_in['Wk'], 'L0_cond_Wv': _L0_cond_in['Wv'], 'L0_cond_Wo': _L0_cond_in['Wo'], 'L0_cond_g1w': _L0_cond_in['g1w'], 'L0_cond_g1b': _L0_cond_in['g1b'], 'L0_cond_b1w': _L0_cond_in['b1w'], 'L0_cond_b1b': _L0_cond_in['b1b'], 'L0_cond_g2w': _L0_cond_in['g2w'], 'L0_cond_g2b': _L0_cond_in['g2b'], 'L0_cond_b2w': _L0_cond_in['b2w'], 'L0_cond_b2b': _L0_cond_in['b2b'], 'L0_cond_gate_w': _L0_cond_in['gate_w'], 'L0_cond_hid_w': _L0_cond_in['hid_w'], 'L0_cond_out_w': _L0_cond_in['out_w']}

def reference(x, cond_256, L0_cond_Wq, L0_cond_Wk, L0_cond_Wv, L0_cond_Wo, L0_cond_g1w, L0_cond_g1b, L0_cond_b1w, L0_cond_b1b, L0_cond_g2w, L0_cond_g2b, L0_cond_b2w, L0_cond_b2b, L0_cond_gate_w, L0_cond_hid_w, L0_cond_out_w):
    import jax
    import jax.numpy as jnp

    def _L0_cond_ref(x, t, Wq, Wk, Wv, Wo, g1w, g1b, b1w, b1b, g2w, g2b, b2w, b2b, gate_w, hid_w, out_w):
        import jax, jax.numpy as jnp
        import numpy as np
        D_MODEL = 512
        D_T = 128
        N_HEADS = 16
        HIDDEN = 4 * D_MODEL
        EPS = 1e-06

        def _tc_rmsnorm(x, t, gw, gb, bw, bb):
            g = (t @ gw.T + gb)[:, None, :]
            b = (t @ bw.T + bb)[:, None, :]
            inv_rms = jax.lax.rsqrt(jnp.mean(x * x, axis=-1, keepdims=True) + EPS)
            return g * x * inv_rms + b

        def _attention(x, Wq, Wk, Wv, Wo):
            B, L, D = x.shape
            H = N_HEADS
            dh = D // H
            scale = np.sqrt(dh).astype(np.float32)
            q = (x @ Wq.T).reshape(B, L, H, dh)
            k = (x @ Wk.T).reshape(B, L, H, dh)
            v = (x @ Wv.T).reshape(B, L, H, dh)
            attn = jnp.einsum('blhd,bmhd->bhlm', q, k) / scale
            p = jax.nn.softmax(attn, axis=-1)
            o = jnp.einsum('bhlm,bmhd->blhd', p, v).reshape(B, L, D)
            return o @ Wo.T

        def _swiglu(x, gate_w, hid_w, out_w):
            return jax.nn.silu(x @ gate_w.T) * (x @ hid_w.T) @ out_w.T
        x = x + _attention(_tc_rmsnorm(x, t, g1w, g1b, b1w, b1b), Wq, Wk, Wv, Wo)
        return x + _swiglu(_tc_rmsnorm(x, t, g2w, g2b, b2w, b2b), gate_w, hid_w, out_w)
    x = x + _L0_cond_ref(x, cond_256, L0_cond_Wq, L0_cond_Wk, L0_cond_Wv, L0_cond_Wo, L0_cond_g1w, L0_cond_g1b, L0_cond_b1w, L0_cond_b1b, L0_cond_g2w, L0_cond_g2b, L0_cond_b2w, L0_cond_b2b, L0_cond_gate_w, L0_cond_hid_w, L0_cond_out_w)
    return x

_drawn_inputs = setup_inputs


def setup_inputs(seed=0):
    import zlib

    import numpy as np

    out = dict(_drawn_inputs(seed))
    spreads = {'L0_cond_g1b': (1.0, 0.2),
     'L0_cond_b1b': (0.0, 0.1),
     'L0_cond_g2b': (1.0, 0.2),
     'L0_cond_b2b': (0.0, 0.1)}
    factors = {}
    for name, (base, spread) in spreads.items():
        noise = np.random.default_rng([zlib.crc32(name.encode()), seed]).standard_normal(out[name].shape)
        drawn = base * np.exp(spread * noise) if base else spread * noise
        out[name] = jnp.asarray(drawn.astype(out[name].dtype))
    for name, factor in factors.items():
        out[name] = (out[name] * factor).astype(out[name].dtype)
    return out
```

```python
import numpy as np
import concourse.bass as bass
from concourse import mybir
from contextlib import ExitStack

F32 = mybir.dt.float32
F32R = mybir.dt.float32r
ALU = mybir.AluOpType
ACT = mybir.ActivationFunctionType
AX_X = mybir.AxisListType.X

P = 128
NB, L, D = 4, 1024, 512
H, DH = 16, 32
HID = 2048
DT = 128
EPS = 1e-6
KT = D // P
GH = P // DH
NG = H // GH
QB = 512
NHALF = L // QB
NU = NG * NHALF
NS = L // P
NT = L // P
TPH = QB // P
POOL_HEADS = 3
SB, MB = 3, 2
NMAX = GH * TPH * NHALF
MAX_PER_STEP = [0, 4, 5, 5, 5, 5, 5, 3]
SCALE = 1.0 / float(np.sqrt(np.float32(DH)))



class Counter:

    def __init__(self, lead, per):
        self.lead, self.per = lead, per

    def __call__(self, b, n):
        if b is None:
            return n
        return b * self.per + (self.lead + n)


def misc_order(body):
    if not body:
        return ([("hT", k, hf) for hf in range(NHALF) for k in range(KT)]
                + [("K", 0), ("K", 1), ("Q", 0), ("Q", 1), ("mT", 0)])
    out = []
    for u in range(NU):
        for s in range(NS):
            out += unit_misc(u, s)
        out.append(("mT", u + 1))
    return out


def unit_misc(u, s):
    out = []
    if u % 2 == 0 and s in (1, 3):
        out.append(("K", u + 2, s // 2))
    if s == (0 if u == 5 else NS - 1):
        out.append(("Q", u + 2))
    if u == 5:
        out += {1: [("hT", 0, 0), ("hT", 1, 0)], 2: [("hT", 2, 0), ("hT", 3, 0)],
                6: [("hT", 0, 1), ("hT", 1, 1)], 7: [("hT", 2, 1), ("hT", 3, 1)]}.get(s, [])
    return out


LEAD_MISC = misc_order(False)
BODY_MISC = misc_order(True)
MISC = Counter(len(LEAD_MISC), len(BODY_MISC))
LEAD_DVE = [m for m in LEAD_MISC if m[0] != "mT"]
BODY_DVE = [m for m in BODY_MISC if m[0] != "mT"]
MISC_DVE = Counter(len(LEAD_DVE), len(BODY_DVE))
LEAD_PROJ = [m for m in LEAD_MISC if m[0] in "KQ"]
BODY_PROJ = [m for m in BODY_MISC if m[0] in "KQ"]
PROJ = Counter(len(LEAD_PROJ), len(BODY_PROJ))
SCORES_T = Counter(0, NT + NU * NS * GH)
SCORES_Q = Counter(NMAX, NU * NMAX + NT)
LINKS_PER_BATCH = NU * (2 + 4) + NHALF * KT
STACK_INC = 3 * GH * 16


def misc_index(body, tile):
    return (BODY_MISC if body else LEAD_MISC).index(tile)


def dve_before(body, tile):
    order = BODY_MISC if body else LEAD_MISC
    return sum(m[0] != "mT" for m in order[:order.index(tile)])


def hold(sp, held, semaphore, value):
    sp.wait_ge(semaphore, value)
    sp.sem_inc(held, 1)


def next_batch(b):
    return (b + 1) % NB


def attention_program(nc, x, attn, wv_dram, W, cst, psum):
    (wq, wk, wo) = W
    at = cst["at"]
    ident, identr, ones, gain, bias = cst["ident"], cst["identr"], cst["ones"], cst["g1"], cst["b1"]

    hT = [at("hT_hi", [P, KT, L], F32R, "hT_hi"), at("hT_lo", [P, KT, L], F32R, "hT_lo")]
    hT_full = at("hT_full", [P, KT, L], F32, "hT_lo")
    qk = [at("qk_hi", [P, 2, QB], F32R, "qk_hi"), at("qk_lo", [P, 2, QB], F32R, "qk_lo")]
    qs = at("qs", [P, 2, GH, QB], F32R, "qs")
    ks = at("ks", [P, 2, GH, L], F32R, "ks")
    v = at("v", [P, NS, D], F32, "v")
    probs = at("probs", [P, 2, GH, QB], F32, "probs")
    wv = at("wv", [P, 2, KT, D], F32R, "probs")
    sums = at("sums", [P, POOL_HEADS, QB], F32, "sums")
    mt = at("mt", [P, TPH, P], F32R, "mt")
    o = at("o", [P, NG, L], F32, "o")
    den = at("den", [P, QB], F32, "den")
    x4 = at("x4", [P, TPH, D], F32, "x4")
    osplit = at("osplit", [P, 2, 2, NG, P], F32R, "x4")
    yout = at("yout", [P, 2, D], F32, "yout")
    pmax = at("pmax", [P, TPH, GH, NHALF], F32, "pmax")
    mx = at("mx", [P, TPH, GH], F32, "mx")
    ssq = at("ssq", [P, TPH], F32, "ssq")
    var = at("var", [P, TPH], F32, "var")
    inv = at("inv", [P, TPH], F32, "inv")
    mhalf = at("mhalf", [P, TPH], F32, "mhalf")
    dsmall = at("dsmall", [P, QB // 32], F32, "dsmall")
    zero = at("zero", [P, 1], F32, "zero")
    indc = at("indc", [P, GH], F32, "indc")

    sbank = psum[0:SB]
    mbank = psum[SB:SB + MB]
    obank, dbank, wbank = psum[5], psum[6], psum[7]

    with ExitStack() as ctx:
        def sem(name):
            return ctx.enter_context(nc.semaphore(name))

        held = sem("held")
        x_loaded = sem("x_loaded")
        wv_loaded = sem("wv_loaded")
        st_ready = sem("st_ready")
        st_done = sem("st_done")
        sq_ready = sem("sq_ready")
        sq_done = sem("sq_done")
        w_ready = sem("w_ready")
        w_act = sem("w_act")
        w_dve = sem("w_dve")
        stacked = [sem("stacked0"), sem("stacked1")]
        pv_done = sem("pv_done")
        sum_done = sem("sum_done")
        mt_ready = sem("mt_ready")
        od_act = sem("od_act")
        d_ready = sem("d_ready")
        on_done = sem("on_done")
        os_act = sem("os_act")
        os_dve = sem("os_dve")
        y_stored = [sem("y_stored0"), sem("y_stored1")]
        sq_sum = sem("sq_sum")
        var_ready = sem("var_ready")
        inv_ready = sem("inv_ready")
        x_scaled = sem("x_scaled")
        const_pool = sem("const_pool")
        const_dve = sem("const_dve")
        dve_step = sem("dve_step")
        block = ctx.enter_context(nc.Block())

        def stacked_value(b, n):
            slot = n % 2
            lead, per = len(LEAD_PROJ) // 2, len(BODY_PROJ) // 2
            if b is None:
                return slot, (n // 2 + 1) * STACK_INC
            return slot, b * (per * STACK_INC) + (lead + n // 2 + 1) * STACK_INC

        def proj_index(body, tile):
            return (BODY_PROJ if body else LEAD_PROJ).index(tile)

        @block.sync
        def _(sp):
            def load_x(b, hf, src_b):
                if hf == 1:
                    body = b is not None
                    hold(sp, held, w_ready, MISC(b, misc_index(body, ("hT", KT - 1, 0)) + 1))
                elif b is not None:
                    hold(sp, held, sq_ready, SCORES_Q(b, 0))
                sp.dma_start(x4[:], x[src_b, hf * QB:(hf + 1) * QB, :].rearrange("(t p) d -> p t d", p=P)) \
                    .then_inc(x_loaded, 16)

            def stack(b, tile, slot_dst, hf):
                body = b is not None
                hold(sp, held, w_dve, MISC_DVE(b, dve_before(body, tile) + 1))
                n = proj_index(body, tile)
                src = n % 2
                for h in range(GH):
                    rows = slice(DH * h, DH * h + DH)
                    for part, to in ((0, 0), (1, 1), (0, 2)) if tile[0] == "Q" else ((0, 0), (0, 1), (1, 2)):
                        dst = (qs[DH * to:DH * to + DH, slot_dst, h, :] if tile[0] == "Q"
                               else ks[DH * to:DH * to + DH, slot_dst, h, hf * QB:(hf + 1) * QB])
                        sp.dma_start(dst.bitcast(F32), qk[part][rows, src, :].bitcast(F32)).then_inc(stacked[src], 16)

            def load_wv():
                sp.dma_start(wv[:].bitcast(F32), wv_dram).then_inc(wv_loaded, 16)

            load_x(None, 0, 0)
            load_wv()
            load_x(None, 1, 0)
            stack(None, ("K", 0), 0, 0)
            stack(None, ("K", 1), 0, 1)
            stack(None, ("Q", 0), 0, 0)
            with sp.Fori(0, NB) as b:
                prepared = sp.snap(next_batch(b))
                for u in range(NU):
                    hold(sp, held, st_ready, SCORES_T(b, NT + u * NS * GH) if u else SCORES_T(b, 0))
                    if u == 0:
                        n = proj_index(True, ("Q", NU + 1))
                        hold(sp, held, w_dve, b * len(BODY_DVE) + len(LEAD_DVE))
                        src = n % 2
                        for h in range(GH):
                            for part, to in ((0, 0), (1, 1), (0, 2)):
                                sp.dma_start(qs[DH * to:DH * to + DH, 1, h, :].bitcast(F32),
                                             qk[part][DH * h:DH * h + DH, src, :].bitcast(F32)).then_inc(stacked[src], 16)
                    else:
                        stack(b, ("Q", u + 1), (u + 1) % 2, 0)
                    if u % 2 == 0:
                        for hf in range(NHALF):
                            stack(b, ("K", u + 2, hf), (u // 2 + 1) % 2, hf)
                    if u == 3:
                        load_x(b, 0, prepared)
                    if u == 5:
                        load_x(b, 1, prepared)
                hold(sp, held, pv_done, b * (NU * NS) + NU * NS + 2)
                hold(sp, held, sum_done, b * (NU * NS) + NU * NS + 2)
                load_wv()
                for t in range(NT):
                    hold(sp, held, sq_done, SCORES_Q(b, NU * NMAX + t + 1) + MB)
                    sp.dma_start(attn[b, t * P:(t + 1) * P, :], yout[:, t % 2, :]).then_inc(y_stored[t % 2], 16)
            for s in y_stored:
                hold(sp, held, s, NB * (NT // 2) * 16)
            hold(sp, held, wv_loaded, (NB + 1) * 16)

        @block.gpsimd
        def _(pool):
            nc.gpsimd.memset(mhalf[:], -0.5).then_inc(const_pool, 1)
            nc.gpsimd.memset(zero[:], 0.0).then_inc(const_pool, 1)
            pool.sem_inc(sum_done, 2)
            pool.wait_ge(const_pool, 2)

            def inverse_root(b, n):
                pool.wait_ge(var_ready, n + 1)
                nc.gpsimd.tensor_tensor(inv[:], var[:], mhalf[:], ALU.pow).then_inc(inv_ready, 1)

            inverse_root(None, 0)
            inverse_root(None, 1)
            with pool.Fori(0, NB) as b:
                for u in range(NU):
                    for s in range(NS):
                        n = u * NS + s
                        if u == 4 and s == 5:
                            inverse_root(b, b * 2 + 2)
                        if u == 5 and s == 5:
                            inverse_root(b, b * 2 + 3)
                        pool.wait_ge(st_done, SCORES_T(b, NT + (n * GH) + POOL_HEADS) + SB)
                        if s == 0:
                            pool.wait_ge(d_ready, b * NU + u)
                        pool.wait_ge(sum_done, b * (NU * NS) + n + 2)
                        prev = sums[:] if s else zero[:, 0:1].unsqueeze(2).to_broadcast([P, POOL_HEADS, QB])
                        nc.gpsimd.tensor_tensor(sums[:], probs[:, s % 2, 0:POOL_HEADS, :], prev, ALU.add) \
                            .then_inc(sum_done, 1)

        @block.scalar
        def _(act):
            act.sem_inc(st_done, SB)
            act.sem_inc(od_act, 1)

            def squares(b, hf):
                n = 2 * hf if b is None else b * 8 + 8 + 4 * hf
                n = 4 * hf if b is None else n
                act.wait_ge(x_loaded, 16 * (hf + 1) if b is None else b * 32 + 32 + 16 * (hf + 1))
                if b is not None and hf == 0:
                    for s in y_stored:
                        act.wait_ge(s, b * (NT // 2 * 16))
                act.wait_ge(var_ready, hf if b is None else b * 2 + 2 + hf)
                for t in range(TPH):
                    act.wait_ge(sq_sum, n + t)
                    nc.scalar.activation(yout[:, 0, :], x4[:, t, :], ACT.Square,
                                         accum_out=ssq[:, t:t + 1]).then_inc(sq_sum, 1)

            def work_tile(b, tile):
                body = b is not None
                i = misc_index(body, tile)
                act.wait_ge(w_ready, MISC(b, i + 1))
                if tile[0] == "hT":
                    _, k, hf = tile
                    nc.scalar.activation(hT[0][:, k, hf * QB:(hf + 1) * QB], wbank[:], ACT.Identity,
                                         bias=cur_bias[:, k:k + 1],
                                         scale=cur_gain[:, k:k + 1]).then_inc(w_act, 1)
                elif tile[0] == "mT":
                    slot = tile[1] % 2
                    nc.scalar.activation(qs[96:128, slot, :, :],
                                         wbank[96:128, :].unsqueeze(1).to_broadcast([32, GH, QB]),
                                         ACT.Copy).then_inc(w_act, 1)
                else:
                    n = proj_index(body, tile)
                    if b is not None or n >= 2:
                        if b is None:
                            slot, val = stacked_value(None, n - 2)
                        elif n >= 2:
                            slot, val = stacked_value(b, n - 2)
                        else:
                            slot, val = n % 2, b * (len(BODY_PROJ) // 2 * STACK_INC) + len(LEAD_PROJ) // 2 * STACK_INC
                        act.wait_ge(stacked[slot], val)
                    nc.scalar.activation(qk[0][:, n % 2, :], wbank[:], ACT.Copy).then_inc(w_act, 1)

            cur_gain, cur_bias = cst["gain_now"], cst["bias_now"]

            def denominators(b, u):
                act.wait_ge(d_ready, b * NU + u + 1)
                nc.scalar.activation(den[0:96, :], dbank[0:96, :], ACT.Copy).then_inc(od_act, 1)

            squares(None, 0)
            act.wait_ge(const_dve, 3)
            for tile in LEAD_MISC[:KT]:
                work_tile(None, tile)
            squares(None, 1)
            for tile in LEAD_MISC[KT:]:
                work_tile(None, tile)
            with act.Fori(0, NB) as b:
                for t in range(NT):
                    act.wait_ge(st_ready, SCORES_T(b, t + 1))
                    if t == 0:
                        act.wait_ge(pv_done, b * (NU * NS) + 2)
                    nc.scalar.activation(v[:, t, :], sbank[t % SB][:], ACT.Copy).then_inc(st_done, 1)
                for u in range(NU):
                    for s in range(NS):
                        n = u * NS + s
                        act.wait_ge(pv_done, b * (NU * NS) + n + 1)
                        act.wait_ge(sum_done, b * (NU * NS) + n + 1)
                        for h in range(GH):
                            i = NT + n * GH + h
                            act.wait_ge(st_ready, SCORES_T(b, i + 1))
                            nc.scalar.activation(probs[:, s % 2, h, :], sbank[i % SB][:], ACT.Exp,
                                                 scale=SCALE).then_inc(st_done, 1)
                        if s == 1 and u:
                            denominators(b, u - 1)
                        if u == 4 and s == 4:
                            squares(b, 0)
                        if u == 5 and s == 0:
                            act.wait_ge(const_dve, b * 2 + 5)
                        if u == 5 and s == 4:
                            squares(b, 1)
                        for tile in unit_misc(u, s):
                            work_tile(b, tile)
                    work_tile(b, ("mT", u + 1))
                    act.wait_ge(pv_done, b * (NU * NS) + (u + 1) * NS + 2)
                    if u == 0:
                        act.wait_ge(os_dve, b * NT)
                    g, hf = u // 2, u % 2
                    nc.scalar.activation(o[:, g, hf * QB:(hf + 1) * QB], obank[:], ACT.Copy).then_inc(od_act, 1)
                    act.wait_ge(on_done, b * NU + u)
                    nc.scalar.activation(den[96:128, :], dbank[96:128, :], ACT.Copy).then_inc(od_act, 1)
                for t in range(NT):
                    act.wait_ge(on_done, b * NU + (NU - 1 if t < TPH else NU))
                    if t >= 2:
                        act.wait_ge(sq_ready, SCORES_Q(b, NU * NMAX + t - 1))
                    nc.scalar.activation(osplit[:, t % 2, 0, :, :], o[:, :, t * P:(t + 1) * P],
                                         ACT.Copy).then_inc(os_act, 1)
                    if t == 1:
                        denominators(b, NU - 1)

        @block.vector
        def _(dve):
            class Link:
                lead = 0
                n = 0
                b = None

            def link(ins):
                ins.then_inc(dve_step, 1)
                Link.n += 1
                dve.wait_ge(dve_step, Link.n if Link.b is None else Link.b * LINKS_PER_BATCH + (Link.lead + Link.n))

            dve.sem_inc(sq_done, MB)
            link(nc.vector.tensor_tensor(indc[96:128, :], ident[96:128, 96:96 + 2 * GH:2],
                                         ident[96:128, 97:97 + 2 * GH:2], ALU.add))
            for sl in range(2):
                for h in range(GH):
                    link(nc.vector.tensor_copy(ks[96:128, sl, h, :], indc[96:128, h:h + 1].to_broadcast([32, L])))
            nc.vector.tensor_scalar(mt[:], mt_zero_source(ident), 0.0, None, ALU.mult).then_inc(const_dve, 1)
            cur_gain, cur_bias = cst["gain_now"], cst["bias_now"]
            nc.vector.tensor_copy(cur_gain[:], gain[:, 0, :]).then_inc(const_dve, 1)
            nc.vector.tensor_copy(cur_bias[:], bias[:, 0, :]).then_inc(const_dve, 1)
            dve.wait_ge(const_dve, 3)

            def mean_square(b, hf):
                n = hf if b is None else b * 2 + 2 + hf
                dve.wait_ge(sq_sum, 4 * (n + 1))
                dve.wait_ge(inv_ready, n)
                nc.vector.tensor_scalar(var[:], ssq[:], 1.0 / D, EPS, ALU.mult, ALU.add).then_inc(var_ready, 1)

            def scale_x(b, hf):
                n = hf if b is None else b * 2 + 2 + hf
                dve.wait_ge(inv_ready, n + 1)
                for t in range(TPH):
                    nc.vector.tensor_scalar(x4[:, t, :], x4[:, t, :], inv[:, t:t + 1], None,
                                            ALU.mult).then_inc(x_scaled, 1)

            def work_tile(b, tile):
                body = b is not None
                dve.wait_ge(w_ready, MISC(b, misc_index(body, tile) + 1))
                dve.wait_ge(w_act, MISC(b, misc_index(body, tile) + 1))
                if tile[0] == "hT":
                    _, k, hf = tile
                    cols = slice(hf * QB, (hf + 1) * QB)
                    link(nc.vector.tensor_scalar(hT_full[:, k, cols], wbank[:], cur_gain[:, k:k + 1],
                                                 cur_bias[:, k:k + 1], ALU.mult, ALU.add))
                    nc.vector.tensor_tensor(hT[1][:, k, cols], hT_full[:, k, cols],
                                            hT[0][:, k, cols].bitcast(F32), ALU.subtract).then_inc(w_dve, 1)
                else:
                    n = proj_index(body, tile)
                    nc.vector.tensor_tensor(qk[1][:, n % 2, :], wbank[:], qk[0][:, n % 2, :].bitcast(F32),
                                            ALU.subtract).then_inc(w_dve, 1)

            def max_tile(b, n, i):
                h, t, hf = i // (TPH * NHALF), i // NHALF % TPH, i % NHALF
                dve.wait_ge(sq_ready, SCORES_Q(b, n + 1) if b is not None else n + 1)
                nc.vector.reduce_max(pmax[:, t, h, hf:hf + 1], mbank[n % MB][:], AX_X).then_inc(sq_done, 1)

            def maxima(b, u, n):
                dve.wait_ge(sq_done, (SCORES_Q(b, n) if b is not None else n) + MB)
                link(nc.vector.tensor_tensor(mx[:], pmax[:, :, :, 0], pmax[:, :, :, 1], ALU.max))
                if b is not None:
                    dve.wait_ge(w_ready, MISC(b, misc_index(True, ("mT", u))) + 1 if u else MISC(b, 0))
                hi, lo = mt[:, :, 96:96 + 2 * GH:2], mt[:, :, 97:97 + 2 * GH:2]
                link(nc.vector.tensor_scalar(hi, mx[:], -1.0, None, ALU.mult))
                nc.vector.scalar_tensor_tensor(lo, mx[:], -1.0, hi.bitcast(F32), ALU.mult,
                                               ALU.subtract).then_inc(mt_ready, 1)

            def normalise(b, u):
                g, hf = u // 2, u % 2
                dve.wait_ge(od_act, b * (3 * NU) + (3 * (u + 1) + 1))
                link(nc.vector.transpose(den[:], den[:]))
                cols = den[:].rearrange("p (c i) -> p c i", i=32)
                link(nc.vector.reciprocal(dsmall[:], cols[:, :, 0]))
                link(nc.vector.tensor_copy(cols, dsmall[:].unsqueeze(2).to_broadcast([P, QB // 32, 32])))
                link(nc.vector.transpose(den[:], den[:]))
                part = o[:, g, hf * QB:(hf + 1) * QB]
                nc.vector.tensor_tensor(part, part, den[:], ALU.mult).then_inc(on_done, 1)

            mean_square(None, 0)
            scale_x(None, 0)
            for tile in LEAD_MISC[:KT]:
                work_tile(None, tile)
            mean_square(None, 1)
            scale_x(None, 1)
            for tile in LEAD_MISC[KT:-1]:
                work_tile(None, tile)
            for i in range(NMAX):
                max_tile(None, i, i)
            maxima(None, 0, NMAX)

            Link.lead, Link.n = Link.n, 0
            with dve.Fori(0, NB) as b:
                Link.b = b
                for u in range(NU):
                    done = 0
                    if u == 0:
                        dve.wait_ge(mt_ready, b * NU + 1)
                    for s in range(NS):
                        if u == 4 and s == 5:
                            mean_square(b, 0)
                        if u == 4 and s == 7:
                            scale_x(b, 0)
                        if u == 5 and s == 0:
                            dve.wait_ge(const_dve, b * 2 + 5)
                        if u == 5 and s == 5:
                            mean_square(b, 1)
                            scale_x(b, 1)
                        if u == 4 and s == 0:
                            nb = next_batch(b)
                            nc.vector.tensor_copy(cur_gain[:], gain[:, bass.ds(nb, 1), :].squeeze(1)).then_inc(const_dve, 1)
                            nc.vector.tensor_copy(cur_bias[:], bias[:, bass.ds(nb, 1), :].squeeze(1)).then_inc(const_dve, 1)
                        for _ in range(MAX_PER_STEP[s]):
                            max_tile(b, u * NMAX + done, done)
                            done += 1
                        if s == 2 and u:
                            normalise(b, u - 1)
                        for tile in unit_misc(u, s):
                            if s == NS - 1 and tile[0] == "Q":
                                maxima(b, u, (u + 1) * NMAX)
                            work_tile(b, tile)
                    if u == 5:
                        maxima(b, u, (u + 1) * NMAX)
                    dve.wait_ge(mt_ready, b * NU + u + 2)

                def lo_part(t):
                    dve.wait_ge(os_act, b * NT + t + 1)
                    nc.vector.tensor_tensor(osplit[:, t % 2, 1, :, :], o[:, :, t * P:(t + 1) * P],
                                            osplit[:, t % 2, 0, :, :].bitcast(F32), ALU.subtract).then_inc(os_dve, 1)

                def out_tile(t):
                    n = NU * NMAX + t
                    dve.wait_ge(sq_ready, SCORES_Q(b, n + 1))
                    dve.wait_ge(y_stored[t % 2], b * (NT // 2 * 16) + t // 2 * 16)
                    nc.vector.tensor_copy(yout[:, t % 2, :], mbank[n % MB][:]).then_inc(sq_done, 1)

                lo_part(0)
                lo_part(1)
                out_tile(0)
                lo_part(2)
                out_tile(1)
                lo_part(3)
                normalise(b, NU - 1)
                for t in range(2, NT):
                    out_tile(t)
                    if t + 2 < NT:
                        lo_part(t + 2)
            assert Link.n == LINKS_PER_BATCH, Link.n

        @block.tensor
        def _(pe):
            def product3(out, lhs, rhs, kdim, last_sem):
                steps = [(k, a, c) for k in range(kdim) for a, c in ((0, 0), (0, 1), (1, 0))]
                for i, (k, a, c) in enumerate(steps):
                    last = nc.tensor.matmul(out, lhs(a, k), rhs(c, k), start=(i == 0), stop=(i == len(steps) - 1))
                last.then_inc(last_sem, 1)

            def work_tile(b, tile, g=None):
                body = b is not None
                i = misc_index(body, tile)
                if body or i:
                    pe.wait_ge(w_act, MISC(b, i))
                    pe.wait_ge(w_dve, MISC_DVE(b, dve_before(body, tile)))
                if tile[0] == "hT":
                    _, k, hf = tile
                    if k == 0:
                        pe.wait_ge(x_scaled, TPH * (hf + 1) if b is None else b * 8 + 8 + TPH * (hf + 1))
                    for j in range(TPH):
                        last = nc.tensor.transpose(wbank[:, j * P:(j + 1) * P], x4[:, j, k * P:(k + 1) * P], ident[:])
                    last.then_inc(w_ready, 1)
                elif tile[0] == "mT":
                    pe.wait_ge(mt_ready, 1 if b is None else b * NU + tile[1] + 1)
                    for j in range(TPH):
                        last = nc.tensor.matmul(wbank[:, j * P:(j + 1) * P], mt[:, j, :], identr[:],
                                                start=True, stop=True)
                    last.then_inc(w_ready, 1)
                else:
                    w = wq if tile[0] == "Q" else wk
                    if b is None:
                        g, hf = 0, tile[1]
                    elif tile[0] == "Q":
                        g, hf = tile[1] // 2 % NG, tile[1] % 2
                    else:
                        g, hf = tile[1] // 2 % NG, tile[2]
                    product3(wbank[:], lambda a, k: w[a][:, k, g * P:(g + 1) * P],
                             lambda c, k: hT[c][:, k, hf * QB:(hf + 1) * QB], KT, w_ready)

            def max_tile(b, n, i, g, u):
                h, t, hf = i // (TPH * NHALF), i // NHALF % TPH, i % NHALF
                pe.wait_ge(sq_done, SCORES_Q(b, n + 1) if b is not None else n + 1)
                nc.tensor.matmul(mbank[n % MB][:], qs[0:96, u % 2, h, t * P:(t + 1) * P],
                                 ks[0:96, g % 2, h, hf * QB:(hf + 1) * QB], start=True, stop=True).then_inc(sq_ready, 1)

            def denominators(b, u):
                pe.wait_ge(sum_done, b * (NU * NS) + (u + 1) * NS + 2)
                pe.wait_ge(od_act, b * (3 * NU) + 3 * u + 1)
                for h in range(POOL_HEADS):
                    last = nc.tensor.matmul(dbank[DH * h:DH * h + DH, :], ones[:], sums[:, h, :], start=True, stop=True)
                last.then_inc(d_ready, 1)

            def values(b, u, s):
                g = u // 2
                pe.wait_ge(st_done, SCORES_T(b, NT + (u * NS + s + 1) * GH) + SB)
                if s == 0:
                    pe.wait_ge(od_act, b * (3 * NU) + 3 * u)
                for h in range(GH):
                    nc.tensor.matmul(obank[DH * h:DH * h + DH, :], v[:, s, (g * GH + h) * DH:(g * GH + h + 1) * DH],
                                     probs[:, s % 2, h, :], start=(s == 0), stop=(s == NS - 1))
                for h in range(POOL_HEADS, GH):
                    last = nc.tensor.matmul(dbank[DH * h:DH * h + DH, :], ones[:], probs[:, s % 2, h, :],
                                            start=(s == 0), stop=(s == NS - 1))
                last.then_inc(pv_done, 1)

            pe.sem_inc(pv_done, 2)
            for tile in LEAD_MISC[:-1]:
                work_tile(None, tile)
            for n in (0, 1, 2):
                slot, val = stacked_value(None, n)
                pe.wait_ge(stacked[slot], val)
            for i in range(NMAX):
                max_tile(None, i, i, 0, 0)
            work_tile(None, ("mT", 0))
            with pe.Fori(0, NB) as b:
                pe.wait_ge(wv_loaded, b * 16 + 16)
                for t in range(NT):
                    pe.wait_ge(st_done, SCORES_T(b, t + 1))
                    product3(sbank[t % SB][:], lambda a, k: hT[a][:, k, t * P:(t + 1) * P],
                             lambda c, k: wv[:, c, k, :], KT, st_ready)
                pe.wait_ge(w_act, MISC(b, 0))
                for u in range(NU):
                    g = u // 2
                    done = 0
                    for s in range(NS):
                        for h in range(GH):
                            i = NT + (u * NS + s) * GH + h
                            pe.wait_ge(st_done, SCORES_T(b, i + 1))
                            nc.tensor.matmul(sbank[i % SB][:], ks[:, g % 2, h, s * P:(s + 1) * P],
                                             qs[:, u % 2, h, :], start=True, stop=True).then_inc(st_ready, 1)
                        if s == 1:
                            if u == 0:
                                pe.wait_ge(stacked[1], b * (len(BODY_PROJ) // 2 * STACK_INC)
                                           + len(LEAD_PROJ) // 2 * STACK_INC)
                            else:
                                slot, val = stacked_value(b, proj_index(True, ("Q", u + 1)))
                                pe.wait_ge(stacked[slot], val)
                            if u % 2:
                                for hf in range(NHALF):
                                    slot, val = stacked_value(b, proj_index(True, ("K", u + 1, hf)))
                                    pe.wait_ge(stacked[slot], val)
                        for _ in range(MAX_PER_STEP[s]):
                            max_tile(b, u * NMAX + done, done, (u + 1) // 2, u + 1)
                            done += 1
                        if s == 1 and u:
                            denominators(b, u - 1)
                        if s:
                            values(b, u, s - 1)
                        for tile in unit_misc(u, s):
                            work_tile(b, tile)
                    work_tile(b, ("mT", u + 1))
                    values(b, u, NS - 1)
                    pe.wait_ge(w_act, MISC(b, misc_index(True, ("mT", u + 1)) + 1))
                for t in range(NT):
                    pe.wait_ge(sq_done, SCORES_Q(b, NU * NMAX + t + 1))
                    pe.wait_ge(os_act, b * NT + t + 1)
                    pe.wait_ge(os_dve, b * NT + t + 1)
                    product3(mbank[(NU * NMAX + t) % MB][:], lambda a, k: osplit[:, t % 2, a, k, :],
                             lambda c, k: wo[c][:, k, :], NG, sq_ready)
                    if t == 1:
                        denominators(b, NU - 1)


def mt_zero_source(ident):
    return ident[:, 0:P].unsqueeze(1).to_broadcast([P, TPH, P])


def attention_setup(nc, t_in, W_in, cond_in, wv_dram, W, cst, psum):
    at = cst["at"]
    ident, identr, ones = cst["ident"], cst["identr"], cst["ones"]
    raw = at("w_raw", [P, 4, KT, D], F32, "setup_raw")
    wvs = at("wv_split", [P, 2, KT, D], F32R, "setup_wv")
    t_sb = at("t_sb", [NB, DT], F32, "setup_t")
    t_T = at("t_T", [P, NB], F32, "setup_tT")
    gw = at("gw", [P, 4, KT, DT], F32, "setup_gw")
    gwT = at("gwT", [P, 4, D], F32, "setup_gwT")
    gb = at("gb", [P, 4, KT], F32, "setup_gb")
    parts = [W[0], W[1], [wvs[:, 0, :, :], wvs[:, 1, :, :]], W[2]]
    RING = 4
    with ExitStack() as ctx:
        def sem(name):
            return ctx.enter_context(nc.semaphore(name))

        id_step = sem("id_step")
        cond_loaded = sem("cond_loaded")
        w_loaded = [sem(f"w_loaded{i}") for i in range(4)]
        t_ready = sem("t_ready")
        t_act = sem("t_act")
        t_dve = sem("t_dve")
        wv_stored = sem("wv_stored")
        block = ctx.enter_context(nc.Block())
        tiles = ([("tT",)] + [("gwT", m) for m in range(4)] + [("cond", m) for m in range(4)]
                 + [("w", w, k) for w in (2, 0, 1, 3) for k in range(KT)])

        @block.gpsimd
        def _(pool):
            nc.gpsimd.memset(ident[:], 0.0).then_inc(id_step, 1)
            nc.gpsimd.memset(ones[:], 1.0).then_inc(id_step, 1)
            pool.wait_ge(id_step, 2)
            nc.gpsimd.affine_select(out=ident[:], in_=ident[:], compare_op=ALU.not_equal, fill=1.0, base=0,
                                    pattern=[[-1, P]], channel_multiplier=1).then_inc(id_step, 1)

        @block.sync
        def _(sp):
            sp.dma_start(t_sb[:], t_in).then_inc(cond_loaded, 16)
            for m in range(4):
                sp.dma_start(gw[:, m, :, :], cond_in[m][0].rearrange("(k p) t -> p k t", p=P)).then_inc(cond_loaded, 16)
                with nc.allow_non_contiguous_dma(reason="512 bias values, once"):
                    sp.dma_start(gb[:, m, :], cond_in[m][1].rearrange("(k p) -> p k", p=P)).then_inc(cond_loaded, 16)
            for w in (2, 0, 1, 3):
                sp.dma_start(raw[:, w, :, :], W_in[w].rearrange("(j p) d -> p j d", p=P)).then_inc(w_loaded[w], 16)
            n = tiles.index(("w", 2, KT - 1)) + 1
            sp.wait_ge(t_dve, n)
            sp.dma_start(wv_dram, wvs[:].bitcast(F32)).then_inc(wv_stored, 16)
            sp.wait_ge(wv_stored, 16)

        @block.tensor
        def _(pe):
            pe.wait_ge(id_step, 3)
            pe.wait_ge(cond_loaded, 16 * 9)
            for n, tile in enumerate(tiles):
                if n >= RING:
                    pe.wait_ge(t_act, n - RING + 1)
                    pe.wait_ge(t_dve, n - RING + 1)
                bank = psum[n % RING]
                if tile[0] == "tT":
                    last = nc.tensor.transpose(bank[:, 0:NB], t_sb[:], ident[0:NB, 0:NB])
                elif tile[0] == "gwT":
                    for k in range(KT):
                        last = nc.tensor.transpose(bank[:, k * P:(k + 1) * P], gw[:, tile[1], k, :], ident[:])
                elif tile[0] == "cond":
                    pe.wait_ge(t_dve, tiles.index(("gwT", tile[1])) + 1)
                    for k in range(KT):
                        last = nc.tensor.matmul(bank[:, k * NB:(k + 1) * NB], gwT[:, tile[1], k * P:(k + 1) * P],
                                                t_T[:], start=True, stop=True)
                else:
                    _, w, k = tile
                    if k == 0:
                        pe.wait_ge(w_loaded[w], 16)
                    for j in range(KT):
                        last = nc.tensor.transpose(bank[:, j * P:(j + 1) * P], raw[:, w, j, k * P:(k + 1) * P], ident[:])
                last.then_inc(t_ready, 1)

        @block.scalar
        def _(act):
            for n, tile in enumerate(tiles):
                act.wait_ge(t_ready, n + 1)
                if tile[0] == "w":
                    nc.scalar.activation(parts[tile[1]][0][:, tile[2], :], psum[n % RING][:], ACT.Copy).then_inc(t_act, 1)
                else:
                    act.sem_inc(t_act, 1)

        @block.vector
        def _(dve):
            dve.wait_ge(id_step, 3)
            nc.vector.tensor_copy(identr[:], ident[:])
            for n, tile in enumerate(tiles):
                bank = psum[n % RING]
                dve.wait_ge(t_ready, n + 1)
                if tile[0] == "tT":
                    ins = nc.vector.tensor_copy(t_T[:], bank[:, 0:NB])
                elif tile[0] == "gwT":
                    ins = nc.vector.tensor_copy(gwT[:, tile[1], :], bank[:])
                elif tile[0] == "cond":
                    dve.wait_ge(cond_loaded, 16 * 9)
                    ins = nc.vector.tensor_tensor(cst["cond"][tile[1]][:].rearrange("p b k -> p k b"),
                                                  bank[:, 0:KT * NB].rearrange("p (k b) -> p k b", b=NB),
                                                  gb[:, tile[1], :].unsqueeze(2).to_broadcast([P, KT, NB]), ALU.add)
                else:
                    dve.wait_ge(t_act, n + 1)
                    hi, lo = parts[tile[1]]
                    ins = nc.vector.tensor_tensor(lo[:, tile[2], :], bank[:], hi[:, tile[2], :].bitcast(F32), ALU.subtract)
                ins.then_inc(t_dve, 1)


NJ = HID // P
NBLK = L // QB
PREP_J = 8
GU_BANKS = 4


def ffn_program(nc, x, attn, gate_w, up_w, out_w, out, cst, psum):
    at = cst["at"]
    ident, gain, bias = cst["ident"], cst["g2"], cst["b2"]
    gain_now, bias_now = cst["gain_now"], cst["bias_now"]
    wT = at("wT", [P, 2, KT, HID], F32, "wT")
    woT = at("woT", [P, NJ, D], F32, "woT")
    gu = [at("gu_hi", [P, 2, 2, KT, P], F32R, "gu_hi"), at("gu_lo", [P, 2, 2, KT, P], F32R, "gu_lo")]
    wo = [at("wo_hi", [P, 2, D], F32R, "wo_hi2"), at("wo_lo", [P, 2, D], F32R, "wo_lo2")]
    hT = [at("h2_hi", [P, 2, KT, QB], F32R, "h2_hi"), at("h2_lo", [P, 2, KT, QB], F32R, "h2_lo")]
    hT_full = at("h2_full", [P, 2, KT, QB], F32, "h2_lo")
    raw = [at("raw0", [P, 2, 4, QB], F32, "h2_hi")[:, 1, :, :], at("raw1", [P, 2, 4, QB], F32, "h2_lo")[:, 1, :, :]]
    x1 = at("x1", [P, TPH, D], F32, "x1")
    res = at("res", [P, 2, TPH, D], F32, "res")
    sg = at("sg", [P, 2, QB], F32, "sg")
    a = [at("a_hi", [P, 2, QB], F32R, "a_hi"), at("a_lo", [P, 2, QB], F32R, "a_lo")]
    junk = at("junk", [P, D], F32, "junk")
    ssq = at("ssq2", [P, TPH], F32, "ssq")
    var = at("var2", [P, TPH], F32, "var")
    inv = at("inv2", [P, TPH], F32, "inv")
    mhalf = at("mhalf2", [P, TPH], F32, "mhalf")
    ybank = psum[GU_BANKS:]

    loads = ([("gu", w, q) for q in range(4) for w in range(2)] + [("o", 0, q) for q in range(4)])
    NW = 4 * len(loads)
    RING = Counter(NW + KT, NBLK * (2 * NJ + KT))

    def ring_tile(hf, j, kind):
        base = hf * (2 * NJ + KT)
        if kind < 2:
            return base + 2 * j + kind + max(0, min(KT, j - PREP_J))
        return base + 2 * (PREP_J + kind - 2) + 2 + kind - 2

    with ExitStack() as ctx:
        def sem(name):
            return ctx.enter_context(nc.semaphore(name))

        held = sem("held2")
        raw_loaded = [sem("raw_loaded0"), sem("raw_loaded1")]
        x_loaded = sem("x_loaded2")
        attn_loaded = sem("attn_loaded")
        g_ready = sem("g_ready")
        g_act = sem("g_act")
        g_dve = sem("g_dve")
        out_mm = sem("out_mm")
        guh = sem("guh")
        gul = sem("gul")
        woh = sem("woh")
        wol = sem("wol")
        ah = sem("ah")
        al = sem("al")
        prod = sem("prod")
        summed = sem("summed")
        sq_sum = sem("sq_sum2")
        var_ready = sem("var_ready2")
        inv_ready = sem("inv_ready2")
        x_scaled = sem("x_scaled2")
        norm_now = sem("norm_now")
        full = sem("full")
        y_added = sem("y_added")
        y_stored = [sem("out_stored0"), sem("out_stored1")]
        block = ctx.enter_context(nc.Block())

        def nxt(b, hf):
            return (b, 1) if hf == 0 else (next_batch(b), 0)

        def blocks(b, hf, per, off=0):
            return b * (NBLK * per) + hf * per + off

        def weight_place(n):
            kind, w, q = loads[n // 4]
            c = n % 4
            if kind == "gu":
                return wT[:, w, c, q * QB:(q + 1) * QB]
            return woT[:, q * 4 + c, :]

        def act_ring(b, hf, j):
            return b * (NBLK * (NJ + KT)) + (NW // 2 + KT + hf * (NJ + KT) + j + max(0, min(KT, j - PREP_J)))

        def dve_ring(b, hf, j):
            return b * (NBLK * KT) + (NW // 2 + KT + hf * KT + max(0, min(KT, j - PREP_J)))

        def first_tiles_free(pe, b, n):
            j = NJ - 2 + n // 2
            if n % 2 == 0:
                pe.wait_ge(g_act, b * (NBLK * (NJ + KT)) + NW // 2 + KT - (NJ - 1 - j))
            else:
                pe.wait_ge(prod, b * (NBLK * NJ))

        @block.sync
        def _(sp):
            def load_tokens(b, hf, slot, prev):
                sp.dma_start(res[:, slot, :, :], x[b, hf * QB:(hf + 1) * QB, :].rearrange("(t p) d -> p t d", p=P)) \
                    .then_inc(x_loaded, 16)
                sp.dma_start(x1[:], attn[b, hf * QB:(hf + 1) * QB, :].rearrange("(t p) d -> p t d", p=P)) \
                    .then_inc(attn_loaded, 16)

            load_tokens(0, 0, 0, None)
            for n, (kind, w, q) in enumerate(loads):
                if n >= 2:
                    hold(sp, held, g_ready, 4 * (n - 1))
                if kind == "gu":
                    src = (gate_w, up_w)[w][q * QB:(q + 1) * QB, :].rearrange("(j p) d -> p j d", p=P)
                else:
                    src = out_w[:, q * QB:(q + 1) * QB].rearrange("(j p) d -> p j d", p=P)
                sp.dma_start(raw[n % 2], src).then_inc(raw_loaded[n % 2], 16)
            with sp.Fori(0, NB) as b:
                prepared = sp.snap(next_batch(b))
                for hf in range(NBLK):
                    slot = (hf + 1) % 2
                    hold(sp, held, y_stored[slot], b * (TPH * 16) + (TPH * 16 if slot == 0 else 0))
                    hold(sp, held, g_ready, RING(b, ring_tile(hf, 0, 0)))
                    nb, nh = (b, 1) if hf == 0 else (prepared, 0)
                    load_tokens(nb, nh, slot, b)
                    for t in range(TPH):
                        hold(sp, held, y_added, blocks(b, hf, TPH, t + 1))
                        row = hf * QB + t * P
                        sp.dma_start(out[b, row:row + P, :], res[:, hf, t, :]).then_inc(y_stored[hf], 16)
            for s in y_stored:
                hold(sp, held, s, NB * TPH * 16)
            hold(sp, held, x_loaded, 16 * (NB * NBLK + 1))
            hold(sp, held, attn_loaded, 16 * (NB * NBLK + 1))

        @block.gpsimd
        def _(pool):
            def prepare(x_val, n_sum, n_inv, slot):
                pool.wait_ge(x_loaded, x_val)
                pool.wait_ge(attn_loaded, x_val)
                nc.gpsimd.tensor_tensor(x1[:], x1[:], res[:, slot, :, :], ALU.add).then_inc(summed, 1)
                pool.wait_ge(summed, n_sum + 1)
                nc.gpsimd.tensor_tensor(res[:, slot, :, :], res[:, slot, :, :], x1[:], ALU.add).then_inc(summed, 1)
                pool.wait_ge(var_ready, n_inv + 1)
                nc.gpsimd.tensor_tensor(inv[:], var[:], mhalf[:], ALU.pow).then_inc(inv_ready, 1)

            prepare(16, 0, 0, 0)
            with pool.Fori(0, NB) as b:
                for hf in range(NBLK):
                    prepare(blocks(b, hf, 16, 32), blocks(b, hf, 2, 2), blocks(b, hf, 1, 1), (hf + 1) % 2)

        @block.scalar
        def _(act):
            def square(n, t):
                act.wait_ge(sq_sum, n + t)
                nc.scalar.activation(junk[:], x1[:, t, :], ACT.Square, accum_out=ssq[:, t:t + 1]).then_inc(sq_sum, 1)

            def norm_tile(n, k, slot, bank):
                act.wait_ge(g_ready, n + 1)
                nc.scalar.activation(hT[0][:, slot, k, :], psum[bank][:], ACT.Identity, bias=bias_now[:, k:k + 1],
                                     scale=gain_now[:, k:k + 1]).then_inc(g_act, 1)

            def gu_hi(j, slot):
                for w in range(2):
                    nc.scalar.activation(gu[0][:, slot, w, :, :], wT[:, w, :, j * P:(j + 1) * P], ACT.Copy).then_inc(guh, 1)

            for n in range(NW):
                if n % 2 == 0:
                    act.wait_ge(g_ready, n + 1)
                    nc.scalar.activation(weight_place(n), psum[n % GU_BANKS][:], ACT.Copy).then_inc(g_act, 1)
            act.wait_ge(summed, 1)
            for t in range(TPH):
                square(0, t)
            act.wait_ge(norm_now, 2)
            for k in range(KT):
                norm_tile(NW + k, k, 0, (NW + k) % GU_BANKS)
            act.wait_ge(g_act, NW // 2)
            act.wait_ge(g_dve, NW // 2)
            gu_hi(0, 0)
            with act.Fori(0, NB) as b:
                for hf in range(NBLK):
                    for j in range(NJ):
                        act.wait_ge(g_ready, RING(b, ring_tile(hf, j - 1, 1) + 1 if j else
                                                  (ring_tile(hf - 1, NJ - 1, 1) + 1 if hf else 0)))
                        gu_hi((j + 1) % NJ, (j + 1) % 2)
                        act.wait_ge(out_mm, blocks(b, hf, NJ, j - 1 + 2))
                        nc.scalar.activation(wo[0][:, j % 2, :], woT[:, j, :], ACT.Copy).then_inc(woh, 1)
                        n = ring_tile(hf, j, 0)
                        act.wait_ge(g_ready, RING(b, n + 1))
                        act.wait_ge(al, blocks(b, hf, NJ, j - 1 + 2))
                        nc.scalar.activation(sg[:, j % 2, :], psum[n % GU_BANKS][:], ACT.Silu).then_inc(g_act, 1)
                        act.wait_ge(prod, blocks(b, hf, NJ, j + 1))
                        nc.scalar.activation(a[0][:, j % 2, :], sg[:, j % 2, :], ACT.Copy).then_inc(ah, 1)
                        if 2 <= j < 2 + TPH:
                            if j == 2:
                                act.wait_ge(summed, blocks(b, hf, 2, 3))
                                act.wait_ge(var_ready, blocks(b, hf, 1, 1))
                            square(blocks(b, hf, TPH, TPH), j - 2)
                        if j == PREP_J:
                            act.wait_ge(norm_now, blocks(b, hf, 2, 4))
                        if PREP_J <= j < PREP_J + KT:
                            k = j - PREP_J
                            n = ring_tile(hf, j, 2 + k)
                            norm_tile(RING(b, n), k, (hf + 1) % 2, n % GU_BANKS)

        @block.vector
        def _(dve):
            dve.sem_inc(al, 2)
            nc.vector.memset(mhalf[:], -0.5)
            for n in range(NW):
                if n % 2:
                    dve.wait_ge(g_ready, n + 1)
                    nc.vector.tensor_copy(weight_place(n), psum[n % GU_BANKS][:]).then_inc(g_dve, 1)

            def mean_square(n):
                dve.wait_ge(sq_sum, TPH * (n + 1))
                dve.wait_ge(inv_ready, n)
                nc.vector.tensor_scalar(var[:], ssq[:], 1.0 / D, EPS, ALU.mult, ALU.add).then_inc(var_ready, 1)
                return n

            def scale_x(n):
                dve.wait_ge(inv_ready, n + 1)
                dve.wait_ge(summed, 2 * (n + 1))
                for t in range(TPH):
                    nc.vector.tensor_scalar(x1[:, t, :], x1[:, t, :], inv[:, t:t + 1], None, ALU.mult).then_inc(x_scaled, 1)

            def set_norm(nb):
                nc.vector.tensor_copy(gain_now[:], gain[:, bass.ds(nb, 1), :].squeeze(1)).then_inc(norm_now, 1)
                nc.vector.tensor_copy(bias_now[:], bias[:, bass.ds(nb, 1), :].squeeze(1)).then_inc(norm_now, 1)

            def norm_tile(n, n_act, n_full, k, slot, bank):
                dve.wait_ge(g_ready, n + 1)
                dve.wait_ge(g_act, n_act + 1)
                nc.vector.tensor_scalar(hT_full[:, slot, k, :], psum[bank][:], gain_now[:, k:k + 1],
                                        bias_now[:, k:k + 1], ALU.mult, ALU.add).then_inc(full, 1)
                dve.wait_ge(full, n_full + 1)
                nc.vector.tensor_tensor(hT[1][:, slot, k, :], hT_full[:, slot, k, :],
                                        hT[0][:, slot, k, :].bitcast(F32), ALU.subtract).then_inc(g_dve, 1)

            def gu_lo(n, j, slot):
                for w in range(2):
                    dve.wait_ge(guh, n + w + 1)
                    nc.vector.tensor_tensor(gu[1][:, slot, w, :, :], wT[:, w, :, j * P:(j + 1) * P],
                                            gu[0][:, slot, w, :, :].bitcast(F32), ALU.subtract).then_inc(gul, 1)

            mean_square(0)
            scale_x(0)
            set_norm(0)
            dve.wait_ge(norm_now, 2)
            for k in range(KT):
                norm_tile(NW + k, NW // 2 + k, k, k, 0, (NW + k) % GU_BANKS)
            dve.wait_ge(g_act, NW // 2)
            dve.wait_ge(g_dve, NW // 2 + KT)
            gu_lo(0, 0, 0)
            with dve.Fori(0, NB) as b:
                for hf in range(NBLK):
                    for j in range(NJ):
                        gu_lo(blocks(b, hf, 2 * NJ, 2 * (j + 1)), (j + 1) % NJ, (j + 1) % 2)
                        dve.wait_ge(woh, blocks(b, hf, NJ, j + 1))
                        nc.vector.tensor_tensor(wo[1][:, j % 2, :], woT[:, j, :], wo[0][:, j % 2, :].bitcast(F32),
                                                ALU.subtract).then_inc(wol, 1)
                        n = ring_tile(hf, j, 1)
                        dve.wait_ge(g_ready, RING(b, n + 1))
                        dve.wait_ge(g_act, act_ring(b, hf, j) + 1)
                        nc.vector.tensor_tensor(sg[:, j % 2, :], psum[n % GU_BANKS][:], sg[:, j % 2, :],
                                                ALU.mult).then_inc(prod, 1)
                        dve.wait_ge(ah, blocks(b, hf, NJ, j + 1))
                        dve.wait_ge(prod, blocks(b, hf, NJ, j + 1))
                        nc.vector.tensor_tensor(a[1][:, j % 2, :], sg[:, j % 2, :], a[0][:, j % 2, :].bitcast(F32),
                                                ALU.subtract).then_inc(al, 1)
                        if j == 6:
                            mean_square(blocks(b, hf, 1, 1))
                        if j == 7:
                            set_norm(nxt(b, hf)[0])
                            scale_x(blocks(b, hf, 1, 1))
                            dve.wait_ge(norm_now, blocks(b, hf, 2, 4))
                        if PREP_J <= j < PREP_J + KT:
                            k = j - PREP_J
                            n = ring_tile(hf, j, 2 + k)
                            norm_tile(RING(b, n), act_ring(b, hf, j) + 1, blocks(b, hf, KT, KT + k), k,
                                      (hf + 1) % 2, n % GU_BANKS)
                    dve.wait_ge(out_mm, blocks(b, hf, NJ, NJ + 2))
                    for t in range(TPH):
                        nc.vector.tensor_tensor(res[:, hf, t, :], ybank[t][:], res[:, hf, t, :],
                                                ALU.add).then_inc(y_added, 1)

        @block.tensor
        def _(pe):
            pe.sem_inc(out_mm, 2)

            def bank_free(b, hf, n_in):
                kinds = []
                for h in range(NBLK):
                    for j in range(NJ):
                        kinds += [("g", h, j), ("u", h, j)] + ([("t", h, j)] if PREP_J <= j < PREP_J + KT else [])
                m = n_in - GU_BANKS
                if m >= 0:
                    kind, h, j = kinds[m]
                    bb = b
                else:
                    kind, h, j = kinds[m]
                    bb = b - 1
                if kind == "g":
                    pe.wait_ge(g_act, act_ring(bb, h, j) + 1)
                elif kind == "u":
                    pe.wait_ge(prod, blocks(bb, h, NJ, j + 1))
                else:
                    pe.wait_ge(g_act, act_ring(bb, h, j) + 2)
                    pe.wait_ge(g_dve, dve_ring(bb, h, j) + 1)

            for n in range(NW):
                if n >= GU_BANKS:
                    m = n - GU_BANKS
                    pe.wait_ge(g_dve if m % 2 else g_act, m // 2 + 1)
                if n % 4 == 0:
                    pe.wait_ge(raw_loaded[n // 4 % 2], n // 8 * 16 + 16)
                for j in range(4):
                    last = nc.tensor.transpose(psum[n % GU_BANKS][:, j * P:(j + 1) * P],
                                               raw[n // 4 % 2][:, j, n % 4 * P:(n % 4 + 1) * P], ident[:])
                last.then_inc(g_ready, 1)

            def transposes(k, bank):
                for t in range(TPH):
                    last = nc.tensor.transpose(psum[bank][:, t * P:(t + 1) * P], x1[:, t, k * P:(k + 1) * P], ident[:])
                last.then_inc(g_ready, 1)

            pe.wait_ge(g_act, NW // 2)
            pe.wait_ge(g_dve, NW // 2)
            pe.wait_ge(x_scaled, TPH)
            for k in range(KT):
                transposes(k, (NW + k) % GU_BANKS)
            pe.wait_ge(g_act, NW // 2 + KT)
            pe.wait_ge(g_dve, NW // 2 + KT)

            def out_product(b, hf, j):
                for s in (ah, wol):
                    pe.wait_ge(s, blocks(b, hf, NJ, j + 1))
                pe.wait_ge(al, blocks(b, hf, NJ, j + 3))
                if j == 0:
                    pe.wait_ge(y_added, blocks(b, hf, TPH))
                for t in range(TPH):
                    for p, q in ((0, 0), (0, 1), (1, 0)):
                        last = nc.tensor.matmul(ybank[t][:], a[p][:, j % 2, t * P:(t + 1) * P], wo[q][:, j % 2, :],
                                                start=(j == 0 and p == 0 and q == 0),
                                                stop=(j == NJ - 1 and p == 1))
                last.then_inc(out_mm, 1)

            with pe.Fori(0, NB) as b:
                for hf in range(NBLK):
                    for j in range(NJ):
                        pe.wait_ge(gul, blocks(b, hf, 2 * NJ, 2 * (j + 1)))
                        for w in range(2):
                            n = ring_tile(hf, j, w)
                            if n >= GU_BANKS:
                                bank_free(b, hf, n)
                            else:
                                first_tiles_free(pe, b, n)
                            steps = [(k, p, q) for k in range(KT) for p, q in ((0, 0), (0, 1), (1, 0))]
                            for i, (k, p, q) in enumerate(steps):
                                last = nc.tensor.matmul(psum[n % GU_BANKS][:], gu[p][:, j % 2, w, k, :],
                                                        hT[q][:, hf, k, :], start=(i == 0), stop=(i == len(steps) - 1))
                            last.then_inc(g_ready, 1)
                        if PREP_J <= j < PREP_J + KT:
                            k = j - PREP_J
                            n = ring_tile(hf, j, 2 + k)
                            bank_free(b, hf, n)
                            if k == 0:
                                pe.wait_ge(x_scaled, blocks(b, hf, TPH, 2 * TPH))
                            transposes(k, n % GU_BANKS)
                        if j:
                            out_product(b, hf, j - 1)
                    out_product(b, hf, NJ - 1)



def condition_block(nc, x, t, wq, wk, wv, wo, cond, gate_w, up_w, out_w, out):
    attn = nc.dram_tensor("attn_out", (NB, L, D), F32, kind="Internal").ap()
    wv_dram = nc.dram_tensor("wv_parts", (P, 2, KT, D), F32, kind="Internal").ap()
    base = (nc.sbuf_base + 31) // 32 * 32
    sizes = {F32: 4, F32R: 4}

    def plan(start, regions):
        places = {}
        for name, words in regions:
            places[name] = start
            start += (4 * words + 31) // 32 * 32
        return places, start

    small = [("ident", P), ("identr", P), ("ones", DH)] + [(f"cond{m}", NB * KT) for m in range(4)] \
        + [("gain_now", KT), ("bias_now", KT), ("ssq", TPH), ("var", TPH), ("inv", TPH), ("mhalf", TPH)]
    const_at, base = plan(base, small)
    weights_at, after_weights = plan(base, [(f"{n}_{p}", KT * D) for n in ("wq", "wk", "wo") for p in ("hi", "lo")])
    setup_at, _ = plan(after_weights, [("setup_raw", 4 * KT * D), ("setup_wv", 2 * KT * D), ("setup_t", DT),
                                       ("setup_tT", NB), ("setup_gw", 4 * KT * DT), ("setup_gwT", 4 * D),
                                       ("setup_gb", 4 * KT)])
    attention_at, _ = plan(after_weights, [
        ("hT_hi", KT * L), ("hT_lo", KT * L), ("qk_hi", 2 * QB), ("qk_lo", 2 * QB), ("qs", 2 * GH * QB),
        ("ks", 2 * GH * L), ("v", NS * D), ("probs", 2 * GH * QB), ("sums", POOL_HEADS * QB), ("mt", TPH * P),
        ("o", NG * L), ("den", QB), ("x4", TPH * D), ("yout", 2 * D), ("pmax", TPH * GH * NHALF),
        ("mx", TPH * GH), ("dsmall", QB // 32), ("zero", 1), ("indc", GH)])
    ffn_at, _ = plan(base, [
        ("wT", 2 * KT * HID), ("woT", NJ * D), ("gu_hi", 4 * KT * P), ("gu_lo", 4 * KT * P), ("wo_hi2", 2 * D),
        ("wo_lo2", 2 * D), ("h2_hi", 2 * KT * QB), ("h2_lo", 2 * KT * QB), ("x1", TPH * D), ("res", 2 * TPH * D),
        ("sg", 2 * QB), ("a_hi", 2 * QB), ("a_lo", 2 * QB), ("junk", D)])
    places = {**const_at, **weights_at, **setup_at, **attention_at, **ffn_at}

    def at(name, shape, dtype, region):
        return nc.alloc_sbuf_tensor_at(name, shape, dtype, offset=places[region])

    cst = {"at": at, "ident": at("ident", [P, P], F32, "ident"), "identr": at("identr", [P, P], F32R, "identr"),
           "ones": at("ones", [P, DH], F32, "ones"), "gain_now": at("gain_now", [P, KT], F32, "gain_now"),
           "bias_now": at("bias_now", [P, KT], F32, "bias_now"),
           "cond": [at(f"cond{m}", [P, NB, KT], F32, f"cond{m}") for m in range(4)]}
    cst["g1"], cst["b1"], cst["g2"], cst["b2"] = cst["cond"]
    W = [[at(f"{n}_{p}", [P, KT, D], F32R, f"{n}_{p}") for p in ("hi", "lo")] for n in ("wq", "wk", "wo")]
    with ExitStack() as ctx:
        psum = [ctx.enter_context(nc.psum_tensor(f"bank{i}", [P, QB], F32)) for i in range(8)]
        attention_setup(nc, t, [wq, wk, wv, wo], cond, wv_dram, W, cst, psum)
        attention_program(nc, x, attn, wv_dram, W, cst, psum)
        ffn_program(nc, x, attn, gate_w, up_w, out_w, out, cst, psum)


_INS = ["x", "cond_256"] + ["L0_cond_" + n for n in ("Wq", "Wk", "Wv", "Wo", "g1w", "g1b", "b1w", "b1b", "g2w", "g2b",
                                                     "b2w", "b2b", "gate_w", "hid_w", "out_w")]


def kernel(**inputs):
    import concourse.bacc as bacc
    from concourse.bass_utils import run_bass_kernel_spmd

    nc = bacc.Bacc("TRN2", target_bir_lowering=False, num_devices=1)
    arrays, ap = {}, {}
    for name in _INS:
        a = np.ascontiguousarray(inputs[name])
        arrays[f"in_{name}"] = a
        ap[name.replace("L0_cond_", "")] = nc.dram_tensor(f"in_{name}", a.shape, mybir.dt.from_np(a.dtype),
                                                          kind="ExternalInput").ap()
    out = nc.dram_tensor("out_0", (NB, L, D), F32, kind="ExternalOutput").ap()
    cond = [(ap[f"{n}w"], ap[f"{n}b"]) for n in ("g1", "b1", "g2", "b2")]
    condition_block(nc, ap["x"], ap["cond_256"], ap["Wq"], ap["Wk"], ap["Wv"], ap["Wo"], cond,
                    ap["gate_w"], ap["hid_w"], ap["out_w"], out)
    r = run_bass_kernel_spmd(nc, [arrays], core_ids=[0])
    return r.results[0]["out_0"]
```

```python
import numpy as np
import concourse.bass as bass
from concourse import mybir
from contextlib import ExitStack

F32 = mybir.dt.float32
F32R = mybir.dt.float32r
ALU = mybir.AluOpType
ACT = mybir.ActivationFunctionType
AX_X = mybir.AxisListType.X

P = 128
NB, L, D = 4, 1024, 512
H, DH = 16, 32
HID = 2048
DT = 128
EPS = 1e-6
KT = D // P
GH = P // DH
NG = H // GH
QB = 512
NHALF = L // QB
NU = NG * NHALF
NS = L // P
NT = L // P
TPH = QB // P
POOL_HEADS = 3
SB, MB = 3, 2
NMAX = GH * TPH * NHALF
MAX_AT = [0] * GH + [1 if j % 3 else 2 for j in range(1, 1 + (NS - 2) * GH)] + [0] * GH
assert sum(MAX_AT) == NMAX
SCALE = 1.0 / float(np.sqrt(np.float32(DH)))



class Counter:

    def __init__(self, lead, per):
        self.lead, self.per = lead, per

    def __call__(self, b, n):
        if b is None:
            return n
        return b * self.per + (self.lead + n)


def misc_order(body):
    if not body:
        return ([("hT", k, hf) for hf in range(NHALF) for k in range(KT)]
                + [("K", 0, 0), ("K", 0, 1), ("Q", 0), ("Q", 1), ("mT", 0)])
    return [tile for u in range(NU) for s in range(NS) for h in range(GH) for tile in done_at(u, s, h)]


def projected_in(u, s):
    keys, queries = ((3, 5), 6) if u == 6 else ((1, 3), 0 if u == 5 else 5)
    if u % 2 == 0 and s in keys:
        return ("K", u + 2, keys.index(s))
    return ("Q", u + 2) if s == queries else None


def made_at(u, s, h):
    if u == 5 and h == 0 and 1 <= s <= KT:
        return ("hT", s - 1, 0)
    if u == 6 and s in (1, 2) and h % 2 == 0:
        return ("hT", 2 * (s - 1) + h // 2, 1)
    return ("mT", u + 1) if (s, h) == (NS - 1, 1) else None


def done_at(u, s, h):
    tiles = [made_at(u, s, h), projected_in(u, s) if h == GH - 1 else None]
    return [tile for tile in tiles if tile]


LEAD_MISC = misc_order(False)
BODY_MISC = misc_order(True)
MISC = Counter(len(LEAD_MISC), len(BODY_MISC))
LEAD_DVE = [m for m in LEAD_MISC if m[0] != "mT"]
BODY_DVE = [m for m in BODY_MISC if m[0] != "mT"]
MISC_DVE = Counter(len(LEAD_DVE), len(BODY_DVE))
LEAD_PROJ = [m for m in LEAD_MISC if m[0] in "KQ"]
BODY_PROJ = [m for m in BODY_MISC if m[0] in "KQ"]
PROJ = Counter(len(LEAD_PROJ), len(BODY_PROJ))
SCORES_T = Counter(0, NT + NU * NS * GH)
SCORES_Q = Counter(NMAX, NU * NMAX + NT)
LINKS_PER_BATCH = NU * (2 + 3) + NHALF * KT
HEAD_INC = 3 * 16


def misc_index(body, tile):
    return (BODY_MISC if body else LEAD_MISC).index(tile)


def dve_before(body, tile):
    order = BODY_MISC if body else LEAD_MISC
    return sum(m[0] != "mT" for m in order[:order.index(tile)])


def hold(sp, held, semaphore, value):
    sp.wait_ge(semaphore, value)
    sp.sem_inc(held, 1)


def next_batch(b):
    return (b + 1) % NB


def attention_program(nc, x, attn, wv_dram, W, cst, psum):
    (wq, wk, wo) = W
    at = cst["at"]
    ident, identr, ones, gain, bias = cst["ident"], cst["identr"], cst["ones"], cst["g1"], cst["b1"]

    hT = [at("hT_hi", [P, KT, L], F32R, "hT_hi"), at("hT_lo", [P, KT, L], F32R, "hT_lo")]
    hT_full = at("hT_full", [P, KT, L], F32, "hT_lo")
    qk = [at("qk_hi", [P, 2, QB], F32R, "qk_hi"), at("qk_lo", [P, 2, QB], F32R, "qk_lo")]
    qs = at("qs", [P, 2, GH, QB], F32R, "qs")
    ks = at("ks", [P, 2, GH, L], F32R, "ks")
    v = at("v", [P, NS, D], F32, "v")
    probs = at("probs", [P, 2, GH, QB], F32, "probs")
    wv = at("wv", [P, 2, KT, D], F32R, "probs")
    sums = at("sums", [P, POOL_HEADS, QB], F32, "sums")
    mt = at("mt", [P, TPH, P], F32R, "mt")
    o = at("o", [P, NG, L], F32, "o")
    den = at("den", [P, QB], F32, "den")
    x4 = at("x4", [P, TPH, D], F32, "x4")
    osplit = at("osplit", [P, 2, 2, NG, P], F32R, "x4")
    yout = at("yout", [P, 2, D], F32, "yout")
    pmax = at("pmax", [P, TPH, GH, NHALF], F32, "pmax")
    mx = at("mx", [P, TPH, GH], F32, "mx")
    ssq = at("ssq", [P, TPH], F32, "ssq")
    var = at("var", [P, TPH], F32, "var")
    inv = at("inv", [P, TPH], F32, "inv")
    mhalf = at("mhalf", [P, TPH], F32, "mhalf")
    dsmall = at("dsmall", [P, QB // 32], F32, "dsmall")
    zero = at("zero", [P, 1], F32, "zero")
    indc = at("indc", [P, GH], F32, "indc")

    sbank = psum[0:SB]
    mbank = psum[SB:SB + MB]
    obank, dbank, wbank = psum[5], psum[6], psum[7]

    with ExitStack() as ctx:
        def sem(name):
            return ctx.enter_context(nc.semaphore(name))

        held = sem("held")
        x_loaded = sem("x_loaded")
        wv_loaded = sem("wv_loaded")
        st_ready = sem("st_ready")
        st_done = sem("st_done")
        sq_ready = sem("sq_ready")
        sq_done = sem("sq_done")
        w_ready = sem("w_ready")
        w_act = sem("w_act")
        w_dve = sem("w_dve")
        q_stacked = [sem(f"q_stacked{h}") for h in range(GH)]
        k_stacked = [sem(f"k_stacked{hf}") for hf in range(NHALF)]
        m_rows = sem("m_rows")
        pv_done = sem("pv_done")
        sum_done = sem("sum_done")
        mt_ready = sem("mt_ready")
        od_act = sem("od_act")
        d_ready = sem("d_ready")
        on_done = sem("on_done")
        os_act = sem("os_act")
        os_dve = sem("os_dve")
        y_stored = [sem("y_stored0"), sem("y_stored1")]
        sq_sum = sem("sq_sum")
        var_ready = sem("var_ready")
        inv_ready = sem("inv_ready")
        x_scaled = sem("x_scaled")
        const_pool = sem("const_pool")
        const_dve = sem("const_dve")
        dve_step = sem("dve_step")
        block = ctx.enter_context(nc.Block())

        def proj_index(body, tile):
            return (BODY_PROJ if body else LEAD_PROJ).index(tile)

        @block.sync
        def _(sp):
            def load_x(b, hf, src_b):
                if hf == 1:
                    body = b is not None
                    hold(sp, held, w_ready, MISC(b, misc_index(body, ("hT", KT - 1, 0)) + 1))
                elif b is not None:
                    hold(sp, held, sq_ready, SCORES_Q(b, 0))
                sp.dma_start(x4[:], x[src_b, hf * QB:(hf + 1) * QB, :].rearrange("(t p) d -> p t d", p=P)) \
                    .then_inc(x_loaded, 16)

            def stack(b, tile, slot, half=0):
                if tile == ("Q", 1) and b is not None:
                    src = 1
                    hold(sp, held, w_dve, MISC_DVE(b, 0))
                else:
                    src = proj_index(b is not None, tile) % 2
                    hold(sp, held, w_dve, MISC_DVE(b, dve_before(b is not None, tile) + 1))
                for h in range(GH):
                    rows = slice(DH * h, DH * h + DH)
                    for part, to in ((0, 0), (1, 1), (0, 2)) if tile[0] == "Q" else ((0, 0), (0, 1), (1, 2)):
                        to = slice(DH * to, DH * to + DH)
                        if tile[0] == "Q":
                            sp.dma_start(qs[to, slot, h, :].bitcast(F32), qk[part][rows, src, :].bitcast(F32)) \
                                .then_inc(q_stacked[h], 16)
                        else:
                            sp.dma_start(ks[to, slot, h, half * QB:(half + 1) * QB].bitcast(F32),
                                         qk[part][rows, src, :].bitcast(F32)).then_inc(k_stacked[half], 16)

            def load_wv():
                sp.dma_start(wv[:].bitcast(F32), wv_dram).then_inc(wv_loaded, 16)

            for s in y_stored:
                sp.sem_inc(s, 16)
            load_x(None, 0, 0)
            load_wv()
            load_x(None, 1, 0)
            stack(None, ("K", 0, 0), 0, 0)
            stack(None, ("K", 0, 1), 0, 1)
            stack(None, ("Q", 0), 0)
            with sp.Fori(0, NB) as b:
                prepared = sp.snap(next_batch(b))
                for u in range(NU):
                    if u:
                        hold(sp, held, st_ready, SCORES_T(b, NT + u * NS * GH))
                    else:
                        hold(sp, held, w_ready, MISC(b, 0))
                        hold(sp, held, sq_ready, SCORES_Q(b, 0))
                    stack(b, ("Q", u + 1), (u + 1) % 2)
                    if u % 2 == 0:
                        for hf in range(NHALF):
                            stack(b, ("K", u + 2, hf), (u // 2 + 1) % 2, hf)
                    if u == 3:
                        load_x(b, 0, prepared)
                    if u == 5:
                        load_x(b, 1, prepared)
                hold(sp, held, pv_done, b * (NU * NS) + NU * NS + 2)
                hold(sp, held, sum_done, b * (NU * NS) + NU * NS + 2)
                load_wv()
                for t in range(NT):
                    hold(sp, held, sq_done, SCORES_Q(b, NU * NMAX + t + 1) + MB)
                    sp.dma_start(attn[b, t * P:(t + 1) * P, :], yout[:, t % 2, :]).then_inc(y_stored[t % 2], 16)
            for s in y_stored:
                hold(sp, held, s, (NB * (NT // 2) + 1) * 16)
            hold(sp, held, wv_loaded, (NB + 1) * 16)

        @block.gpsimd
        def _(pool):
            nc.gpsimd.memset(mhalf[:], -0.5).then_inc(const_pool, 1)
            nc.gpsimd.memset(zero[:], 0.0).then_inc(const_pool, 1)
            pool.sem_inc(sum_done, 2)
            pool.wait_ge(const_pool, 2)

            def inverse_root(b, n):
                pool.wait_ge(var_ready, n + 1)
                nc.gpsimd.tensor_tensor(inv[:], var[:], mhalf[:], ALU.pow).then_inc(inv_ready, 1)

            inverse_root(None, 0)
            inverse_root(None, 1)
            with pool.Fori(0, NB) as b:
                for u in range(NU):
                    for s in range(NS):
                        n = u * NS + s
                        if (u, s) == (4, 6):
                            inverse_root(b, b * 2 + 2)
                        if (u, s) == (5, 7):
                            inverse_root(b, b * 2 + 3)
                        pool.wait_ge(st_done, SCORES_T(b, NT + (n * GH) + POOL_HEADS) + SB)
                        if s == 0:
                            pool.wait_ge(d_ready, b * NU + (u + 1))
                        pool.wait_ge(sum_done, b * (NU * NS) + n + 2)
                        prev = sums[:] if s else zero[:, 0:1].unsqueeze(2).to_broadcast([P, POOL_HEADS, QB])
                        nc.gpsimd.tensor_tensor(sums[:], probs[:, s % 2, 0:POOL_HEADS, :], prev, ALU.add) \
                            .then_inc(sum_done, 1)

        @block.scalar
        def _(act):
            act.sem_inc(st_done, SB)
            act.sem_inc(od_act, 2)

            def square(b, hf, t):
                n = (0 if b is None else b * 8 + 8) + (4 * hf + t)
                if t == 0:
                    act.wait_ge(x_loaded, 16 * (hf + 1) if b is None else b * 32 + 32 + 16 * (hf + 1))
                    if b is not None and hf == 0:
                        for s in y_stored:
                            act.wait_ge(s, b * (NT // 2 * 16) + 16)
                    if b is not None or hf:
                        act.wait_ge(var_ready, hf if b is None else b * 2 + 2 + hf)
                if b is not None or n:
                    act.wait_ge(sq_sum, n)
                nc.scalar.activation(yout[:, 0, :], x4[:, t, :], ACT.Square,
                                     accum_out=ssq[:, t:t + 1]).then_inc(sq_sum, 1)

            def work_tile(b, tile):
                body = b is not None
                i = misc_index(body, tile)
                act.wait_ge(w_ready, MISC(b, i + 1))
                if tile[0] == "hT":
                    _, k, hf = tile
                    nc.scalar.activation(hT[0][:, k, hf * QB:(hf + 1) * QB], wbank[:], ACT.Identity,
                                         bias=cur_bias[:, k:k + 1],
                                         scale=cur_gain[:, k:k + 1]).then_inc(w_act, 1)
                elif tile[0] == "mT":
                    slot = tile[1] % 2
                    rows = wbank[96:128, :].unsqueeze(1).to_broadcast([32, GH // 2, QB])
                    nc.scalar.activation(qs[96:128, slot, 0:GH // 2, :], rows, ACT.Copy).then_inc(m_rows, 1)
                    nc.scalar.activation(qs[96:128, slot, GH // 2:GH, :], rows, ACT.Copy).then_inc(w_act, 1)
                else:
                    n = proj_index(body, tile)
                    if b is None:
                        if tile[0] == "Q":
                            act.wait_ge(k_stacked[n % 2], GH * HEAD_INC)
                    elif tile[0] == "K":
                        u = tile[1] - 2
                        for s in q_stacked:
                            act.wait_ge(s, b * (NU * HEAD_INC) + (u + 1 + tile[2]) * HEAD_INC)
                    else:
                        u = tile[1] - 2
                        act.wait_ge(k_stacked[n % 2], b * (NG * GH * HEAD_INC) + (u // 2 + 2) * (GH * HEAD_INC))
                    nc.scalar.activation(qk[0][:, n % 2, :], wbank[:], ACT.Copy).then_inc(w_act, 1)

            cur_gain, cur_bias = cst["gain_now"], cst["bias_now"]

            def output(b, u):
                act.wait_ge(pv_done, b * (NU * NS) + (u + 1) * NS + 2)
                if u == 0:
                    act.wait_ge(sq_ready, SCORES_Q(b, 0))
                g, hf = u // 2, u % 2
                nc.scalar.activation(o[:, g, hf * QB:(hf + 1) * QB], obank[:], ACT.Copy).then_inc(od_act, 1)
                act.wait_ge(on_done, b * NU + (u + 1))
                nc.scalar.activation(den[96:128, :], dbank[96:128, :], ACT.Copy).then_inc(od_act, 1)

            def denominators(b, u):
                act.wait_ge(d_ready, b * NU + (u + 2))
                nc.scalar.activation(den[0:96, :], dbank[0:96, :], ACT.Copy).then_inc(od_act, 1)

            for t in range(TPH):
                square(None, 0, t)
            act.wait_ge(const_dve, 3)
            for tile in LEAD_MISC[:KT]:
                work_tile(None, tile)
            for t in range(TPH):
                square(None, 1, t)
            for tile in LEAD_MISC[KT:]:
                work_tile(None, tile)
            with act.Fori(0, NB) as b:
                for t in range(NT):
                    act.wait_ge(st_ready, SCORES_T(b, t + 1))
                    if t == 0:
                        act.wait_ge(pv_done, b * (NU * NS) + 2)
                    nc.scalar.activation(v[:, t, :], sbank[t % SB][:], ACT.Copy).then_inc(st_done, 1)
                for u in range(NU):
                    for s in range(NS):
                        n = u * NS + s
                        act.wait_ge(pv_done, b * (NU * NS) + n + 1)
                        act.wait_ge(sum_done, b * (NU * NS) + n + 1)
                        if u == 5 and s == 0:
                            act.wait_ge(const_dve, b * 2 + 5)
                        for h in range(GH):
                            i = NT + n * GH + h
                            act.wait_ge(st_ready, SCORES_T(b, i + 1))
                            nc.scalar.activation(probs[:, s % 2, h, :], sbank[i % SB][:], ACT.Exp,
                                                 scale=SCALE).then_inc(st_done, 1)
                            if (u, s) == (4, 5):
                                square(b, 0, h)
                            if (u, s) == (5, 6):
                                square(b, 1, h)
                            for tile in done_at(u, s, h):
                                work_tile(b, tile)
                            if (s, h) == (2, 1) and u:
                                denominators(b, u - 1)
                        if s == 0 and u:
                            output(b, u - 1)
                output(b, NU - 1)
                for t in range(NT):
                    act.wait_ge(on_done, b * NU + (NU if t < TPH else NU + 1))
                    if t >= 2:
                        act.wait_ge(sq_ready, SCORES_Q(b, NU * NMAX + t - 1))
                    nc.scalar.activation(osplit[:, t % 2, 0, :, :], o[:, :, t * P:(t + 1) * P],
                                         ACT.Copy).then_inc(os_act, 1)
                    if t == 1:
                        denominators(b, NU - 1)

        @block.vector
        def _(dve):
            class Link:
                lead = 0
                n = 0
                b = None

            def link(ins):
                ins.then_inc(dve_step, 1)
                Link.n += 1
                dve.wait_ge(dve_step, Link.n if Link.b is None else Link.b * LINKS_PER_BATCH + (Link.lead + Link.n))

            dve.sem_inc(sq_done, MB)
            dve.sem_inc(on_done, 1)
            link(nc.vector.tensor_tensor(indc[96:128, :], ident[96:128, 96:96 + 2 * GH:2],
                                         ident[96:128, 97:97 + 2 * GH:2], ALU.add))
            for sl in range(2):
                for h in range(GH):
                    link(nc.vector.tensor_copy(ks[96:128, sl, h, :], indc[96:128, h:h + 1].to_broadcast([32, L])))
            nc.vector.tensor_scalar(mt[:], mt_zero_source(ident), 0.0, None, ALU.mult).then_inc(const_dve, 1)
            cur_gain, cur_bias = cst["gain_now"], cst["bias_now"]
            nc.vector.tensor_copy(cur_gain[:], gain[:, 0, :]).then_inc(const_dve, 1)
            nc.vector.tensor_copy(cur_bias[:], bias[:, 0, :]).then_inc(const_dve, 1)
            dve.wait_ge(const_dve, 3)

            def mean_square(b, hf):
                n = hf if b is None else b * 2 + 2 + hf
                dve.wait_ge(sq_sum, 4 * (n + 1))
                dve.wait_ge(inv_ready, n)
                nc.vector.tensor_scalar(var[:], ssq[:], 1.0 / D, EPS, ALU.mult, ALU.add).then_inc(var_ready, 1)

            def scale_x(b, hf, t):
                n = hf if b is None else b * 2 + 2 + hf
                dve.wait_ge(inv_ready, n + 1)
                nc.vector.tensor_scalar(x4[:, t, :], x4[:, t, :], inv[:, t:t + 1], None, ALU.mult).then_inc(x_scaled, 1)

            def work_tile(b, tile):
                body = b is not None
                dve.wait_ge(w_ready, MISC(b, misc_index(body, tile) + 1))
                dve.wait_ge(w_act, MISC(b, misc_index(body, tile) + 1))
                if tile[0] == "hT":
                    _, k, hf = tile
                    cols = slice(hf * QB, (hf + 1) * QB)
                    link(nc.vector.tensor_scalar(hT_full[:, k, cols], wbank[:], cur_gain[:, k:k + 1],
                                                 cur_bias[:, k:k + 1], ALU.mult, ALU.add))
                    nc.vector.tensor_tensor(hT[1][:, k, cols], hT_full[:, k, cols],
                                            hT[0][:, k, cols].bitcast(F32), ALU.subtract).then_inc(w_dve, 1)
                else:
                    n = proj_index(body, tile)
                    nc.vector.tensor_tensor(qk[1][:, n % 2, :], wbank[:], qk[0][:, n % 2, :].bitcast(F32),
                                            ALU.subtract).then_inc(w_dve, 1)

            def max_tile(b, n, i):
                h, t, hf = i // (TPH * NHALF), i // NHALF % TPH, i % NHALF
                dve.wait_ge(sq_ready, SCORES_Q(b, n + 1) if b is not None else n + 1)
                nc.vector.reduce_max(pmax[:, t, h, hf:hf + 1], mbank[n % MB][:], AX_X).then_inc(sq_done, 1)

            def maxima(b, u, n):
                dve.wait_ge(sq_done, (SCORES_Q(b, n) if b is not None else n) + MB)
                link(nc.vector.tensor_tensor(mx[:], pmax[:, :, :, 0], pmax[:, :, :, 1], ALU.max))
                if b is not None:
                    dve.wait_ge(w_ready, MISC(b, misc_index(True, ("mT", u))) + 1 if u else MISC(b, 0))
                hi, lo = mt[:, :, 96:96 + 2 * GH:2], mt[:, :, 97:97 + 2 * GH:2]
                link(nc.vector.tensor_scalar(hi, mx[:], -1.0, None, ALU.mult))
                nc.vector.scalar_tensor_tensor(lo, mx[:], -1.0, hi.bitcast(F32), ALU.mult,
                                               ALU.subtract).then_inc(mt_ready, 1)

            def normalise(b, u, part):
                g, hf = u // 2, u % 2
                if part == 0:
                    dve.wait_ge(od_act, b * (3 * NU) + (3 * (u + 1) + 2))
                    link(nc.vector.transpose(den[:], den[:]))
                elif part == 1:
                    cols = den[:].rearrange("p (c i) -> p c i", i=32)
                    link(nc.vector.reciprocal(dsmall[:], cols[:, :, 0]))
                elif part == 2:
                    link(nc.vector.transpose(den[:], dsmall[:].unsqueeze(2).to_broadcast([P, QB // 32, 32])))
                else:
                    cols = o[:, g, hf * QB:(hf + 1) * QB]
                    nc.vector.tensor_tensor(cols, cols, den[:], ALU.mult).then_inc(on_done, 1)

            mean_square(None, 0)
            for t in range(TPH):
                scale_x(None, 0, t)
            for tile in LEAD_MISC[:KT]:
                work_tile(None, tile)
            mean_square(None, 1)
            for t in range(TPH):
                scale_x(None, 1, t)
            for tile in LEAD_MISC[KT:-1]:
                work_tile(None, tile)
            for i in range(NMAX):
                max_tile(None, i, i)
            maxima(None, 0, NMAX)

            Link.lead, Link.n = Link.n, 0
            with dve.Fori(0, NB) as b:
                Link.b = b
                for u in range(NU):
                    done = 0
                    if u == 0:
                        dve.wait_ge(mt_ready, b * NU + 1)
                    for s in range(NS):
                        if (u, s) == (4, 0):
                            nb = next_batch(b)
                            nc.vector.tensor_copy(cur_gain[:], gain[:, bass.ds(nb, 1), :].squeeze(1)).then_inc(const_dve, 1)
                            nc.vector.tensor_copy(cur_bias[:], bias[:, bass.ds(nb, 1), :].squeeze(1)).then_inc(const_dve, 1)
                        if (u, s) == (4, 6):
                            mean_square(b, 0)
                        if (u, s) == (5, 7):
                            mean_square(b, 1)
                        if (u, s) == (5, 0):
                            dve.wait_ge(const_dve, b * 2 + 5)
                        for h in range(GH):
                            for _ in range(MAX_AT[s * GH + h]):
                                max_tile(b, u * NMAX + done, done)
                                done += 1
                            if (s, h) == (NS - 1, 0):
                                maxima(b, u, (u + 1) * NMAX)
                            if (u, s) == (4, 7):
                                scale_x(b, 0, h)
                            if (u, s) == (6, 0):
                                scale_x(b, 1, h)
                            for tile in done_at(u, s, h):
                                if tile[0] != "mT":
                                    work_tile(b, tile)
                            if s == 3 and u:
                                normalise(b, u - 1, h)
                    dve.wait_ge(mt_ready, b * NU + u + 2)

                def lo_part(t):
                    dve.wait_ge(os_act, b * NT + t + 1)
                    nc.vector.tensor_tensor(osplit[:, t % 2, 1, :, :], o[:, :, t * P:(t + 1) * P],
                                            osplit[:, t % 2, 0, :, :].bitcast(F32), ALU.subtract).then_inc(os_dve, 1)

                def out_tile(t):
                    n = NU * NMAX + t
                    dve.wait_ge(sq_ready, SCORES_Q(b, n + 1))
                    dve.wait_ge(y_stored[t % 2], b * (NT // 2 * 16) + (t // 2 + 1) * 16)
                    nc.vector.tensor_copy(yout[:, t % 2, :], mbank[n % MB][:]).then_inc(sq_done, 1)

                lo_part(0)
                lo_part(1)
                out_tile(0)
                lo_part(2)
                out_tile(1)
                lo_part(3)
                for part in range(4):
                    normalise(b, NU - 1, part)
                for t in range(2, NT):
                    out_tile(t)
                    if t + 2 < NT:
                        lo_part(t + 2)
            assert Link.n == LINKS_PER_BATCH, Link.n

        @block.tensor
        def _(pe):
            def product3_part(out, lhs, rhs, k, kdim, last_sem):
                for a, c in ((0, 0), (0, 1), (1, 0)):
                    last = nc.tensor.matmul(out, lhs(a, k), rhs(c, k), start=(k == 0 and a == 0 and c == 0),
                                            stop=(k == kdim - 1 and a == 1))
                if k == kdim - 1:
                    last.then_inc(last_sem, 1)

            def product3(out, lhs, rhs, kdim, last_sem):
                for k in range(kdim):
                    product3_part(out, lhs, rhs, k, kdim, last_sem)

            def work_bank_empty(b, tile):
                i = misc_index(b is not None, tile)
                if b is not None or i:
                    pe.wait_ge(w_act, MISC(b, i))
                    if b is not None or dve_before(False, tile):
                        pe.wait_ge(w_dve, MISC_DVE(b, dve_before(b is not None, tile)))

            def project(b, tile, k):
                if k == 0:
                    work_bank_empty(b, tile)
                w = wq if tile[0] == "Q" else wk
                g = 0 if b is None else tile[1] // 2 % NG
                hf = tile[1] % 2 if tile[0] == "Q" else tile[2]
                product3_part(wbank[:], lambda a, k: w[a][:, k, g * P:(g + 1) * P],
                              lambda c, k: hT[c][:, k, hf * QB:(hf + 1) * QB], k, KT, w_ready)

            def work_tile(b, tile):
                work_bank_empty(b, tile)
                if tile[0] == "hT":
                    _, k, hf = tile
                    if k == 0:
                        pe.wait_ge(x_scaled, TPH * (hf + 1) if b is None else b * 8 + 8 + TPH * (hf + 1))
                    for j in range(TPH):
                        last = nc.tensor.transpose(wbank[:, j * P:(j + 1) * P], x4[:, j, k * P:(k + 1) * P], ident[:])
                else:
                    pe.wait_ge(mt_ready, 1 if b is None else b * NU + (tile[1] + 1))
                    for j in range(TPH):
                        last = nc.tensor.matmul(wbank[:, j * P:(j + 1) * P], mt[:, j, :], identr[:],
                                                start=True, stop=True)
                last.then_inc(w_ready, 1)

            def max_tile(b, n, i, g, u):
                h, t, hf = i // (TPH * NHALF), i // NHALF % TPH, i % NHALF
                pe.wait_ge(sq_done, SCORES_Q(b, n + 1) if b is not None else n + 1)
                nc.tensor.matmul(mbank[n % MB][:], qs[0:96, u % 2, h, t * P:(t + 1) * P],
                                 ks[0:96, g % 2, h, hf * QB:(hf + 1) * QB], start=True, stop=True).then_inc(sq_ready, 1)

            def denominators(b, u):
                pe.wait_ge(sum_done, b * (NU * NS) + (u + 1) * NS + 2)
                pe.wait_ge(od_act, b * (3 * NU) + (3 * u + 2))
                for h in range(POOL_HEADS):
                    last = nc.tensor.matmul(dbank[DH * h:DH * h + DH, :], ones[:], sums[:, h, :], start=True, stop=True)
                last.then_inc(d_ready, 1)

            def values(b, u, s):
                g = u // 2
                pe.wait_ge(st_done, SCORES_T(b, NT + (u * NS + s + 1) * GH) + SB)
                if s == 0:
                    pe.wait_ge(od_act, b * (3 * NU) + (3 * u + 1))
                for h in range(GH):
                    nc.tensor.matmul(obank[DH * h:DH * h + DH, :], v[:, s, (g * GH + h) * DH:(g * GH + h + 1) * DH],
                                     probs[:, s % 2, h, :], start=(s == 0), stop=(s == NS - 1))
                for h in range(POOL_HEADS, GH):
                    last = nc.tensor.matmul(dbank[DH * h:DH * h + DH, :], ones[:], probs[:, s % 2, h, :],
                                            start=(s == 0), stop=(s == NS - 1))
                last.then_inc(pv_done, 1)

            pe.sem_inc(pv_done, 2)
            pe.sem_inc(d_ready, 1)
            for tile in LEAD_MISC[:-1]:
                if tile[0] == "hT":
                    work_tile(None, tile)
                else:
                    for k in range(KT):
                        project(None, tile, k)
            for s in k_stacked:
                pe.wait_ge(s, GH * HEAD_INC)
            for s in q_stacked:
                pe.wait_ge(s, HEAD_INC)
            for i in range(NMAX):
                max_tile(None, i, i, 0, 0)
            work_tile(None, ("mT", 0))
            with pe.Fori(0, NB) as b:
                pe.wait_ge(wv_loaded, b * 16 + 16)
                for t in range(NT):
                    pe.wait_ge(st_done, SCORES_T(b, t + 1))
                    product3(sbank[t % SB][:], lambda a, k: hT[a][:, k, t * P:(t + 1) * P],
                             lambda c, k: wv[:, c, k, :], KT, st_ready)
                for u in range(NU):
                    g = u // 2
                    done = 0
                    for s in range(NS):
                        for h in range(GH):
                            if s == 0 and h == 0:
                                pe.wait_ge(m_rows, b * NU + (u + 1))
                            if s == 0 and h == GH // 2:
                                pe.wait_ge(w_act, MISC(b, misc_index(True, ("mT", u)) + 1 if u else 0))
                            i = NT + (u * NS + s) * GH + h
                            pe.wait_ge(st_done, SCORES_T(b, i + 1))
                            nc.tensor.matmul(sbank[i % SB][:], ks[:, g % 2, h, s * P:(s + 1) * P],
                                             qs[:, u % 2, h, :], start=True, stop=True).then_inc(st_ready, 1)
                            for _ in range(MAX_AT[s * GH + h]):
                                if done % (TPH * NHALF) == 0:
                                    pe.wait_ge(q_stacked[done // (TPH * NHALF)],
                                               b * (NU * HEAD_INC) + (u + 2) * HEAD_INC)
                                if done == 0 and u % 2:
                                    for sem_k in k_stacked:
                                        pe.wait_ge(sem_k, b * (NG * GH * HEAD_INC) + (g + 2) * (GH * HEAD_INC))
                                max_tile(b, u * NMAX + done, done, (u + 1) // 2, u + 1)
                                done += 1
                            tile = projected_in(u, s)
                            if tile:
                                project(b, tile, h)
                            tile = made_at(u, s, h)
                            if tile:
                                work_tile(b, tile)
                            if h == 1 and (u or s):
                                values(b, u if s else u - 1, (s - 1) % NS)
                            if (s, h) == (1, GH - 1) and u:
                                denominators(b, u - 1)
                values(b, NU - 1, NS - 1)
                for t in range(NT):
                    pe.wait_ge(sq_done, SCORES_Q(b, NU * NMAX + t + 1))
                    pe.wait_ge(os_act, b * NT + t + 1)
                    pe.wait_ge(os_dve, b * NT + t + 1)
                    product3(mbank[(NU * NMAX + t) % MB][:], lambda a, k: osplit[:, t % 2, a, k, :],
                             lambda c, k: wo[c][:, k, :], NG, sq_ready)
                    if t == 1:
                        denominators(b, NU - 1)


def mt_zero_source(ident):
    return ident[:, 0:P].unsqueeze(1).to_broadcast([P, TPH, P])


def attention_setup(nc, t_in, W_in, cond_in, wv_dram, W, cst, psum):
    at = cst["at"]
    ident, identr, ones = cst["ident"], cst["identr"], cst["ones"]
    raw = at("w_raw", [P, 4, KT, D], F32, "setup_raw")
    wvs = at("wv_split", [P, 2, KT, D], F32R, "setup_wv")
    t_sb = at("t_sb", [NB, DT], F32, "setup_t")
    t_T = at("t_T", [P, NB], F32, "setup_tT")
    gw = at("gw", [P, 4, KT, DT], F32, "setup_gw")
    gwT = at("gwT", [P, 4, D], F32, "setup_gwT")
    gb = at("gb", [P, 4, KT], F32, "setup_gb")
    parts = [W[0], W[1], [wvs[:, 0, :, :], wvs[:, 1, :, :]], W[2]]
    RING = 4
    with ExitStack() as ctx:
        def sem(name):
            return ctx.enter_context(nc.semaphore(name))

        id_step = sem("id_step")
        cond_loaded = sem("cond_loaded")
        w_loaded = [sem(f"w_loaded{i}") for i in range(4)]
        t_ready = sem("t_ready")
        t_act = sem("t_act")
        t_dve = sem("t_dve")
        wv_stored = sem("wv_stored")
        block = ctx.enter_context(nc.Block())
        tiles = ([("tT",)] + [("gwT", m) for m in range(4)] + [("cond", m) for m in range(4)]
                 + [("w", w, k) for w in (2, 0, 1, 3) for k in range(KT)])

        @block.gpsimd
        def _(pool):
            nc.gpsimd.memset(ident[:], 0.0).then_inc(id_step, 1)
            nc.gpsimd.memset(ones[:], 1.0).then_inc(id_step, 1)
            pool.wait_ge(id_step, 2)
            nc.gpsimd.affine_select(out=ident[:], in_=ident[:], compare_op=ALU.not_equal, fill=1.0, base=0,
                                    pattern=[[-1, P]], channel_multiplier=1).then_inc(id_step, 1)

        @block.sync
        def _(sp):
            sp.dma_start(t_sb[:], t_in).then_inc(cond_loaded, 16)
            for m in range(4):
                sp.dma_start(gw[:, m, :, :], cond_in[m][0].rearrange("(k p) t -> p k t", p=P)).then_inc(cond_loaded, 16)
                with nc.allow_non_contiguous_dma(reason="512 bias values, once"):
                    sp.dma_start(gb[:, m, :], cond_in[m][1].rearrange("(k p) -> p k", p=P)).then_inc(cond_loaded, 16)
            for w in (2, 0, 1, 3):
                sp.dma_start(raw[:, w, :, :], W_in[w].rearrange("(j p) d -> p j d", p=P)).then_inc(w_loaded[w], 16)
            n = tiles.index(("w", 2, KT - 1)) + 1
            sp.wait_ge(t_dve, n)
            sp.dma_start(wv_dram, wvs[:].bitcast(F32)).then_inc(wv_stored, 16)
            sp.wait_ge(wv_stored, 16)

        @block.tensor
        def _(pe):
            pe.wait_ge(id_step, 3)
            pe.wait_ge(cond_loaded, 16 * 9)
            for n, tile in enumerate(tiles):
                if n >= RING:
                    pe.wait_ge(t_act, n - RING + 1)
                    pe.wait_ge(t_dve, n - RING + 1)
                bank = psum[n % RING]
                if tile[0] == "tT":
                    last = nc.tensor.transpose(bank[:, 0:NB], t_sb[:], ident[0:NB, 0:NB])
                elif tile[0] == "gwT":
                    for k in range(KT):
                        last = nc.tensor.transpose(bank[:, k * P:(k + 1) * P], gw[:, tile[1], k, :], ident[:])
                elif tile[0] == "cond":
                    pe.wait_ge(t_dve, tiles.index(("gwT", tile[1])) + 1)
                    for k in range(KT):
                        last = nc.tensor.matmul(bank[:, k * NB:(k + 1) * NB], gwT[:, tile[1], k * P:(k + 1) * P],
                                                t_T[:], start=True, stop=True)
                else:
                    _, w, k = tile
                    if k == 0:
                        pe.wait_ge(w_loaded[w], 16)
                    for j in range(KT):
                        last = nc.tensor.transpose(bank[:, j * P:(j + 1) * P], raw[:, w, j, k * P:(k + 1) * P], ident[:])
                last.then_inc(t_ready, 1)

        @block.scalar
        def _(act):
            for n, tile in enumerate(tiles):
                act.wait_ge(t_ready, n + 1)
                if tile[0] == "w":
                    nc.scalar.activation(parts[tile[1]][0][:, tile[2], :], psum[n % RING][:], ACT.Copy).then_inc(t_act, 1)
                else:
                    act.sem_inc(t_act, 1)

        @block.vector
        def _(dve):
            dve.wait_ge(id_step, 3)
            nc.vector.tensor_copy(identr[:], ident[:])
            for n, tile in enumerate(tiles):
                bank = psum[n % RING]
                dve.wait_ge(t_ready, n + 1)
                if tile[0] == "tT":
                    ins = nc.vector.tensor_copy(t_T[:], bank[:, 0:NB])
                elif tile[0] == "gwT":
                    ins = nc.vector.tensor_copy(gwT[:, tile[1], :], bank[:])
                elif tile[0] == "cond":
                    dve.wait_ge(cond_loaded, 16 * 9)
                    ins = nc.vector.tensor_tensor(cst["cond"][tile[1]][:].rearrange("p b k -> p k b"),
                                                  bank[:, 0:KT * NB].rearrange("p (k b) -> p k b", b=NB),
                                                  gb[:, tile[1], :].unsqueeze(2).to_broadcast([P, KT, NB]), ALU.add)
                else:
                    dve.wait_ge(t_act, n + 1)
                    hi, lo = parts[tile[1]]
                    ins = nc.vector.tensor_tensor(lo[:, tile[2], :], bank[:], hi[:, tile[2], :].bitcast(F32), ALU.subtract)
                ins.then_inc(t_dve, 1)


NJ = HID // P
NBLK = L // QB
PREP_J = 8
GU_BANKS = 4


def ffn_program(nc, x, attn, gate_w, up_w, out_w, out, cst, psum):
    at = cst["at"]
    ident, gain, bias = cst["ident"], cst["g2"], cst["b2"]
    gain_now, bias_now = cst["gain_now"], cst["bias_now"]
    wT = at("wT", [P, 2, KT, HID], F32, "wT")
    woT = at("woT", [P, NJ, D], F32, "woT")
    gu = [at("gu_hi", [P, 2, 2, KT, P], F32R, "gu_hi"), at("gu_lo", [P, 2, 2, KT, P], F32R, "gu_lo")]
    wo = [at("wo_hi", [P, 2, D], F32R, "wo_hi2"), at("wo_lo", [P, 2, D], F32R, "wo_lo2")]
    hT = [at("h2_hi", [P, 2, KT, QB], F32R, "h2_hi"), at("h2_lo", [P, 2, KT, QB], F32R, "h2_lo")]
    hT_full = at("h2_full", [P, 2, KT, QB], F32, "h2_lo")
    raw = [at("raw0", [P, 2, 4, QB], F32, "h2_hi")[:, 1, :, :], at("raw1", [P, 2, 4, QB], F32, "h2_lo")[:, 1, :, :]]
    x1 = at("x1", [P, TPH, D], F32, "x1")
    res = at("res", [P, 2, TPH, D], F32, "res")
    sg = at("sg", [P, 2, QB], F32, "sg")
    a = [at("a_hi", [P, 2, QB], F32R, "a_hi"), at("a_lo", [P, 2, QB], F32R, "a_lo")]
    junk = at("junk", [P, D], F32, "junk")
    ssq = at("ssq2", [P, TPH], F32, "ssq")
    var = at("var2", [P, TPH], F32, "var")
    inv = at("inv2", [P, TPH], F32, "inv")
    mhalf = at("mhalf2", [P, TPH], F32, "mhalf")
    ybank = psum[GU_BANKS:]

    loads = ([("gu", w, q) for q in range(4) for w in range(2)] + [("o", 0, q) for q in range(4)])
    NW = 4 * len(loads)
    RING = Counter(NW + KT, NBLK * (2 * NJ + KT))

    def ring_tile(hf, j, kind):
        base = hf * (2 * NJ + KT)
        if kind < 2:
            return base + 2 * j + kind + max(0, min(KT, j - PREP_J))
        return base + 2 * (PREP_J + kind - 2) + 2 + kind - 2

    with ExitStack() as ctx:
        def sem(name):
            return ctx.enter_context(nc.semaphore(name))

        held = sem("held2")
        raw_loaded = [sem("raw_loaded0"), sem("raw_loaded1")]
        x_loaded = sem("x_loaded2")
        attn_loaded = sem("attn_loaded")
        g_ready = sem("g_ready")
        g_act = sem("g_act")
        g_dve = sem("g_dve")
        out_mm = sem("out_mm")
        guh = sem("guh")
        gul = sem("gul")
        woh = sem("woh")
        wol = sem("wol")
        ah = sem("ah")
        al = sem("al")
        prod = sem("prod")
        summed = sem("summed")
        sq_sum = sem("sq_sum2")
        var_ready = sem("var_ready2")
        inv_ready = sem("inv_ready2")
        x_scaled = sem("x_scaled2")
        norm_now = sem("norm_now")
        full = sem("full")
        y_added = sem("y_added")
        y_stored = [sem("out_stored0"), sem("out_stored1")]
        block = ctx.enter_context(nc.Block())

        def nxt(b, hf):
            return (b, 1) if hf == 0 else (next_batch(b), 0)

        def blocks(b, hf, per, off=0):
            return b * (NBLK * per) + hf * per + off

        def weight_place(n):
            kind, w, q = loads[n // 4]
            c = n % 4
            if kind == "gu":
                return wT[:, w, c, q * QB:(q + 1) * QB]
            return woT[:, q * 4 + c, :]

        def act_ring(b, hf, j):
            return b * (NBLK * (NJ + KT)) + (NW // 2 + KT + hf * (NJ + KT) + j + max(0, min(KT, j - PREP_J)))

        def dve_ring(b, hf, j):
            return b * (NBLK * KT) + (NW // 2 + KT + hf * KT + max(0, min(KT, j - PREP_J)))

        def first_tiles_free(pe, b, n):
            j = NJ - 2 + n // 2
            if n % 2 == 0:
                pe.wait_ge(g_act, b * (NBLK * (NJ + KT)) + NW // 2 + KT - (NJ - 1 - j))
            else:
                pe.wait_ge(prod, b * (NBLK * NJ) + 1)

        @block.sync
        def _(sp):
            def load_tokens(b, hf, slot, prev):
                sp.dma_start(res[:, slot, :, :], x[b, hf * QB:(hf + 1) * QB, :].rearrange("(t p) d -> p t d", p=P)) \
                    .then_inc(x_loaded, 16)
                sp.dma_start(x1[:], attn[b, hf * QB:(hf + 1) * QB, :].rearrange("(t p) d -> p t d", p=P)) \
                    .then_inc(attn_loaded, 16)

            for s in y_stored:
                sp.sem_inc(s, 16)
            load_tokens(0, 0, 0, None)
            for n, (kind, w, q) in enumerate(loads):
                if n >= 2:
                    hold(sp, held, g_ready, 4 * (n - 1))
                if kind == "gu":
                    src = (gate_w, up_w)[w][q * QB:(q + 1) * QB, :].rearrange("(j p) d -> p j d", p=P)
                else:
                    src = out_w[:, q * QB:(q + 1) * QB].rearrange("(j p) d -> p j d", p=P)
                sp.dma_start(raw[n % 2], src).then_inc(raw_loaded[n % 2], 16)
            with sp.Fori(0, NB) as b:
                prepared = sp.snap(next_batch(b))
                for hf in range(NBLK):
                    slot = (hf + 1) % 2
                    hold(sp, held, y_stored[slot], b * (TPH * 16) + (TPH * 16 + 16 if slot == 0 else 16))
                    hold(sp, held, g_ready, RING(b, ring_tile(hf, 0, 0)))
                    nb, nh = (b, 1) if hf == 0 else (prepared, 0)
                    load_tokens(nb, nh, slot, b)
                    for t in range(TPH):
                        hold(sp, held, y_added, blocks(b, hf, TPH, t + 2))
                        row = hf * QB + t * P
                        sp.dma_start(out[b, row:row + P, :], res[:, hf, t, :]).then_inc(y_stored[hf], 16)
            for s in y_stored:
                hold(sp, held, s, NB * TPH * 16 + 16)
            hold(sp, held, x_loaded, 16 * (NB * NBLK + 1))
            hold(sp, held, attn_loaded, 16 * (NB * NBLK + 1))

        @block.gpsimd
        def _(pool):
            def prepare(x_val, n_sum, n_inv, slot):
                pool.wait_ge(x_loaded, x_val)
                pool.wait_ge(attn_loaded, x_val)
                nc.gpsimd.tensor_tensor(x1[:], x1[:], res[:, slot, :, :], ALU.add).then_inc(summed, 1)
                pool.wait_ge(summed, n_sum + 1)
                nc.gpsimd.tensor_tensor(res[:, slot, :, :], res[:, slot, :, :], x1[:], ALU.add).then_inc(summed, 1)
                pool.wait_ge(var_ready, n_inv + 1)
                nc.gpsimd.tensor_tensor(inv[:], var[:], mhalf[:], ALU.pow).then_inc(inv_ready, 1)

            prepare(16, 0, 0, 0)
            with pool.Fori(0, NB) as b:
                for hf in range(NBLK):
                    prepare(blocks(b, hf, 16, 32), blocks(b, hf, 2, 2), blocks(b, hf, 1, 1), (hf + 1) % 2)

        @block.scalar
        def _(act):
            def square(n, t):
                act.wait_ge(sq_sum, n + t)
                nc.scalar.activation(junk[:], x1[:, t, :], ACT.Square, accum_out=ssq[:, t:t + 1]).then_inc(sq_sum, 1)

            def norm_tile(n, k, slot, bank):
                act.wait_ge(g_ready, n + 1)
                nc.scalar.activation(hT[0][:, slot, k, :], psum[bank][:], ACT.Identity, bias=bias_now[:, k:k + 1],
                                     scale=gain_now[:, k:k + 1]).then_inc(g_act, 1)

            def gu_hi(j, slot):
                for w in range(2):
                    nc.scalar.activation(gu[0][:, slot, w, :, :], wT[:, w, :, j * P:(j + 1) * P], ACT.Copy).then_inc(guh, 1)

            for n in range(NW):
                if n % 2 == 0:
                    act.wait_ge(g_ready, n + 1)
                    nc.scalar.activation(weight_place(n), psum[n % GU_BANKS][:], ACT.Copy).then_inc(g_act, 1)
            act.wait_ge(summed, 1)
            for t in range(TPH):
                square(0, t)
            act.wait_ge(norm_now, 2)
            for k in range(KT):
                norm_tile(NW + k, k, 0, (NW + k) % GU_BANKS)
            act.wait_ge(g_act, NW // 2)
            act.wait_ge(g_dve, NW // 2)
            gu_hi(0, 0)
            with act.Fori(0, NB) as b:
                for hf in range(NBLK):
                    for j in range(NJ):
                        act.wait_ge(g_ready, RING(b, ring_tile(hf, j - 1, 1) + 1 if j else
                                                  (ring_tile(hf - 1, NJ - 1, 1) + 1 if hf else 0)))
                        gu_hi((j + 1) % NJ, (j + 1) % 2)
                        act.wait_ge(out_mm, blocks(b, hf, NJ, j - 1 + 2))
                        nc.scalar.activation(wo[0][:, j % 2, :], woT[:, j, :], ACT.Copy).then_inc(woh, 1)
                        n = ring_tile(hf, j, 0)
                        act.wait_ge(g_ready, RING(b, n + 1))
                        act.wait_ge(al, blocks(b, hf, NJ, j - 1 + 2))
                        nc.scalar.activation(sg[:, j % 2, :], psum[n % GU_BANKS][:], ACT.Silu).then_inc(g_act, 1)
                        act.wait_ge(prod, blocks(b, hf, NJ, j + 2))
                        nc.scalar.activation(a[0][:, j % 2, :], sg[:, j % 2, :], ACT.Copy).then_inc(ah, 1)
                        if 2 <= j < 2 + TPH:
                            if j == 2:
                                act.wait_ge(summed, blocks(b, hf, 2, 3))
                                act.wait_ge(var_ready, blocks(b, hf, 1, 1))
                            square(blocks(b, hf, TPH, TPH), j - 2)
                        if j == PREP_J:
                            act.wait_ge(norm_now, blocks(b, hf, 2, 4))
                        if PREP_J <= j < PREP_J + KT:
                            k = j - PREP_J
                            n = ring_tile(hf, j, 2 + k)
                            norm_tile(RING(b, n), k, (hf + 1) % 2, n % GU_BANKS)

        @block.vector
        def _(dve):
            dve.sem_inc(al, 2)
            dve.sem_inc(prod, 1)
            dve.sem_inc(y_added, 1)
            nc.vector.memset(mhalf[:], -0.5)
            for n in range(NW):
                if n % 2:
                    dve.wait_ge(g_ready, n + 1)
                    nc.vector.tensor_copy(weight_place(n), psum[n % GU_BANKS][:]).then_inc(g_dve, 1)

            def mean_square(n):
                dve.wait_ge(sq_sum, TPH * (n + 1))
                dve.wait_ge(inv_ready, n)
                nc.vector.tensor_scalar(var[:], ssq[:], 1.0 / D, EPS, ALU.mult, ALU.add).then_inc(var_ready, 1)
                return n

            def scale_x(n):
                dve.wait_ge(inv_ready, n + 1)
                dve.wait_ge(summed, 2 * (n + 1))
                for t in range(TPH):
                    nc.vector.tensor_scalar(x1[:, t, :], x1[:, t, :], inv[:, t:t + 1], None, ALU.mult).then_inc(x_scaled, 1)

            def set_norm(nb):
                nc.vector.tensor_copy(gain_now[:], gain[:, bass.ds(nb, 1), :].squeeze(1)).then_inc(norm_now, 1)
                nc.vector.tensor_copy(bias_now[:], bias[:, bass.ds(nb, 1), :].squeeze(1)).then_inc(norm_now, 1)

            def norm_tile(n, n_act, n_full, k, slot, bank):
                dve.wait_ge(g_ready, n + 1)
                dve.wait_ge(g_act, n_act + 1)
                nc.vector.tensor_scalar(hT_full[:, slot, k, :], psum[bank][:], gain_now[:, k:k + 1],
                                        bias_now[:, k:k + 1], ALU.mult, ALU.add).then_inc(full, 1)
                dve.wait_ge(full, n_full + 1)
                nc.vector.tensor_tensor(hT[1][:, slot, k, :], hT_full[:, slot, k, :],
                                        hT[0][:, slot, k, :].bitcast(F32), ALU.subtract).then_inc(g_dve, 1)

            def gu_lo(n, j, slot):
                for w in range(2):
                    dve.wait_ge(guh, n + w + 1)
                    nc.vector.tensor_tensor(gu[1][:, slot, w, :, :], wT[:, w, :, j * P:(j + 1) * P],
                                            gu[0][:, slot, w, :, :].bitcast(F32), ALU.subtract).then_inc(gul, 1)

            mean_square(0)
            scale_x(0)
            set_norm(0)
            dve.wait_ge(norm_now, 2)
            for k in range(KT):
                norm_tile(NW + k, NW // 2 + k, k, k, 0, (NW + k) % GU_BANKS)
            dve.wait_ge(g_act, NW // 2)
            dve.wait_ge(g_dve, NW // 2 + KT)
            gu_lo(0, 0, 0)
            with dve.Fori(0, NB) as b:
                for hf in range(NBLK):
                    for j in range(NJ):
                        gu_lo(blocks(b, hf, 2 * NJ, 2 * (j + 1)), (j + 1) % NJ, (j + 1) % 2)
                        dve.wait_ge(woh, blocks(b, hf, NJ, j + 1))
                        nc.vector.tensor_tensor(wo[1][:, j % 2, :], woT[:, j, :], wo[0][:, j % 2, :].bitcast(F32),
                                                ALU.subtract).then_inc(wol, 1)
                        n = ring_tile(hf, j, 1)
                        dve.wait_ge(g_ready, RING(b, n + 1))
                        dve.wait_ge(g_act, act_ring(b, hf, j) + 1)
                        nc.vector.tensor_tensor(sg[:, j % 2, :], psum[n % GU_BANKS][:], sg[:, j % 2, :],
                                                ALU.mult).then_inc(prod, 1)
                        dve.wait_ge(ah, blocks(b, hf, NJ, j + 1))
                        dve.wait_ge(prod, blocks(b, hf, NJ, j + 2))
                        nc.vector.tensor_tensor(a[1][:, j % 2, :], sg[:, j % 2, :], a[0][:, j % 2, :].bitcast(F32),
                                                ALU.subtract).then_inc(al, 1)
                        if j == 6:
                            mean_square(blocks(b, hf, 1, 1))
                        if j == 7:
                            set_norm(nxt(b, hf)[0])
                            scale_x(blocks(b, hf, 1, 1))
                            dve.wait_ge(norm_now, blocks(b, hf, 2, 4))
                        if PREP_J <= j < PREP_J + KT:
                            k = j - PREP_J
                            n = ring_tile(hf, j, 2 + k)
                            norm_tile(RING(b, n), act_ring(b, hf, j) + 1, blocks(b, hf, KT, KT + k), k,
                                      (hf + 1) % 2, n % GU_BANKS)
                    dve.wait_ge(out_mm, blocks(b, hf, NJ, NJ + 2))
                    for t in range(TPH):
                        nc.vector.tensor_tensor(res[:, hf, t, :], ybank[t][:], res[:, hf, t, :],
                                                ALU.add).then_inc(y_added, 1)

        @block.tensor
        def _(pe):
            pe.sem_inc(out_mm, 2)

            def bank_free(b, hf, n_in):
                kinds = []
                for h in range(NBLK):
                    for j in range(NJ):
                        kinds += [("g", h, j), ("u", h, j)] + ([("t", h, j)] if PREP_J <= j < PREP_J + KT else [])
                m = n_in - GU_BANKS
                if m >= 0:
                    kind, h, j = kinds[m]
                    bb = b
                else:
                    kind, h, j = kinds[m]
                    bb = b - 1
                if kind == "g":
                    pe.wait_ge(g_act, act_ring(bb, h, j) + 1)
                elif kind == "u":
                    pe.wait_ge(prod, blocks(bb, h, NJ, j + 2))
                else:
                    pe.wait_ge(g_act, act_ring(bb, h, j) + 2)
                    pe.wait_ge(g_dve, dve_ring(bb, h, j) + 1)

            for n in range(NW):
                if n >= GU_BANKS:
                    m = n - GU_BANKS
                    pe.wait_ge(g_dve if m % 2 else g_act, m // 2 + 1)
                if n % 4 == 0:
                    pe.wait_ge(raw_loaded[n // 4 % 2], n // 8 * 16 + 16)
                for j in range(4):
                    last = nc.tensor.transpose(psum[n % GU_BANKS][:, j * P:(j + 1) * P],
                                               raw[n // 4 % 2][:, j, n % 4 * P:(n % 4 + 1) * P], ident[:])
                last.then_inc(g_ready, 1)

            def transposes(k, bank):
                for t in range(TPH):
                    last = nc.tensor.transpose(psum[bank][:, t * P:(t + 1) * P], x1[:, t, k * P:(k + 1) * P], ident[:])
                last.then_inc(g_ready, 1)

            pe.wait_ge(g_act, NW // 2)
            pe.wait_ge(g_dve, NW // 2)
            pe.wait_ge(x_scaled, TPH)
            for k in range(KT):
                transposes(k, (NW + k) % GU_BANKS)
            pe.wait_ge(g_act, NW // 2 + KT)
            pe.wait_ge(g_dve, NW // 2 + KT)

            def out_product(b, hf, j):
                for s in (ah, wol):
                    pe.wait_ge(s, blocks(b, hf, NJ, j + 1))
                pe.wait_ge(al, blocks(b, hf, NJ, j + 3))
                if j == 0:
                    pe.wait_ge(y_added, blocks(b, hf, TPH, 1))
                for t in range(TPH):
                    for p, q in ((0, 0), (0, 1), (1, 0)):
                        last = nc.tensor.matmul(ybank[t][:], a[p][:, j % 2, t * P:(t + 1) * P], wo[q][:, j % 2, :],
                                                start=(j == 0 and p == 0 and q == 0),
                                                stop=(j == NJ - 1 and p == 1))
                last.then_inc(out_mm, 1)

            with pe.Fori(0, NB) as b:
                for hf in range(NBLK):
                    for j in range(NJ):
                        pe.wait_ge(gul, blocks(b, hf, 2 * NJ, 2 * (j + 1)))
                        for w in range(2):
                            n = ring_tile(hf, j, w)
                            if n >= GU_BANKS:
                                bank_free(b, hf, n)
                            else:
                                first_tiles_free(pe, b, n)
                            steps = [(k, p, q) for k in range(KT) for p, q in ((0, 0), (0, 1), (1, 0))]
                            for i, (k, p, q) in enumerate(steps):
                                last = nc.tensor.matmul(psum[n % GU_BANKS][:], gu[p][:, j % 2, w, k, :],
                                                        hT[q][:, hf, k, :], start=(i == 0), stop=(i == len(steps) - 1))
                            last.then_inc(g_ready, 1)
                        if PREP_J <= j < PREP_J + KT:
                            k = j - PREP_J
                            n = ring_tile(hf, j, 2 + k)
                            bank_free(b, hf, n)
                            if k == 0:
                                pe.wait_ge(x_scaled, blocks(b, hf, TPH, 2 * TPH))
                            transposes(k, n % GU_BANKS)
                        if j:
                            out_product(b, hf, j - 1)
                    out_product(b, hf, NJ - 1)



def condition_block(nc, x, t, wq, wk, wv, wo, cond, gate_w, up_w, out_w, out):
    attn = nc.dram_tensor("attn_out", (NB, L, D), F32, kind="Internal").ap()
    wv_dram = nc.dram_tensor("wv_parts", (P, 2, KT, D), F32, kind="Internal").ap()
    base = (nc.sbuf_base + 31) // 32 * 32
    sizes = {F32: 4, F32R: 4}

    def plan(start, regions):
        places = {}
        for name, words in regions:
            places[name] = start
            start += (4 * words + 31) // 32 * 32
        return places, start

    small = [("ident", P), ("identr", P), ("ones", DH)] + [(f"cond{m}", NB * KT) for m in range(4)] \
        + [("gain_now", KT), ("bias_now", KT), ("ssq", TPH), ("var", TPH), ("inv", TPH), ("mhalf", TPH)]
    const_at, base = plan(base, small)
    weights_at, after_weights = plan(base, [(f"{n}_{p}", KT * D) for n in ("wq", "wk", "wo") for p in ("hi", "lo")])
    setup_at, _ = plan(after_weights, [("setup_raw", 4 * KT * D), ("setup_wv", 2 * KT * D), ("setup_t", DT),
                                       ("setup_tT", NB), ("setup_gw", 4 * KT * DT), ("setup_gwT", 4 * D),
                                       ("setup_gb", 4 * KT)])
    attention_at, _ = plan(after_weights, [
        ("hT_hi", KT * L), ("hT_lo", KT * L), ("qk_hi", 2 * QB), ("qk_lo", 2 * QB), ("qs", 2 * GH * QB),
        ("ks", 2 * GH * L), ("v", NS * D), ("probs", 2 * GH * QB), ("sums", POOL_HEADS * QB), ("mt", TPH * P),
        ("o", NG * L), ("den", QB), ("x4", TPH * D), ("yout", 2 * D), ("pmax", TPH * GH * NHALF),
        ("mx", TPH * GH), ("dsmall", QB // 32), ("zero", 1), ("indc", GH)])
    ffn_at, _ = plan(base, [
        ("wT", 2 * KT * HID), ("woT", NJ * D), ("gu_hi", 4 * KT * P), ("gu_lo", 4 * KT * P), ("wo_hi2", 2 * D),
        ("wo_lo2", 2 * D), ("h2_hi", 2 * KT * QB), ("h2_lo", 2 * KT * QB), ("x1", TPH * D), ("res", 2 * TPH * D),
        ("sg", 2 * QB), ("a_hi", 2 * QB), ("a_lo", 2 * QB), ("junk", D)])
    places = {**const_at, **weights_at, **setup_at, **attention_at, **ffn_at}

    def at(name, shape, dtype, region):
        return nc.alloc_sbuf_tensor_at(name, shape, dtype, offset=places[region])

    cst = {"at": at, "ident": at("ident", [P, P], F32, "ident"), "identr": at("identr", [P, P], F32R, "identr"),
           "ones": at("ones", [P, DH], F32, "ones"), "gain_now": at("gain_now", [P, KT], F32, "gain_now"),
           "bias_now": at("bias_now", [P, KT], F32, "bias_now"),
           "cond": [at(f"cond{m}", [P, NB, KT], F32, f"cond{m}") for m in range(4)]}
    cst["g1"], cst["b1"], cst["g2"], cst["b2"] = cst["cond"]
    W = [[at(f"{n}_{p}", [P, KT, D], F32R, f"{n}_{p}") for p in ("hi", "lo")] for n in ("wq", "wk", "wo")]
    with ExitStack() as ctx:
        psum = [ctx.enter_context(nc.psum_tensor(f"bank{i}", [P, QB], F32)) for i in range(8)]
        attention_setup(nc, t, [wq, wk, wv, wo], cond, wv_dram, W, cst, psum)
        attention_program(nc, x, attn, wv_dram, W, cst, psum)
        ffn_program(nc, x, attn, gate_w, up_w, out_w, out, cst, psum)


_INS = ["x", "cond_256"] + ["L0_cond_" + n for n in ("Wq", "Wk", "Wv", "Wo", "g1w", "g1b", "b1w", "b1b", "g2w", "g2b",
                                                     "b2w", "b2b", "gate_w", "hid_w", "out_w")]


def kernel(**inputs):
    import concourse.bacc as bacc
    from concourse.bass_utils import run_bass_kernel_spmd

    nc = bacc.Bacc("TRN2", target_bir_lowering=False, num_devices=1)
    arrays, ap = {}, {}
    for name in _INS:
        a = np.ascontiguousarray(inputs[name])
        arrays[f"in_{name}"] = a
        ap[name.replace("L0_cond_", "")] = nc.dram_tensor(f"in_{name}", a.shape, mybir.dt.from_np(a.dtype),
                                                          kind="ExternalInput").ap()
    out = nc.dram_tensor("out_0", (NB, L, D), F32, kind="ExternalOutput").ap()
    cond = [(ap[f"{n}w"], ap[f"{n}b"]) for n in ("g1", "b1", "g2", "b2")]
    condition_block(nc, ap["x"], ap["cond_256"], ap["Wq"], ap["Wk"], ap["Wv"], ap["Wo"], cond,
                    ap["gate_w"], ap["hid_w"], ap["out_w"], out)
    r = run_bass_kernel_spmd(nc, [arrays], core_ids=[0])
    return r.results[0]["out_0"]
```

```python
import numpy as np
import concourse.bass as bass
from concourse import mybir
from contextlib import ExitStack

F32 = mybir.dt.float32
F32R = mybir.dt.float32r
ALU = mybir.AluOpType
ACT = mybir.ActivationFunctionType
AX_X = mybir.AxisListType.X

P = 128
NB, L, D = 4, 1024, 512
H, DH = 16, 32
HID = 2048
DT = 128
EPS = 1e-6
KT = D // P
GH = P // DH
NG = H // GH
QB = 512
NHALF = L // QB
NU = NG * NHALF
NS = L // P
NT = L // P
TPH = QB // P
POOL_HEADS = 3
LEAD_BANKS = 4
IN_V = {1: ("Q", 1), NT - 3: ("K", 2, 0), NT - 2: ("mT", 0)}
UNIT = NS * GH
PROJECTED = {("K", 2, 1): (0, 1), ("Q", 2): (9, 2)}
for odd in (1, 3):
    PROJECTED.update({("Q", odd + 2): (odd * UNIT, 2), ("K", odd + 3, 0): (odd * UNIT + 18, 2),
                      ("K", odd + 3, 1): ((odd + 1) * UNIT, 1), ("Q", odd + 3): ((odd + 1) * UNIT + 9, 2)})
PROJECTED.update({("Q", NU - 1): (5 * UNIT, 2), ("Q", NU): (6 * UNIT, 2), ("K", NU, 0): (7 * UNIT + 16, 2),
                  ("K", NU, 1): (7 * UNIT + 24, 2)})
HT_AT = {5: (10, 14, 18, 22), 7: (0, 4, 8, 12)}
MAXIMA_AT = (6, 3)
SB, MB = 2, 3
NMAX = GH * TPH * NHALF
V_ALONE = (2 * KT, 6)
MAX_END = 25


def spread(count, quarters):
    return [(q + 1) * count // quarters - q * count // quarters for q in range(quarters)]


MAX_IN_V = [0] * V_ALONE[0] + spread(NMAX, NT * KT - sum(V_ALONE)) + [0] * V_ALONE[1]
MAX_AT = spread(NMAX, MAX_END) + [1] * ((NU - 2) * NMAX) + [0] * (NU * NS * GH - MAX_END - (NU - 2) * NMAX)
assert sum(MAX_IN_V) == NMAX and sum(MAX_AT) == (NU - 1) * NMAX and KT == GH and NMAX == NS * GH
SCALE = 1.0 / float(np.sqrt(np.float32(DH)))



class Counter:

    def __init__(self, lead, per):
        self.lead, self.per = lead, per

    def __call__(self, b, n):
        if b is None:
            return n
        return b * self.per + (self.lead + n)


def misc_order(body):
    if not body:
        return ([("hT", k, 0) for k in range(KT)] + [("hT", 0, 1), ("hT", 1, 1), ("Q", 0)]
                + [("hT", k, 1) for k in range(2, KT)] + [("K", 0, hf) for hf in range(NHALF)])
    return list(IN_V.values()) + [tile for u in range(NU) for s in range(NS) for h in range(GH)
                                    for tile in done_at(u, s, h)]


def part_at(u, s, h):
    q = (u * NS + s) * GH + h
    return next(((tile, (q - at) // gap) for tile, (at, gap) in PROJECTED.items()
                 if q - at in range(0, gap * KT, gap)), None)


def made_at(u, s, h):
    q = s * GH + h
    if u in HT_AT and q in HT_AT[u]:
        return ("hT", HT_AT[u].index(q), list(HT_AT).index(u))
    return ("mT", u + 1) if (s, h) == MAXIMA_AT and u < NU - 1 else None


def next_maxima(u, s, h):
    q = (u * NS + s) * GH + h
    return range(sum(MAX_AT[:q]), sum(MAX_AT[:q + 1]))


def done_at(u, s, h):
    tile, part = part_at(u, s, h) or (None, 0)
    return [m for m in (made_at(u, s, h), tile if part == KT - 1 else None) if m]


LEAD_MISC = misc_order(False)
BODY_MISC = misc_order(True)
MISC = Counter(len(LEAD_MISC), len(BODY_MISC))
LEAD_DVE = [m for m in LEAD_MISC if m[0] != "mT"]
BODY_DVE = [m for m in BODY_MISC if m[0] != "mT"]
MISC_DVE = Counter(len(LEAD_DVE), len(BODY_DVE))
ST_LEAD = NMAX - NT
SCORES_T = Counter(ST_LEAD, NT + NU * NS * GH)
SCORES_Q = Counter(0, NU * NMAX + NT)
SUMS = (NS - 2) * POOL_HEADS
LINKS_PER_BATCH = NU * (2 + 3)
HEAD_INC = 3 * 16


def misc_index(body, tile):
    return (BODY_MISC if body else LEAD_MISC).index(tile)


def slot_users(tile):
    order = [m for m in LEAD_MISC + BODY_MISC if m[0] in "KQ"]
    before = order[:order.index(tile)]
    last = max(i for i, m in enumerate(before) if qk_slot(m) == qk_slot(tile))
    kind = [m for m in before[:last + 1] if m[0] == before[last][0] and qk_slot(m) == qk_slot(tile)]
    return before[last][0], len(kind)


def qk_slot(tile):
    return tile[2] if tile[0] == "K" else 0


def sums_done(b, u, s, h):
    return b * (NU * SUMS) + (SUMS * (u + 1) + POOL_HEADS * max(s - 1, 0) + h + 1)


def dve_before(body, tile):
    order = BODY_MISC if body else LEAD_MISC
    return sum(m[0] != "mT" for m in order[:order.index(tile)])


def hold(sp, held, semaphore, value):
    sp.wait_ge(semaphore, value)
    sp.sem_inc(held, 1)


def next_batch(b):
    return (b + 1) % NB


def attention_program(nc, x, attn, wv_dram, wo_dram, W, ffn_loads, cst, psum):
    wq, wk, wo_lo = W
    at = cst["at"]
    ident, identr, ones, gain, bias = cst["ident"], cst["identr"], cst["ones"], cst["g1"], cst["b1"]

    hT = [at("hT_hi", [P, KT, L], F32R, "hT_hi"), at("hT_lo", [P, KT, L], F32R, "hT_lo")]
    hT_full = at("hT_full", [P, KT, L], F32, "hT_lo")
    qk = [at("qk_hi", [P, 2, QB], F32R, "qk_hi"), at("qk_lo", [P, 2, QB], F32R, "qk_lo")]
    qs = at("qs", [P, 3, GH, QB], F32R, "qs")
    ks = at("ks", [P, 2, GH, L], F32R, "ks")
    v = at("v", [P, NS, D], F32, "v")
    probs = at("probs", [P, 2, GH, QB], F32, "probs")
    wo = [cst["wo_hi"], wo_lo]
    wv = cst["wv"]
    sums = at("sums", [P, POOL_HEADS, QB], F32, "sums")
    mt = at("mt", [P, TPH, P], F32R, "mt")
    o = at("o", [P, NG, L], F32, "o")
    den = at("den", [P, QB], F32, "den")
    x_half = cst["x_first"]
    x4 = x_half[0]
    osplit = at("osplit", [P, 2, 2, NG, P], F32R, "x4")
    yout = at("yout", [P, 2, D], F32, "yout")
    pmax = at("pmax", [P, TPH, GH, NHALF], F32, "pmax")
    mx = at("mx", [P, TPH, GH], F32, "mx")
    ssq = at("ssq", [P, TPH], F32, "ssq")
    var = at("var", [P, TPH], F32, "var")
    inv = at("inv", [P, TPH], F32, "inv")
    mhalf = at("mhalf", [P, TPH], F32, "mhalf")
    dsmall = at("dsmall", [P, QB // 32], F32, "dsmall")
    indc = at("indc", [P, GH], F32, "indc")

    sbank = psum[0:SB]
    mbank = psum[SB:SB + MB]
    obank, dbank, wbank = psum[5], psum[6], psum[7]

    with ExitStack() as ctx:
        def sem(name):
            return ctx.enter_context(nc.semaphore(name))

        held = sem("held")
        x_loaded = sem("x_loaded")
        wv_loaded = sem("wv_loaded")
        wo_loaded = sem("wo_loaded")
        st_ready = sem("st_ready")
        st_done = sem("st_done")
        sq_ready = sem("sq_ready")
        sq_done = sem("sq_done")
        w_ready = sem("w_ready")
        w_act = sem("w_act")
        w_dve = sem("w_dve")
        full = sem("h_full")
        q_stacked = [sem(f"q_stacked{h}") for h in range(GH)]
        k_stacked = [sem(f"k_stacked{h}") for h in range(GH)]
        m_rows = sem("m_rows")
        pv_done = sem("pv_done")
        sum_done = sem("sum_done")
        mt_ready = sem("mt_ready")
        od_act = sem("od_act")
        d_ready = sem("d_ready")
        on_done = sem("on_done")
        os_act = sem("os_act")
        os_dve = sem("os_dve")
        y_stored = [sem("y_stored0"), sem("y_stored1")]
        sq_sum = sem("sq_sum")
        var_ready = sem("var_ready")
        inv_ready = sem("inv_ready")
        x_scaled = sem("x_scaled")
        early_loaded = sem("early_loaded")
        const_pool = sem("const_pool")
        const_dve = sem("const_dve")
        dve_step = sem("dve_step")
        block = ctx.enter_context(nc.Block())

        def lead_bank(i):
            return (wbank, obank, dbank, mbank[0])[i % LEAD_BANKS]

        def x_tokens(b, hf):
            return x_half[hf if b is None else 0]

        @block.sync
        def _(sp):
            def load_x(b, hf, src_b):
                hold(sp, held, *((w_ready, MISC(b, misc_index(True, ("hT", KT - 1, 0)) + 1)) if hf
                                 else (sq_ready, SCORES_Q(b, NMAX))))
                sp.dma_start(x4[:], x[src_b, hf * QB:(hf + 1) * QB, :].rearrange("(t p) d -> p t d", p=P)) \
                    .then_inc(x_loaded, 16)

            def stack(b, tile, slot):
                hold(sp, held, w_dve, MISC_DVE(b, dve_before(b is not None, tile) + 1))
                queries = tile[0] == "Q"
                for h in range(GH):
                    for to, part in enumerate((0, 1, 0) if queries else (0, 0, 1)):
                        rows, to = slice(DH * h, DH * h + DH), slice(DH * to, DH * to + DH)
                        if queries:
                            sp.dma_start(qs[to, slot, h, :].bitcast(F32), qk[part][rows, 0, :].bitcast(F32)) \
                                .then_inc(q_stacked[h], 16)
                        else:
                            sp.dma_start(ks[to, slot, h, :].bitcast(F32),
                                         qk[part][rows, :, :].rearrange("p a c -> p (a c)").bitcast(F32)) \
                                .then_inc(k_stacked[h], 16)

            def load_wv():
                sp.dma_start(wv[:].bitcast(F32), wv_dram).then_inc(wv_loaded, 16)

            for s in y_stored:
                sp.sem_inc(s, 16)
            hold(sp, held, cst["wv_stored"], 16)
            hold(sp, held, cst["wo_stored"], 16)
            sp.sem_inc(wv_loaded, 16)
            stack(None, ("Q", 0), 0)
            stack(None, ("K", 0, NHALF - 1), 0)
            with sp.Fori(0, NB) as b:
                prepared = sp.snap(next_batch(b))
                stack(b, ("Q", 1), 1)
                for u in range(NU):
                    if u % 2 == 0 and u < NU - 2:
                        stack(b, ("K", u + 2, NHALF - 1), (u // 2 + 1) % 2)
                    if u == NU - 2:
                        hold(sp, held, st_ready, SCORES_T(b, NT + u * NS * GH))
                        sp.dma_start(wo[0][:].bitcast(F32), wo_dram).then_inc(wo_loaded, 16)
                    elif u == NU - 1:
                        hold(sp, held, st_ready, SCORES_T(b, NT + u * NS * GH))
                        stack(b, ("Q", NU), 0)
                        stack(b, ("K", NU, NHALF - 1), 0)
                    else:
                        stack(b, ("Q", u + 2), (u + 2) % 3)
                    if u == 3:
                        load_x(b, 0, prepared)
                    if u == 5:
                        load_x(b, 1, prepared)
                hold(sp, held, pv_done, b * (NU * NS) + NU * NS + 2)
                hold(sp, held, sum_done, sums_done(b, NU - 1, NS - 2, POOL_HEADS - 1))
                load_wv()
                for t in range(NT):
                    hold(sp, held, sq_done, SCORES_Q(b, NU * NMAX + t + 1) + MB)
                    sp.dma_start(attn[b, t * P:(t + 1) * P, :], yout[:, t % 2, :]).then_inc(y_stored[t % 2], 16)
            for s in y_stored:
                hold(sp, held, s, (NB * (NT // 2) + 1) * 16)
            hold(sp, held, wv_loaded, (NB + 1) * 16)

        @block.gpsimd
        def _(pool):
            nc.gpsimd.memset(mhalf[:], -0.5).then_inc(const_pool, 1)
            pool.sem_inc(sum_done, SUMS)
            pool.wait_ge(const_pool, 1)

            def inverse_root(b, n):
                pool.wait_ge(var_ready, n + 1)
                nc.gpsimd.tensor_tensor(inv[:], var[:], mhalf[:], ALU.pow).then_inc(inv_ready, 1)

            inverse_root(None, 0)
            inverse_root(None, 1)
            with pool.Fori(0, NB) as b:
                for u in range(NU):
                    for s in range(NS):
                        n = u * NS + s
                        if (u, s) == (4, 5):
                            inverse_root(b, b * 2 + 2)
                        if (u, s) == (6, 6):
                            inverse_root(b, b * 2 + 3)
                        for h in range(POOL_HEADS if 0 < s < NS - 1 else 0):
                            pool.wait_ge(st_done, SCORES_T(b, NT + n * GH + h + 1) + SB)
                            if s == 1 and h == 0:
                                pool.wait_ge(d_ready, b * NU + (u + 1))
                            if s > 1:
                                pool.wait_ge(sum_done, sums_done(b, u, s - 1, h))
                            before = sums[:, h, :] if s > 1 else probs[:, 0, h, :]
                            nc.gpsimd.tensor_tensor(sums[:, h, :], probs[:, s % 2, h, :], before, ALU.add) \
                                .then_inc(sum_done, 1)

            pool.wait_ge(st_ready, ST_LEAD + NB * (NT + NU * NS * GH))
            pool.wait_ge(pv_done, NB * NU * NS + 2)
            for n, (place, src) in enumerate(ffn_loads):
                pool.wait_ge(sq_ready, NB * (NU * NMAX + NT) - NT + 2 * n + 1)
                pool.dma_start(place, src).then_inc(early_loaded, 16)
            pool.wait_ge(early_loaded, len(ffn_loads) * 16)

        @block.scalar
        def _(act):
            act.sem_inc(st_done, ST_LEAD + SB)
            act.sem_inc(od_act, 2)

            def square(b, hf, t):
                n = (0 if b is None else b * 8 + 8) + (4 * hf + t)
                if t == 0:
                    if b is None:
                        act.wait_ge(cst["x_first_loaded"][hf], 16)
                    else:
                        act.wait_ge(x_loaded, b * 32 + 16 * (hf + 1))
                    if b is not None and hf == 0:
                        for s in y_stored:
                            act.wait_ge(s, b * (NT // 2 * 16) + 16)
                    if b is not None or hf:
                        act.wait_ge(var_ready, hf if b is None else b * 2 + 2 + hf)
                if b is not None or n:
                    act.wait_ge(sq_sum, n)
                nc.scalar.activation(yout[:, 0, :], x_tokens(b, hf)[:, t, :], ACT.Square,
                                     accum_out=ssq[:, t:t + 1]).then_inc(sq_sum, 1)

            def maxima_rows(u, pair):
                nc.scalar.activation(qs[96:128, u % 3, 2 * pair:2 * pair + 2, :],
                                     wbank[96:128, :].unsqueeze(1).to_broadcast([32, 2, QB]),
                                     ACT.Copy).then_inc((m_rows, w_act)[pair], 1)

            def work_tile(b, tile):
                body = b is not None
                i = misc_index(body, tile)
                act.wait_ge(w_ready, MISC(b, i + 1))
                bank = wbank if body else lead_bank(i)
                if tile[0] == "hT":
                    _, k, hf = tile
                    cols = slice(hf * QB, (hf + 1) * QB)
                    nc.scalar.activation(hT_full[:, k, cols], bank[:], ACT.Identity, bias=cur_bias[:, k:k + 1],
                                         scale=cur_gain[:, k:k + 1]).then_inc(full, 1)
                    n = hf * KT + k + 1
                    act.wait_ge(full, n if b is None else b * (NHALF * KT) + (NHALF * KT + n))
                    nc.scalar.activation(hT[0][:, k, cols], hT_full[:, k, cols], ACT.Copy).then_inc(w_act, 1)
                elif tile[0] == "mT":
                    maxima_rows(tile[1], 0)
                else:
                    if body or tile == ("K", 0, 0):
                        kind, n = slot_users(tile)
                        for s in q_stacked if kind == "Q" else k_stacked:
                            if body:
                                act.wait_ge(s, b * ((NU if kind == "Q" else NG) * HEAD_INC) + n * HEAD_INC)
                            else:
                                act.wait_ge(s, n * HEAD_INC)
                    nc.scalar.activation(qk[0][:, qk_slot(tile), :], bank[:], ACT.Copy).then_inc(w_act, 1)

            cur_gain, cur_bias = cst["gain_now"], cst["bias_now"]

            def output(b, u):
                act.wait_ge(pv_done, b * (NU * NS) + (u + 1) * NS + 2)
                if u == 0:
                    act.wait_ge(sq_ready, SCORES_Q(b, NMAX))
                g, hf = u // 2, u % 2
                nc.scalar.activation(o[:, g, hf * QB:(hf + 1) * QB], obank[:], ACT.Copy).then_inc(od_act, 1)
                act.wait_ge(on_done, b * NU + (u + 1))
                nc.scalar.activation(den[96:128, :], dbank[96:128, :], ACT.Copy).then_inc(od_act, 1)

            def denominators(b, u):
                act.wait_ge(d_ready, b * NU + (u + 2))
                nc.scalar.activation(den[0:96, :], dbank[0:96, :], ACT.Copy).then_inc(od_act, 1)

            def output_hi(b, t):
                act.wait_ge(on_done, b * NU + (NU if t < TPH else NU + 1))
                if t >= 2:
                    act.wait_ge(sq_ready, SCORES_Q(b, NU * NMAX + t - 1))
                nc.scalar.activation(osplit[:, t % 2, 0, :, :], o[:, :, t * P:(t + 1) * P],
                                     ACT.Copy).then_inc(os_act, 1)

            for t in range(TPH):
                square(None, 0, t)
            act.wait_ge(const_dve, 2)
            for t in range(TPH):
                square(None, 1, t)
            for tile in LEAD_MISC:
                work_tile(None, tile)
            act.wait_ge(cst["wv_stored"], 16)
            act.wait_ge(cst["wo_stored"], 16)
            with act.Fori(0, NB) as b:
                for t in range(NT):
                    act.wait_ge(st_ready, SCORES_T(b, t + 1))
                    if t == 0:
                        act.wait_ge(pv_done, b * (NU * NS) + 2)
                    nc.scalar.activation(v[:, t, :], sbank[t % SB][:], ACT.Copy).then_inc(st_done, 1)
                    if t in IN_V:
                        work_tile(b, IN_V[t])
                        if IN_V[t][0] == "mT":
                            maxima_rows(0, 1)
                for u in range(NU):
                    for s in range(NS):
                        n = u * NS + s
                        act.wait_ge(pv_done, b * (NU * NS) + n + 1)
                        if u == 5 and s == 0:
                            act.wait_ge(const_dve, b * 2 + 4)
                        for h in range(GH):
                            i = NT + n * GH + h
                            act.wait_ge(st_ready, SCORES_T(b, i + 1))
                            if h < POOL_HEADS and s != 1:
                                act.wait_ge(sum_done, sums_done(b, u, s - 2, h) if s >= 2
                                            else sums_done(b, u - 1, NS - 2, h))
                            nc.scalar.activation(probs[:, s % 2, h, :], sbank[i % SB][:], ACT.Exp,
                                                 scale=SCALE).then_inc(st_done, 1)
                            if (u, s) == (4, 4):
                                square(b, 0, h)
                            if (u, s) == (6, 3):
                                square(b, 1, h)
                            for tile in done_at(u, s, h):
                                work_tile(b, tile)
                            if (s, h) == (NS - 1, 0) and u < NU - 1:
                                maxima_rows(u + 1, 1)
                            if (s, h) == (1, 2) and u:
                                denominators(b, u - 1)
                        if s == 0 and u:
                            output(b, u - 1)
                        if u == NU - 1 and s >= NS - 2:
                            output_hi(b, s - (NS - 2))
                output(b, NU - 1)
                denominators(b, NU - 1)
                for t in range(2, NT):
                    output_hi(b, t)

        @block.vector
        def _(dve):
            class Link:
                lead = 0
                n = 0
                b = None

            def link(ins):
                ins.then_inc(dve_step, 1)
                Link.n += 1
                dve.wait_ge(dve_step, Link.n if Link.b is None else Link.b * LINKS_PER_BATCH + (Link.lead + Link.n))

            dve.sem_inc(sq_done, MB)
            dve.sem_inc(on_done, 1)
            dve.sem_inc(mt_ready, 1)
            cur_gain, cur_bias = cst["gain_now"], cst["bias_now"]
            nc.vector.tensor_copy(cur_gain[:], gain[:, 0, :]).then_inc(const_dve, 1)
            nc.vector.tensor_copy(cur_bias[:], bias[:, 0, :]).then_inc(const_dve, 1)
            dve.wait_ge(const_dve, 2)

            def mean_square(b, hf):
                n = hf if b is None else b * 2 + 2 + hf
                dve.wait_ge(sq_sum, 4 * (n + 1))
                dve.wait_ge(inv_ready, n)
                nc.vector.tensor_scalar(var[:], ssq[:], 1.0 / D, EPS, ALU.mult, ALU.add).then_inc(var_ready, 1)

            def scale_x(b, hf, t):
                n = hf if b is None else b * 2 + 2 + hf
                dve.wait_ge(inv_ready, n + 1)
                tokens = x_tokens(b, hf)[:, t, :]
                nc.vector.tensor_scalar(tokens, tokens, inv[:, t:t + 1], None, ALU.mult).then_inc(x_scaled, 1)

            def work_tile(b, tile):
                body = b is not None
                dve.wait_ge(w_ready, MISC(b, misc_index(body, tile) + 1))
                dve.wait_ge(w_act, MISC(b, misc_index(body, tile) + 1))
                bank = wbank if body else lead_bank(misc_index(body, tile))
                if tile[0] == "hT":
                    _, k, hf = tile
                    cols = slice(hf * QB, (hf + 1) * QB)
                    nc.vector.tensor_tensor(hT[1][:, k, cols], hT_full[:, k, cols],
                                            hT[0][:, k, cols].bitcast(F32), ALU.subtract).then_inc(w_dve, 1)
                else:
                    slot = qk_slot(tile)
                    nc.vector.tensor_tensor(qk[1][:, slot, :], bank[:], qk[0][:, slot, :].bitcast(F32),
                                            ALU.subtract).then_inc(w_dve, 1)

            def max_tile(b, n):
                i = n % NMAX
                h, t, hf = i // (TPH * NHALF), i // NHALF % TPH, i % NHALF
                dve.wait_ge(sq_ready, SCORES_Q(b, n + 1))
                nc.vector.reduce_max(pmax[:, t, h, hf:hf + 1], mbank[n % MB][:], AX_X).then_inc(sq_done, 1)
                if i == NMAX - 1:
                    maxima(b, n // NMAX)

            def maxima(b, u):
                dve.wait_ge(sq_done, SCORES_Q(b, (u + 1) * NMAX) + MB)
                dve.wait_ge(mt_ready, b * NU + (u + 1))
                link(nc.vector.tensor_tensor(mx[:], pmax[:, :, :, 0], pmax[:, :, :, 1], ALU.max))
                dve.wait_ge(w_ready, MISC(b, misc_index(True, ("mT", u - 1)) + 1 if u else 0))
                hi, lo = mt[:, :, 96:96 + 2 * GH:2], mt[:, :, 97:97 + 2 * GH:2]
                link(nc.vector.tensor_scalar(hi, mx[:], -1.0, None, ALU.mult))
                nc.vector.scalar_tensor_tensor(lo, mx[:], -1.0, hi.bitcast(F32), ALU.mult,
                                               ALU.subtract).then_inc(mt_ready, 1)

            def normalise(b, u, part):
                g, hf = u // 2, u % 2
                if part == 0:
                    dve.wait_ge(od_act, b * (3 * NU) + (3 * (u + 1) + 2))
                    link(nc.vector.transpose(den[:], den[:]))
                elif part == 1:
                    cols = den[:].rearrange("p (c i) -> p c i", i=32)
                    link(nc.vector.reciprocal(dsmall[:], cols[:, :, 0]))
                elif part == 2:
                    link(nc.vector.transpose(den[:], dsmall[:].unsqueeze(2).to_broadcast([P, QB // 32, 32])))
                else:
                    cols = o[:, g, hf * QB:(hf + 1) * QB]
                    nc.vector.tensor_tensor(cols, cols, den[:], ALU.mult).then_inc(on_done, 1)

            mean_square(None, 0)
            for t in range(TPH):
                scale_x(None, 0, t)
            mean_square(None, 1)
            for t in range(TPH):
                scale_x(None, 1, t)
            for tile in LEAD_MISC:
                work_tile(None, tile)
            link(nc.vector.tensor_tensor(indc[96:128, :], ident[96:128, 96:96 + 2 * GH:2],
                                         ident[96:128, 97:97 + 2 * GH:2], ALU.add))
            for sl in range(2):
                for h in range(GH):
                    link(nc.vector.tensor_copy(ks[96:128, sl, h, :], indc[96:128, h:h + 1].to_broadcast([32, L])))
            link(nc.vector.tensor_scalar(mt[:], ident[:].unsqueeze(1).to_broadcast([P, TPH, P]), 0.0, None, ALU.mult))

            Link.lead, Link.n = Link.n, 0
            with dve.Fori(0, NB) as b:
                Link.b = b
                for q in range(NT * KT):
                    for n in range(sum(MAX_IN_V[:q]), sum(MAX_IN_V[:q + 1])):
                        max_tile(b, n)
                    tile = IN_V.get(q // KT)
                    if q % KT == KT - 1 and tile and tile[0] != "mT":
                        work_tile(b, tile)
                for u in range(NU):
                    for s in range(NS):
                        if (u, s) == (4, 0):
                            nb = next_batch(b)
                            nc.vector.tensor_copy(cur_gain[:], gain[:, bass.ds(nb, 1), :].squeeze(1)).then_inc(const_dve, 1)
                            nc.vector.tensor_copy(cur_bias[:], bias[:, bass.ds(nb, 1), :].squeeze(1)).then_inc(const_dve, 1)
                        if (u, s) == (4, 5):
                            mean_square(b, 0)
                        if (u, s) == (6, 5):
                            mean_square(b, 1)
                        if (u, s) == (5, 0):
                            dve.wait_ge(const_dve, b * 2 + 4)
                        for h in range(GH):
                            for n in next_maxima(u, s, h):
                                max_tile(b, NMAX + n)
                            if (u, s) == (4, 6):
                                scale_x(b, 0, h)
                            if (u, s) == (6, 7):
                                scale_x(b, 1, h)
                            for tile in done_at(u, s, h):
                                if tile[0] != "mT":
                                    work_tile(b, tile)
                            if s == 3 and u:
                                normalise(b, u - 1, h)

                def lo_part(t):
                    dve.wait_ge(os_act, b * NT + t + 1)
                    nc.vector.tensor_tensor(osplit[:, t % 2, 1, :, :], o[:, :, t * P:(t + 1) * P],
                                            osplit[:, t % 2, 0, :, :].bitcast(F32), ALU.subtract).then_inc(os_dve, 1)

                def out_tile(t):
                    n = NU * NMAX + t
                    dve.wait_ge(sq_ready, SCORES_Q(b, n + 1))
                    dve.wait_ge(y_stored[t % 2], b * (NT // 2 * 16) + (t // 2 + 1) * 16)
                    nc.vector.tensor_copy(yout[:, t % 2, :], mbank[n % MB][:]).then_inc(sq_done, 1)

                for t in range(3):
                    lo_part(t)
                for part in range(4):
                    normalise(b, NU - 1, part)
                for t in range(NT):
                    out_tile(t)
                    if t + 3 < NT:
                        lo_part(t + 3)
            assert Link.n == LINKS_PER_BATCH, Link.n

        @block.tensor
        def _(pe):
            def product3_part(out, lhs, rhs, k, kdim, last_sem):
                for a, c in ((0, 0), (0, 1), (1, 0)):
                    last = nc.tensor.matmul(out, lhs(a, k), rhs(c, k), start=(k == 0 and a == 0 and c == 0),
                                            stop=(k == kdim - 1 and a == 1))
                if k == kdim - 1:
                    last.then_inc(last_sem, 1)

            def product3(out, lhs, rhs, kdim, last_sem):
                for k in range(kdim):
                    product3_part(out, lhs, rhs, k, kdim, last_sem)

            def work_bank(b, tile):
                return lead_bank(misc_index(False, tile)) if b is None else wbank

            def work_bank_empty(b, tile):
                i = misc_index(b is not None, tile)
                if b is not None:
                    pe.wait_ge(w_act, MISC(b, i))
                    pe.wait_ge(w_dve, MISC_DVE(b, dve_before(True, tile)))
                elif i >= LEAD_BANKS:
                    pe.wait_ge(w_act, i - LEAD_BANKS + 1)
                    pe.wait_ge(w_dve, i - LEAD_BANKS + 1)

            def project(b, tile, k):
                if k == 0:
                    work_bank_empty(b, tile)
                    if b is None:
                        pe.wait_ge(w_dve, dve_before(False, ("hT", KT - 1, 0 if tile[0] == "Q" else 1)) + 1)
                w = wq if tile[0] == "Q" else wk
                g = tile[1] // 2 % NG
                hf = tile[1] % 2 if tile[0] == "Q" else tile[2]
                product3_part(work_bank(b, tile)[:], lambda a, k: w[a][:, k, g * P:(g + 1) * P],
                              lambda c, k: hT[c][:, k, hf * QB:(hf + 1) * QB], k, KT, w_ready)

            def work_tile(b, tile):
                work_bank_empty(b, tile)
                bank = work_bank(b, tile)
                if tile[0] == "hT":
                    _, k, hf = tile
                    if k == 0:
                        pe.wait_ge(x_scaled, TPH * (hf + 1) if b is None else b * 8 + 8 + TPH * (hf + 1))
                    for j in range(TPH):
                        last = nc.tensor.transpose(bank[:, j * P:(j + 1) * P],
                                                   x_tokens(b, hf)[:, j, k * P:(k + 1) * P], ident[:])
                else:
                    pe.wait_ge(mt_ready, b * NU + (tile[1] + 2))
                    for j in range(TPH):
                        last = nc.tensor.matmul(bank[:, j * P:(j + 1) * P], mt[:, j, :], identr[:],
                                                start=True, stop=True)
                last.then_inc(w_ready, 1)

            def max_tile(b, n):
                u, i = n // NMAX, n % NMAX
                h, t, hf = i // (TPH * NHALF), i // NHALF % TPH, i % NHALF
                if i % (TPH * NHALF) == 0:
                    pe.wait_ge(q_stacked[h], b * (NU * HEAD_INC) + (u + 1) * HEAD_INC)
                    if u % 2 == 0:
                        pe.wait_ge(k_stacked[h], b * (NG * HEAD_INC) + (u // 2 + 1) * HEAD_INC)
                pe.wait_ge(sq_done, SCORES_Q(b, n + 1))
                nc.tensor.matmul(mbank[n % MB][:], qs[0:96, u % 3, h, t * P:(t + 1) * P],
                                 ks[0:96, u // 2 % 2, h, hf * QB:(hf + 1) * QB],
                                 start=True, stop=True).then_inc(sq_ready, 1)

            def denominators(b, u):
                pe.wait_ge(sum_done, sums_done(b, u, NS - 2, POOL_HEADS - 1))
                for h in range(POOL_HEADS):
                    last = nc.tensor.matmul(dbank[DH * h:DH * h + DH, :], ones[:], sums[:, h, :],
                                            start=False, stop=True)
                last.then_inc(d_ready, 1)

            def values(b, u, s):
                g = u // 2
                pe.wait_ge(st_done, SCORES_T(b, NT + (u * NS + s + 1) * GH) + SB)
                if s == 0:
                    pe.wait_ge(od_act, b * (3 * NU) + (3 * u + 1))
                for h in range(GH):
                    nc.tensor.matmul(obank[DH * h:DH * h + DH, :], v[:, s, (g * GH + h) * DH:(g * GH + h + 1) * DH],
                                     probs[:, s % 2, h, :], start=(s == 0), stop=(s == NS - 1))
                if s == NS - 1:
                    pe.wait_ge(od_act, b * (3 * NU) + (3 * u + 2))
                for h in range(0 if s == NS - 1 else POOL_HEADS, GH):
                    last = nc.tensor.matmul(dbank[DH * h:DH * h + DH, :], ones[:], probs[:, s % 2, h, :],
                                            start=(s == 0 or h < POOL_HEADS), stop=(s == NS - 1 and h >= POOL_HEADS))
                last.then_inc(pv_done, 1)

            pe.sem_inc(pv_done, 2)
            pe.sem_inc(st_ready, ST_LEAD)
            pe.sem_inc(d_ready, 1)
            for tile in LEAD_MISC:
                if tile[0] == "hT":
                    work_tile(None, tile)
                else:
                    for k in range(KT):
                        project(None, tile, k)
            with pe.Fori(0, NB) as b:
                pe.wait_ge(wv_loaded, b * 16 + 16)
                for t in range(NT):
                    pe.wait_ge(st_done, SCORES_T(b, t + 1))
                    for k in range(KT):
                        product3_part(sbank[t % SB][:], lambda a, k: hT[a][:, k, t * P:(t + 1) * P],
                                      lambda c, k: wv[:, c, k, :], k, KT, st_ready)
                        q = t * KT + k
                        for n in range(sum(MAX_IN_V[:q]), sum(MAX_IN_V[:q + 1])):
                            max_tile(b, n)
                    if t in IN_V and IN_V[t][0] == "mT":
                        work_tile(b, IN_V[t])
                    elif t in IN_V:
                        for k in range(KT):
                            project(b, IN_V[t], k)
                for u in range(NU):
                    g = u // 2
                    for s in range(NS):
                        for h in range(GH):
                            if s == 0 and h == 0:
                                pe.wait_ge(m_rows, b * NU + (u + 1))
                            if s == 0 and h == GH // 2:
                                pe.wait_ge(w_act, MISC(b, misc_index(True, ("mT", u)) + 1))
                            i = NT + (u * NS + s) * GH + h
                            pe.wait_ge(st_done, SCORES_T(b, i + 1))
                            nc.tensor.matmul(sbank[i % SB][:], ks[:, g % 2, h, s * P:(s + 1) * P],
                                             qs[:, u % 3, h, :], start=True, stop=True).then_inc(st_ready, 1)
                            for n in next_maxima(u, s, h):
                                max_tile(b, NMAX + n)
                            if part_at(u, s, h):
                                project(b, *part_at(u, s, h))
                            tile = made_at(u, s, h)
                            if tile:
                                work_tile(b, tile)
                            if h == 2 and (u or s):
                                values(b, u if s else u - 1, (s - 1) % NS)
                            if (s, h) == (1, 0) and u:
                                denominators(b, u - 1)
                values(b, NU - 1, NS - 1)
                pe.wait_ge(wo_loaded, b * 16 + 16)
                for t in range(NT):
                    pe.wait_ge(sq_done, SCORES_Q(b, NU * NMAX + t + 1))
                    pe.wait_ge(os_act, b * NT + t + 1)
                    pe.wait_ge(os_dve, b * NT + t + 1)
                    product3(mbank[(NU * NMAX + t) % MB][:], lambda a, k: osplit[:, t % 2, a, k, :],
                             lambda c, k: wo[c][:, k, :], NG, sq_ready)
                    if t == 0:
                        denominators(b, NU - 1)


def attention_setup(nc, x, t_in, W_in, cond_in, wv_dram, wo_dram, W, cst, psum):
    at = cst["at"]
    ident, identr, ones = cst["ident"], cst["identr"], cst["ones"]
    raw = at("w_raw", [P, 4, KT, D], F32, "setup_raw")
    wvs, wos, x_first = cst["wv"], cst["wo_hi"], cst["x_first"]
    t_sb = at("t_sb", [NB, DT], F32, "setup_t")
    t_T = at("t_T", [P, NB], F32, "setup_tT")
    gw = at("gw", [P, 4, KT, DT], F32, "setup_gw")
    gwT = at("gwT", [P, 4, D], F32, "setup_gwT")
    gb = at("gb", [P, 4, KT], F32, "setup_gb")
    parts = [W[0], W[1], [wvs[:, 0, :, :], wvs[:, 1, :, :]], [wos, W[2]]]
    RING = 4
    WEIGHT_ORDER = (0, 1, 2, 3)
    with ExitStack() as ctx:
        def sem(name):
            return ctx.enter_context(nc.semaphore(name))

        id_step = sem("id_step")
        cond_loaded = sem("cond_loaded")
        w_loaded = [sem(f"w_loaded{i}") for i in range(4)]
        t_ready = sem("t_ready")
        t_act = sem("t_act")
        t_dve = sem("t_dve")
        x_first_loaded, wv_stored, wo_stored = cst["x_first_loaded"], cst["wv_stored"], cst["wo_stored"]
        block = ctx.enter_context(nc.Block())
        tiles = ([("tT",)] + [("gwT", m) for m in range(4)] + [("cond", m) for m in range(4)]
                 + [("w", w, k) for w in WEIGHT_ORDER for k in range(KT)])

        @block.gpsimd
        def _(pool):
            nc.gpsimd.memset(ident[:], 0.0).then_inc(id_step, 1)
            nc.gpsimd.memset(ones[:], 1.0).then_inc(id_step, 1)
            pool.wait_ge(id_step, 2)
            nc.gpsimd.affine_select(out=ident[:], in_=ident[:], compare_op=ALU.not_equal, fill=1.0, base=0,
                                    pattern=[[-1, P]], channel_multiplier=1).then_inc(id_step, 1)

        @block.sync
        def _(sp):
            sp.dma_start(t_sb[:], t_in).then_inc(cond_loaded, 16)
            for m in range(4):
                sp.dma_start(gw[:, m, :, :], cond_in[m][0].rearrange("(k p) t -> p k t", p=P)).then_inc(cond_loaded, 16)
                with nc.allow_non_contiguous_dma(reason="512 bias values, once"):
                    sp.dma_start(gb[:, m, :], cond_in[m][1].rearrange("(k p) -> p k", p=P)).then_inc(cond_loaded, 16)
            for w in WEIGHT_ORDER:
                if w < NHALF:
                    sp.dma_start(x_first[w][:], x[0, w * QB:(w + 1) * QB, :].rearrange("(t p) d -> p t d", p=P)) \
                        .then_inc(x_first_loaded[w], 16)
                sp.dma_start(raw[:, w, :, :], W_in[w].rearrange("(j p) d -> p j d", p=P)).then_inc(w_loaded[w], 16)
            sp.wait_ge(t_dve, tiles.index(("w", 2, KT - 1)) + 1)
            sp.dma_start(wv_dram, wvs[:].bitcast(F32)).then_inc(wv_stored, 16)
            sp.wait_ge(t_act, tiles.index(("w", 3, KT - 1)) + 1)
            sp.dma_start(wo_dram, wos[:].bitcast(F32)).then_inc(wo_stored, 16)

        @block.tensor
        def _(pe):
            pe.wait_ge(id_step, 3)
            pe.wait_ge(cond_loaded, 16 * 9)
            for n, tile in enumerate(tiles):
                if n >= RING:
                    pe.wait_ge(t_act, n - RING + 1)
                    pe.wait_ge(t_dve, n - RING + 1)
                bank = psum[n % RING]
                if tile[0] == "tT":
                    last = nc.tensor.transpose(bank[:, 0:NB], t_sb[:], ident[0:NB, 0:NB])
                elif tile[0] == "gwT":
                    for k in range(KT):
                        last = nc.tensor.transpose(bank[:, k * P:(k + 1) * P], gw[:, tile[1], k, :], ident[:])
                elif tile[0] == "cond":
                    pe.wait_ge(t_dve, tiles.index(("gwT", tile[1])) + 1)
                    for k in range(KT):
                        last = nc.tensor.matmul(bank[:, k * NB:(k + 1) * NB], gwT[:, tile[1], k * P:(k + 1) * P],
                                                t_T[:], start=True, stop=True)
                else:
                    _, w, k = tile
                    if k == 0:
                        pe.wait_ge(w_loaded[w], 16)
                    for j in range(KT):
                        last = nc.tensor.transpose(bank[:, j * P:(j + 1) * P], raw[:, w, j, k * P:(k + 1) * P], ident[:])
                last.then_inc(t_ready, 1)

        @block.scalar
        def _(act):
            for n, tile in enumerate(tiles):
                act.wait_ge(t_ready, n + 1)
                if tile[0] == "w":
                    nc.scalar.activation(parts[tile[1]][0][:, tile[2], :], psum[n % RING][:], ACT.Copy).then_inc(t_act, 1)
                else:
                    act.sem_inc(t_act, 1)

        @block.vector
        def _(dve):
            dve.wait_ge(id_step, 3)
            nc.vector.tensor_copy(identr[:], ident[:])
            for n, tile in enumerate(tiles):
                bank = psum[n % RING]
                dve.wait_ge(t_ready, n + 1)
                if tile[0] == "tT":
                    ins = nc.vector.tensor_copy(t_T[:], bank[:, 0:NB])
                elif tile[0] == "gwT":
                    ins = nc.vector.tensor_copy(gwT[:, tile[1], :], bank[:])
                elif tile[0] == "cond":
                    dve.wait_ge(cond_loaded, 16 * 9)
                    ins = nc.vector.tensor_tensor(cst["cond"][tile[1]][:].rearrange("p b k -> p k b"),
                                                  bank[:, 0:KT * NB].rearrange("p (k b) -> p k b", b=NB),
                                                  gb[:, tile[1], :].unsqueeze(2).to_broadcast([P, KT, NB]), ALU.add)
                else:
                    dve.wait_ge(t_act, n + 1)
                    hi, lo = parts[tile[1]]
                    ins = nc.vector.tensor_tensor(lo[:, tile[2], :], bank[:], hi[:, tile[2], :].bitcast(F32), ALU.subtract)
                ins.then_inc(t_dve, 1)


NJ = HID // P
NBLK = L // QB
PREP_J = 8
GU_BANKS = 4


FFN_LOADS = [("gu", w, q) for q in range(HID // QB) for w in range(2)] + [("o", 0, q) for q in range(HID // QB)]
GU_LOADS = 2 * HID // QB
EARLY = 4


def raw_slot(n):
    return n % 4 if n < GU_LOADS else n % 2 * 2 + 1


def weight_source(n, gate_w, up_w, out_w):
    kind, w, q = FFN_LOADS[n]
    if kind == "gu":
        return (gate_w, up_w)[w][q * QB:(q + 1) * QB, :].rearrange("(j p) d -> p j d", p=P)
    return out_w[:, q * QB:(q + 1) * QB].rearrange("(j p) d -> p j d", p=P)


def ffn_program(nc, x, attn, gate_w, up_w, out_w, out, cst, psum):
    at = cst["at"]
    ident, gain, bias = cst["ident"], cst["g2"], cst["b2"]
    gain_now, bias_now = cst["gain_now"], cst["bias_now"]
    wT = at("wT", [P, 2, KT, HID], F32, "wT")
    woT = at("woT", [P, NJ, D], F32, "woT")
    gu = [at("gu_hi", [P, 2, 2, KT, P], F32R, "gu_hi"), at("gu_lo", [P, 2, 2, KT, P], F32R, "gu_lo")]
    wo = [at("wo_hi", [P, 2, D], F32R, "wo_hi2"), at("wo_lo", [P, 2, D], F32R, "wo_lo2")]
    hT = [at("h2_hi", [P, 2, KT, QB], F32R, "h2_hi"), at("h2_lo", [P, 2, KT, QB], F32R, "h2_lo")]
    hT_full = at("h2_full", [P, 2, KT, QB], F32, "h2_lo")
    raw = cst["raw"]
    x1 = at("x1", [P, TPH, D], F32, "x1")
    res = at("res", [P, 2, TPH, D], F32, "res")
    sg = at("sg", [P, 2, QB], F32, "sg")
    a = [at("a_hi", [P, 2, QB], F32R, "a_hi"), at("a_lo", [P, 2, QB], F32R, "a_lo")]
    junk = at("junk", [P, D], F32, "junk")
    ssq = at("ssq2", [P, TPH], F32, "ssq")
    var = at("var2", [P, TPH], F32, "var")
    inv = at("inv2", [P, TPH], F32, "inv")
    mhalf = at("mhalf2", [P, TPH], F32, "mhalf")
    ybank = psum[GU_BANKS:]

    NW = 4 * len(FFN_LOADS)
    lead = [("w", n) for n in range(4 * GU_LOADS)] + [("t", k) for k in range(KT)] \
        + [("w", n) for n in range(4 * GU_LOADS, NW)]

    def act_lead(i):
        return sum(kind == "t" or n % 2 == 0 for kind, n in lead[:i])

    def dve_lead(i):
        return sum(kind == "t" or n % 2 == 1 for kind, n in lead[:i])

    RING = Counter(NW + KT, NBLK * (2 * NJ + KT))

    def ring_tile(hf, j, kind):
        base = hf * (2 * NJ + KT)
        if kind < 2:
            return base + 2 * j + kind + max(0, min(KT, j - PREP_J))
        return base + 2 * (PREP_J + kind - 2) + 2 + kind - 2

    with ExitStack() as ctx:
        def sem(name):
            return ctx.enter_context(nc.semaphore(name))

        held = sem("held2")
        raw_loaded = [sem(f"raw_loaded{i}") for i in range(4)]
        x_loaded = sem("x_loaded2")
        attn_loaded = sem("attn_loaded")
        g_ready = sem("g_ready")
        g_act = sem("g_act")
        g_dve = sem("g_dve")
        out_mm = sem("out_mm")
        guh = sem("guh")
        gul = sem("gul")
        woh = sem("woh")
        wol = sem("wol")
        ah = sem("ah")
        al = sem("al")
        prod = sem("prod")
        summed = sem("summed")
        sq_sum = sem("sq_sum2")
        var_ready = sem("var_ready2")
        inv_ready = sem("inv_ready2")
        x_scaled = sem("x_scaled2")
        norm_now = sem("norm_now")
        full = sem("full")
        y_added = sem("y_added")
        y_stored = [sem("out_stored0"), sem("out_stored1")]
        block = ctx.enter_context(nc.Block())

        def nxt(b, hf):
            return (b, 1) if hf == 0 else (next_batch(b), 0)

        def blocks(b, hf, per, off=0):
            return b * (NBLK * per) + hf * per + off

        def weight_place(n):
            kind, w, q = FFN_LOADS[n // 4]
            c = n % 4
            if kind == "gu":
                return wT[:, w, c, q * QB:(q + 1) * QB]
            return woT[:, q * 4 + c, :]

        def act_ring(b, hf, j):
            return b * (NBLK * (NJ + KT)) + (NW // 2 + KT + hf * (NJ + KT) + j + max(0, min(KT, j - PREP_J)))

        def dve_ring(b, hf, j):
            return b * (NBLK * KT) + (NW // 2 + KT + hf * KT + max(0, min(KT, j - PREP_J)))

        def first_tiles_free(pe, b, n):
            j = NJ - 2 + n // 2
            if n % 2 == 0:
                pe.wait_ge(g_act, b * (NBLK * (NJ + KT)) + NW // 2 + KT - (NJ - 1 - j))
            else:
                pe.wait_ge(prod, b * (NBLK * NJ) + 1)

        @block.sync
        def _(sp):
            def load_tokens(b, hf, slot, prev):
                sp.dma_start(res[:, slot, :, :], x[b, hf * QB:(hf + 1) * QB, :].rearrange("(t p) d -> p t d", p=P)) \
                    .then_inc(x_loaded, 16)
                sp.dma_start(x1[:], attn[b, hf * QB:(hf + 1) * QB, :].rearrange("(t p) d -> p t d", p=P)) \
                    .then_inc(attn_loaded, 16)

            for s in y_stored:
                sp.sem_inc(s, 16)
            load_tokens(0, 0, 0, None)
            for n in range(EARLY, len(FFN_LOADS)):
                before = max(m for m in range(n) if raw_slot(m) == raw_slot(n))
                hold(sp, held, g_ready, lead.index(("w", 4 * before + 3)) + 1)
                sp.dma_start(raw[raw_slot(n)], weight_source(n, gate_w, up_w, out_w)) \
                    .then_inc(raw_loaded[raw_slot(n)], 16)
            with sp.Fori(0, NB) as b:
                prepared = sp.snap(next_batch(b))
                for hf in range(NBLK):
                    slot = (hf + 1) % 2
                    hold(sp, held, y_stored[slot], b * (TPH * 16) + (TPH * 16 + 16 if slot == 0 else 16))
                    hold(sp, held, g_ready, RING(b, ring_tile(hf, 0, 0)))
                    nb, nh = (b, 1) if hf == 0 else (prepared, 0)
                    load_tokens(nb, nh, slot, b)
                    for t in range(TPH):
                        hold(sp, held, y_added, blocks(b, hf, TPH, t + 2))
                        row = hf * QB + t * P
                        sp.dma_start(out[b, row:row + P, :], res[:, hf, t, :]).then_inc(y_stored[hf], 16)
            for s in y_stored:
                hold(sp, held, s, NB * TPH * 16 + 16)
            hold(sp, held, x_loaded, 16 * (NB * NBLK + 1))
            hold(sp, held, attn_loaded, 16 * (NB * NBLK + 1))

        @block.gpsimd
        def _(pool):
            def prepare(x_val, n_sum, n_inv, slot):
                pool.wait_ge(x_loaded, x_val)
                pool.wait_ge(attn_loaded, x_val)
                nc.gpsimd.tensor_tensor(x1[:], x1[:], res[:, slot, :, :], ALU.add).then_inc(summed, 1)
                pool.wait_ge(summed, n_sum + 1)
                nc.gpsimd.tensor_tensor(res[:, slot, :, :], res[:, slot, :, :], x1[:], ALU.add).then_inc(summed, 1)
                pool.wait_ge(var_ready, n_inv + 1)
                nc.gpsimd.tensor_tensor(inv[:], var[:], mhalf[:], ALU.pow).then_inc(inv_ready, 1)

            prepare(16, 0, 0, 0)
            with pool.Fori(0, NB) as b:
                for hf in range(NBLK):
                    prepare(blocks(b, hf, 16, 32), blocks(b, hf, 2, 2), blocks(b, hf, 1, 1), (hf + 1) % 2)

        @block.scalar
        def _(act):
            def square(n, t):
                act.wait_ge(sq_sum, n + t)
                nc.scalar.activation(junk[:], x1[:, t, :], ACT.Square, accum_out=ssq[:, t:t + 1]).then_inc(sq_sum, 1)

            def norm_tile(n, k, slot, bank):
                act.wait_ge(g_ready, n + 1)
                nc.scalar.activation(hT[0][:, slot, k, :], psum[bank][:], ACT.Identity, bias=bias_now[:, k:k + 1],
                                     scale=gain_now[:, k:k + 1]).then_inc(g_act, 1)

            def gu_hi(j, slot):
                for w in range(2):
                    nc.scalar.activation(gu[0][:, slot, w, :, :], wT[:, w, :, j * P:(j + 1) * P], ACT.Copy).then_inc(guh, 1)

            for i, (kind, n) in enumerate(lead):
                if (kind, n) == ("w", 4 * EARLY):
                    act.wait_ge(summed, 1)
                    for t in range(TPH):
                        square(0, t)
                if (kind, n) == ("t", 0):
                    act.wait_ge(norm_now, 2)
                if kind == "t":
                    norm_tile(i, n, 0, i % GU_BANKS)
                elif n % 2 == 0:
                    act.wait_ge(g_ready, i + 1)
                    nc.scalar.activation(weight_place(n), psum[i % GU_BANKS][:], ACT.Copy).then_inc(g_act, 1)
            act.wait_ge(g_act, NW // 2 + KT)
            act.wait_ge(g_dve, NW // 2 + KT)
            gu_hi(0, 0)
            with act.Fori(0, NB) as b:
                for hf in range(NBLK):
                    for j in range(NJ):
                        act.wait_ge(g_ready, RING(b, ring_tile(hf, j - 1, 1) + 1 if j else
                                                  (ring_tile(hf - 1, NJ - 1, 1) + 1 if hf else 0)))
                        gu_hi((j + 1) % NJ, (j + 1) % 2)
                        act.wait_ge(out_mm, blocks(b, hf, NJ, j - 1 + 2))
                        nc.scalar.activation(wo[0][:, j % 2, :], woT[:, j, :], ACT.Copy).then_inc(woh, 1)
                        n = ring_tile(hf, j, 0)
                        act.wait_ge(g_ready, RING(b, n + 1))
                        act.wait_ge(al, blocks(b, hf, NJ, j - 1 + 2))
                        nc.scalar.activation(sg[:, j % 2, :], psum[n % GU_BANKS][:], ACT.Silu).then_inc(g_act, 1)
                        act.wait_ge(prod, blocks(b, hf, NJ, j + 2))
                        nc.scalar.activation(a[0][:, j % 2, :], sg[:, j % 2, :], ACT.Copy).then_inc(ah, 1)
                        if 2 <= j < 2 + TPH:
                            if j == 2:
                                act.wait_ge(summed, blocks(b, hf, 2, 3))
                                act.wait_ge(var_ready, blocks(b, hf, 1, 1))
                            square(blocks(b, hf, TPH, TPH), j - 2)
                        if j == PREP_J:
                            act.wait_ge(norm_now, blocks(b, hf, 2, 4))
                        if PREP_J <= j < PREP_J + KT:
                            k = j - PREP_J
                            n = ring_tile(hf, j, 2 + k)
                            norm_tile(RING(b, n), k, (hf + 1) % 2, n % GU_BANKS)

        @block.vector
        def _(dve):
            dve.sem_inc(al, 2)
            dve.sem_inc(prod, 1)
            dve.sem_inc(y_added, 1)
            nc.vector.memset(mhalf[:], -0.5)
            def mean_square(n):
                dve.wait_ge(sq_sum, TPH * (n + 1))
                dve.wait_ge(inv_ready, n)
                nc.vector.tensor_scalar(var[:], ssq[:], 1.0 / D, EPS, ALU.mult, ALU.add).then_inc(var_ready, 1)
                return n

            def scale_x(n):
                dve.wait_ge(inv_ready, n + 1)
                dve.wait_ge(summed, 2 * (n + 1))
                for t in range(TPH):
                    nc.vector.tensor_scalar(x1[:, t, :], x1[:, t, :], inv[:, t:t + 1], None, ALU.mult).then_inc(x_scaled, 1)

            def set_norm(nb):
                nc.vector.tensor_copy(gain_now[:], gain[:, bass.ds(nb, 1), :].squeeze(1)).then_inc(norm_now, 1)
                nc.vector.tensor_copy(bias_now[:], bias[:, bass.ds(nb, 1), :].squeeze(1)).then_inc(norm_now, 1)

            def norm_tile(n, n_act, n_full, k, slot, bank):
                dve.wait_ge(g_ready, n + 1)
                dve.wait_ge(g_act, n_act + 1)
                nc.vector.tensor_scalar(hT_full[:, slot, k, :], psum[bank][:], gain_now[:, k:k + 1],
                                        bias_now[:, k:k + 1], ALU.mult, ALU.add).then_inc(full, 1)
                dve.wait_ge(full, n_full + 1)
                nc.vector.tensor_tensor(hT[1][:, slot, k, :], hT_full[:, slot, k, :],
                                        hT[0][:, slot, k, :].bitcast(F32), ALU.subtract).then_inc(g_dve, 1)

            def gu_lo(n, j, slot):
                for w in range(2):
                    dve.wait_ge(guh, n + w + 1)
                    nc.vector.tensor_tensor(gu[1][:, slot, w, :, :], wT[:, w, :, j * P:(j + 1) * P],
                                            gu[0][:, slot, w, :, :].bitcast(F32), ALU.subtract).then_inc(gul, 1)

            set_norm(0)
            dve.wait_ge(norm_now, 2)
            for i, (kind, n) in enumerate(lead):
                if (kind, n) == ("w", 4 * EARLY + 8):
                    mean_square(0)
                    scale_x(0)
                if kind == "t":
                    norm_tile(i, act_lead(i), n, n, 0, i % GU_BANKS)
                elif n % 2:
                    dve.wait_ge(g_ready, i + 1)
                    nc.vector.tensor_copy(weight_place(n), psum[i % GU_BANKS][:]).then_inc(g_dve, 1)
            dve.wait_ge(g_act, NW // 2 + KT)
            dve.wait_ge(g_dve, NW // 2 + KT)
            gu_lo(0, 0, 0)
            with dve.Fori(0, NB) as b:
                for hf in range(NBLK):
                    for j in range(NJ):
                        gu_lo(blocks(b, hf, 2 * NJ, 2 * (j + 1)), (j + 1) % NJ, (j + 1) % 2)
                        dve.wait_ge(woh, blocks(b, hf, NJ, j + 1))
                        nc.vector.tensor_tensor(wo[1][:, j % 2, :], woT[:, j, :], wo[0][:, j % 2, :].bitcast(F32),
                                                ALU.subtract).then_inc(wol, 1)
                        n = ring_tile(hf, j, 1)
                        dve.wait_ge(g_ready, RING(b, n + 1))
                        dve.wait_ge(g_act, act_ring(b, hf, j) + 1)
                        nc.vector.tensor_tensor(sg[:, j % 2, :], psum[n % GU_BANKS][:], sg[:, j % 2, :],
                                                ALU.mult).then_inc(prod, 1)
                        dve.wait_ge(ah, blocks(b, hf, NJ, j + 1))
                        dve.wait_ge(prod, blocks(b, hf, NJ, j + 2))
                        nc.vector.tensor_tensor(a[1][:, j % 2, :], sg[:, j % 2, :], a[0][:, j % 2, :].bitcast(F32),
                                                ALU.subtract).then_inc(al, 1)
                        if j == 6:
                            mean_square(blocks(b, hf, 1, 1))
                        if j == 7:
                            set_norm(nxt(b, hf)[0])
                            scale_x(blocks(b, hf, 1, 1))
                            dve.wait_ge(norm_now, blocks(b, hf, 2, 4))
                        if PREP_J <= j < PREP_J + KT:
                            k = j - PREP_J
                            n = ring_tile(hf, j, 2 + k)
                            norm_tile(RING(b, n), act_ring(b, hf, j) + 1, blocks(b, hf, KT, KT + k), k,
                                      (hf + 1) % 2, n % GU_BANKS)
                    dve.wait_ge(out_mm, blocks(b, hf, NJ, NJ + 2))
                    for t in range(TPH):
                        nc.vector.tensor_tensor(res[:, hf, t, :], ybank[t][:], res[:, hf, t, :],
                                                ALU.add).then_inc(y_added, 1)

        @block.tensor
        def _(pe):
            pe.sem_inc(out_mm, 2)

            def bank_free(b, hf, n_in):
                kinds = []
                for h in range(NBLK):
                    for j in range(NJ):
                        kinds += [("g", h, j), ("u", h, j)] + ([("t", h, j)] if PREP_J <= j < PREP_J + KT else [])
                m = n_in - GU_BANKS
                if m >= 0:
                    kind, h, j = kinds[m]
                    bb = b
                else:
                    kind, h, j = kinds[m]
                    bb = b - 1
                if kind == "g":
                    pe.wait_ge(g_act, act_ring(bb, h, j) + 1)
                elif kind == "u":
                    pe.wait_ge(prod, blocks(bb, h, NJ, j + 2))
                else:
                    pe.wait_ge(g_act, act_ring(bb, h, j) + 2)
                    pe.wait_ge(g_dve, dve_ring(bb, h, j) + 1)

            def transposes(k, bank):
                for t in range(TPH):
                    last = nc.tensor.transpose(psum[bank][:, t * P:(t + 1) * P], x1[:, t, k * P:(k + 1) * P], ident[:])
                last.then_inc(g_ready, 1)

            for i, (kind, n) in enumerate(lead):
                if i >= GU_BANKS:
                    before = lead[i - GU_BANKS]
                    if before[0] == "t" or before[1] % 2 == 0:
                        pe.wait_ge(g_act, act_lead(i - GU_BANKS + 1))
                    if before[0] == "t" or before[1] % 2:
                        pe.wait_ge(g_dve, dve_lead(i - GU_BANKS + 1))
                if kind == "t":
                    if n == 0:
                        pe.wait_ge(x_scaled, TPH)
                    transposes(n, i % GU_BANKS)
                    continue
                load, c = n // 4, n % 4
                if load >= EARLY and c == 0:
                    slot = raw_slot(load)
                    pe.wait_ge(raw_loaded[slot], 16 * sum(raw_slot(m) == slot for m in range(EARLY, load + 1)))
                for j in range(4):
                    last = nc.tensor.transpose(psum[i % GU_BANKS][:, j * P:(j + 1) * P],
                                               raw[raw_slot(load)][:, j, c * P:(c + 1) * P], ident[:])
                last.then_inc(g_ready, 1)

            pe.wait_ge(g_act, NW // 2 + KT)
            pe.wait_ge(g_dve, NW // 2 + KT)

            def out_product(b, hf, j):
                for s in (ah, wol):
                    pe.wait_ge(s, blocks(b, hf, NJ, j + 1))
                pe.wait_ge(al, blocks(b, hf, NJ, j + 3))
                if j == 0:
                    pe.wait_ge(y_added, blocks(b, hf, TPH, 1))
                for t in range(TPH):
                    for p, q in ((0, 0), (0, 1), (1, 0)):
                        last = nc.tensor.matmul(ybank[t][:], a[p][:, j % 2, t * P:(t + 1) * P], wo[q][:, j % 2, :],
                                                start=(j == 0 and p == 0 and q == 0),
                                                stop=(j == NJ - 1 and p == 1))
                last.then_inc(out_mm, 1)

            with pe.Fori(0, NB) as b:
                for hf in range(NBLK):
                    for j in range(NJ):
                        pe.wait_ge(gul, blocks(b, hf, 2 * NJ, 2 * (j + 1)))
                        for w in range(2):
                            n = ring_tile(hf, j, w)
                            if n >= GU_BANKS:
                                bank_free(b, hf, n)
                            else:
                                first_tiles_free(pe, b, n)
                            steps = [(k, p, q) for k in range(KT) for p, q in ((0, 0), (0, 1), (1, 0))]
                            for i, (k, p, q) in enumerate(steps):
                                last = nc.tensor.matmul(psum[n % GU_BANKS][:], gu[p][:, j % 2, w, k, :],
                                                        hT[q][:, hf, k, :], start=(i == 0), stop=(i == len(steps) - 1))
                            last.then_inc(g_ready, 1)
                        if PREP_J <= j < PREP_J + KT:
                            k = j - PREP_J
                            n = ring_tile(hf, j, 2 + k)
                            bank_free(b, hf, n)
                            if k == 0:
                                pe.wait_ge(x_scaled, blocks(b, hf, TPH, 2 * TPH))
                            transposes(k, n % GU_BANKS)
                        if j:
                            out_product(b, hf, j - 1)
                    out_product(b, hf, NJ - 1)



def condition_block(nc, x, t, wq, wk, wv, wo, cond, gate_w, up_w, out_w, out):
    attn = nc.dram_tensor("attn_out", (NB, L, D), F32, kind="Internal").ap()
    wv_dram = nc.dram_tensor("wv_parts", (P, 2, KT, D), F32, kind="Internal").ap()
    wo_dram = nc.dram_tensor("wo_part", (P, KT, D), F32, kind="Internal").ap()
    base = (nc.sbuf_base + 31) // 32 * 32
    WEIGHTS = ("wq_hi", "wq_lo", "wk_hi", "wk_lo", "wo_lo")

    def plan(start, regions):
        places = {}
        for name, words in regions:
            places[name] = start
            start += (4 * words + 31) // 32 * 32
        return places, start

    small = [("ident", P), ("identr", P), ("ones", DH)] + [(f"cond{m}", NB * KT) for m in range(4)] \
        + [("gain_now", KT), ("bias_now", KT), ("ssq", TPH), ("var", TPH), ("inv", TPH), ("mhalf", TPH)]
    const_at, base = plan(base, small)
    weights_at, after_weights = plan(base, [(n, KT * D) for n in WEIGHTS])
    setup_at, _ = plan(after_weights, [("setup_raw", 4 * KT * D), ("setup_t", DT),
                                       ("setup_tT", NB), ("setup_gw", 4 * KT * DT), ("setup_gwT", 4 * D),
                                       ("setup_gb", 4 * KT)])
    attention_at, _ = plan(after_weights, [
        ("hT_hi", KT * L), ("hT_lo", KT * L), ("qk_hi", 2 * QB), ("qk_lo", 2 * QB), ("qs", 2 * GH * QB),
        ("qs_2", GH * QB), ("ks", 2 * GH * L), ("v", NS * D), ("probs", 2 * GH * QB), ("sums", POOL_HEADS * QB), ("mt", TPH * P),
        ("o", NG * L), ("den", QB), ("x4", TPH * D), ("yout", 2 * D), ("pmax", TPH * GH * NHALF),
        ("mx", TPH * GH), ("dsmall", QB // 32), ("indc", GH)])
    ffn_at, _ = plan(base, [
        ("wT", 2 * KT * HID), ("woT", NJ * D), ("gu_hi", 4 * KT * P), ("gu_lo", 4 * KT * P), ("wo_hi2", 2 * D),
        ("wo_lo2", 2 * D), ("h2_hi", 2 * KT * QB), ("h2_lo", 2 * KT * QB), ("x1", TPH * D), ("res", 2 * TPH * D),
        ("sg", 2 * QB), ("a_hi", 2 * QB), ("a_lo", 2 * QB), ("junk", D)])
    places = {**const_at, **weights_at, **setup_at, **attention_at, **ffn_at}

    def at(name, shape, dtype, region):
        return nc.alloc_sbuf_tensor_at(name, shape, dtype, offset=places[region])

    cst = {"at": at, "ident": at("ident", [P, P], F32, "ident"), "identr": at("identr", [P, P], F32R, "identr"),
           "ones": at("ones", [P, DH], F32, "ones"), "gain_now": at("gain_now", [P, KT], F32, "gain_now"),
           "bias_now": at("bias_now", [P, KT], F32, "bias_now"),
           "cond": [at(f"cond{m}", [P, NB, KT], F32, f"cond{m}") for m in range(4)]}
    cst["wv"] = at("wv", [P, 2, KT, D], F32R, "probs")
    cst["wo_hi"] = at("wo_hi", [P, KT, D], F32R, "qs_2")
    cst["x_first"] = [at(f"x{hf}", [P, TPH, D], F32, ("x4", "o")[hf]) for hf in range(NHALF)]
    assert places["h2_hi"] >= places["ks"] + 4 * GH * L and places["h2_lo"] >= places["h2_hi"] + 8 * KT * QB \
        and places["x1"] <= places["probs"]
    raw = [at(f"raw{i}", [P, 2, KT, QB], F32, ("h2_hi", "h2_lo")[i]) for i in range(2)]
    cst["raw"] = [raw[i // 2][:, i % 2, :, :] for i in range(4)]
    early = [(cst["raw"][raw_slot(n)], weight_source(n, gate_w, up_w, out_w)) for n in range(EARLY)]
    cst["g1"], cst["b1"], cst["g2"], cst["b2"] = cst["cond"]
    parts = [at(n, [P, KT, D], F32R, n) for n in WEIGHTS]
    W = [parts[0:2], parts[2:4], parts[4]]
    with ExitStack() as ctx:
        cst["x_first_loaded"] = [ctx.enter_context(nc.semaphore(f"x_first_loaded{hf}")) for hf in range(NHALF)]
        cst["wv_stored"], cst["wo_stored"] = [ctx.enter_context(nc.semaphore(n)) for n in ("wv_stored", "wo_stored")]
        psum = [ctx.enter_context(nc.psum_tensor(f"bank{i}", [P, QB], F32)) for i in range(8)]
        attention_setup(nc, x, t, [wq, wk, wv, wo], cond, wv_dram, wo_dram, W, cst, psum)
        attention_program(nc, x, attn, wv_dram, wo_dram, W, early, cst, psum)
        ffn_program(nc, x, attn, gate_w, up_w, out_w, out, cst, psum)


_INS = ["x", "cond_256"] + ["L0_cond_" + n for n in ("Wq", "Wk", "Wv", "Wo", "g1w", "g1b", "b1w", "b1b", "g2w", "g2b",
                                                     "b2w", "b2b", "gate_w", "hid_w", "out_w")]


def kernel(**inputs):
    import concourse.bacc as bacc
    from concourse.bass_utils import run_bass_kernel_spmd

    nc = bacc.Bacc("TRN2", target_bir_lowering=False, num_devices=1)
    arrays, ap = {}, {}
    for name in _INS:
        a = np.ascontiguousarray(inputs[name])
        arrays[f"in_{name}"] = a
        ap[name.replace("L0_cond_", "")] = nc.dram_tensor(f"in_{name}", a.shape, mybir.dt.from_np(a.dtype),
                                                          kind="ExternalInput").ap()
    out = nc.dram_tensor("out_0", (NB, L, D), F32, kind="ExternalOutput").ap()
    cond = [(ap[f"{n}w"], ap[f"{n}b"]) for n in ("g1", "b1", "g2", "b2")]
    condition_block(nc, ap["x"], ap["cond_256"], ap["Wq"], ap["Wk"], ap["Wv"], ap["Wo"], cond,
                    ap["gate_w"], ap["hid_w"], ap["out_w"], out)
    r = run_bass_kernel_spmd(nc, [arrays], core_ids=[0])
    return r.results[0]["out_0"]
```
